# Optimizing a Trainium2 kernel written in Bass

```python
import numpy as np
import jax
import jax.numpy as jnp

def _softmax(x, axis=-1):
    return jax.nn.softmax(x, axis=axis)

def _gelu(x):
    return jax.nn.gelu(x, approximate=True)

def _silu(x):
    return jax.nn.silu(x)

def _sigmoid(x):
    return jax.nn.sigmoid(x)

def _layernorm(x, axis=-1, eps=1e-05):
    m = jnp.mean(x, axis=axis, keepdims=True)
    v = jnp.var(x, axis=axis, keepdims=True)
    return (x - m) / jnp.sqrt(v + eps)

def _scatter_add(tgt, idx, src, axis=0):
    return tgt.at[idx].add(src)

def _segment_sum(src, seg, n):
    return jax.ops.segment_sum(src, seg, n)
kernel_name = 'mk_prb_d2_jaxref_r4_c7d531'

def setup_inputs(seed: int=0):
    np.random.seed(seed)
    _w = jnp.asarray

    def _L0_attn_setup():
        import jax, jax.numpy as jnp
        import numpy as np
        D = 256
        B = 16
        L = 512

        def _lin_init(key, din, dout):
            kw, kb = jax.random.split(key)
            s = 1.0 / np.sqrt(din)
            w = jax.random.uniform(kw, (dout, din), minval=-s, maxval=s, dtype=jnp.float32)
            b = jax.random.uniform(kb, (dout,), minval=-s, maxval=s, dtype=jnp.float32)
            return (w, b)

        def _rms_norm(x, w, eps=1e-06):
            x32 = x.astype(jnp.float32)
            y = x32 * jax.lax.rsqrt(jnp.mean(x32 * x32, axis=-1, keepdims=True) + eps)
            return y.astype(x.dtype) * w
        key = jax.random.key(seed)
        ks = jax.random.split(key, 9)
        fc_w, fc_b = _lin_init(ks[0], D, D)
        fc_r_w, fc_r_b = _lin_init(ks[1], D, D)
        fc_i_w, fc_i_b = _lin_init(ks[2], D, D)
        fc_gate_w, fc_gate_b = _lin_init(ks[3], D, D)
        mlp_gate_w, mlp_gate_b = _lin_init(ks[4], D, 3 * D)
        mlp_fc_w, mlp_fc_b = _lin_init(ks[5], D, 3 * D)
        out_w, out_b = _lin_init(ks[6], 3 * D, D)
        alpha = jax.random.uniform(ks[7], (1, 1, D), dtype=jnp.float32) * (0.999 - 0.9) + 0.9
        hidden_states = jax.random.normal(ks[8], (B, L, D), dtype=jnp.float32)
        return dict(hidden_states=hidden_states, alpha=alpha, fc_w=fc_w, fc_b=fc_b, fc_r_w=fc_r_w, fc_r_b=fc_r_b, fc_i_w=fc_i_w, fc_i_b=fc_i_b, fc_gate_w=fc_gate_w, fc_gate_b=fc_gate_b, norm_w=jnp.ones((D,), jnp.float32), norm2_w=jnp.ones((D,), jnp.float32), mlp_gate_w=mlp_gate_w, mlp_gate_b=mlp_gate_b, mlp_fc_w=mlp_fc_w, mlp_fc_b=mlp_fc_b, out_w=out_w, out_b=out_b)
    _L0_attn_in = _L0_attn_setup()

    def _L0_ffn_setup():
        import jax, jax.numpy as jnp
        import numpy as np

        def _bitlinear(x, w_latent):
            scale = jax.lax.stop_gradient(jnp.clip(jnp.mean(jnp.abs(w_latent), axis=1, keepdims=True), 1e-05, None))
            tern = jnp.clip(jnp.round(w_latent / scale), -1.0, 1.0)
            w = w_latent + jax.lax.stop_gradient(tern - w_latent)
            return x @ (w * scale).T
        key = jax.random.key(seed)
        ks = jax.random.split(key, 6)
        dim, hidden, rank = (256, 1024, 16)
        B, S = (4, 1024)
        x = jax.random.normal(ks[0], (B, S, dim), dtype=jnp.float32)
        w_fc = 0.02 * jax.random.normal(ks[1], (hidden, dim), dtype=jnp.float32)
        w_proj = 0.02 * jax.random.normal(ks[2], (dim, hidden), dtype=jnp.float32)
        u = 0.02 * jax.random.normal(ks[3], (hidden, rank), dtype=jnp.float32)
        v = 0.02 * jax.random.normal(ks[4], (rank, dim), dtype=jnp.float32)
        fast_b = jax.random.normal(ks[5], (rank, rank), dtype=jnp.float32)
        gate = jnp.float32(0.05)
        return {'x': x, 'fast_b': fast_b, 'w_fc': w_fc, 'w_proj': w_proj, 'u': u, 'v': v, 'gate': gate}
    _L0_ffn_in = _L0_ffn_setup()

    def _L1_attn_setup():
        import jax, jax.numpy as jnp
        import numpy as np
        B_, L_, D_, E_, N_, DR_, DC_ = (2, 512, 256, 512, 16, 64, 4)
        key = jax.random.key(seed)
        ks = jax.random.split(key, 12)
        s = lambda fan: 1.0 / np.sqrt(fan)
        inp = {}
        inp['resid'] = jax.random.normal(ks[0], (B_, L_, D_), jnp.float32)
        inp['norm_w'] = jnp.ones((D_,), jnp.float32)
        inp['skip_w'] = jax.random.normal(ks[1], (E_, D_), jnp.float32) * s(D_)
        inp['in_w'] = jax.random.normal(ks[2], (E_, D_), jnp.float32) * s(D_)
        inp['conv_w'] = jax.random.normal(ks[3], (E_, DC_), jnp.float32) * s(DC_)
        inp['conv_b'] = jax.random.normal(ks[4], (E_,), jnp.float32) * 0.1
        inp['wd1'] = jax.random.normal(ks[5], (DR_, E_), jnp.float32) * s(E_)
        inp['wd2'] = jax.random.uniform(ks[6], (E_, DR_), jnp.float32, -1.0, 1.0) * DR_ ** (-0.5)
        dt = jnp.exp(jax.random.uniform(ks[7], (E_,), jnp.float32) * (np.log(0.1) - np.log(0.001)) + np.log(0.001))
        dt = jnp.clip(dt, 0.0001, None)
        inp['wd2_b'] = dt + jnp.log(-jnp.expm1(-dt))
        inp['wB'] = jax.random.normal(ks[8], (N_, E_), jnp.float32) * s(E_)
        inp['wC'] = jax.random.normal(ks[9], (N_, E_), jnp.float32) * s(E_)
        inp['A_log'] = jnp.log(jnp.broadcast_to(jnp.arange(1, N_ + 1, dtype=jnp.float32), (E_, N_)))
        inp['W_D'] = jnp.ones((E_,), jnp.float32)
        inp['out_w'] = jax.random.normal(ks[10], (D_, E_), jnp.float32) * s(E_)
        return inp
    _L1_attn_in = _L1_attn_setup()

    def _L1_ffn_setup():
        import jax, jax.numpy as jnp
        import numpy as np
        D_MODEL = 256
        NUM_EXPERTS = 8
        TOP_K = 2
        B, S = (1, 512)
        key = jax.random.key(seed)
        ks = jax.random.split(key, 8)
        sd = 1.0 / np.sqrt(D_MODEL)
        x = jax.random.normal(ks[0], (B, S, D_MODEL), dtype=jnp.float32)
        gate_w = jax.random.normal(ks[1], (D_MODEL, NUM_EXPERTS), dtype=jnp.float32) * sd
        gate_b = jnp.zeros((NUM_EXPERTS,), dtype=jnp.float32)
        w1 = jax.random.normal(ks[2], (NUM_EXPERTS, D_MODEL, 8 * D_MODEL), dtype=jnp.float32) * sd
        b1 = jnp.zeros((NUM_EXPERTS, 8 * D_MODEL), dtype=jnp.float32)
        w2 = jax.random.normal(ks[3], (NUM_EXPERTS, 4 * D_MODEL, D_MODEL), dtype=jnp.float32) * (1.0 / np.sqrt(4 * D_MODEL))
        b2 = jnp.zeros((NUM_EXPERTS, D_MODEL), dtype=jnp.float32)
        return {'x': x, 'gate_w': gate_w, 'gate_b': gate_b, 'w1': w1, 'b1': b1, 'w2': w2, 'b2': b2}
    _L1_ffn_in = _L1_ffn_setup()
    _d = {'L0_attn_hidden_states': _L0_attn_in['hidden_states'], 'L0_attn_alpha': _L0_attn_in['alpha'], 'L0_attn_fc_w': _L0_attn_in['fc_w'], 'L0_attn_fc_b': _L0_attn_in['fc_b'], 'L0_attn_fc_r_w': _L0_attn_in['fc_r_w'], 'L0_attn_fc_r_b': _L0_attn_in['fc_r_b'], 'L0_attn_fc_i_w': _L0_attn_in['fc_i_w'], 'L0_attn_fc_i_b': _L0_attn_in['fc_i_b'], 'L0_attn_fc_gate_w': _L0_attn_in['fc_gate_w'], 'L0_attn_fc_gate_b': _L0_attn_in['fc_gate_b'], 'L0_attn_norm_w': _L0_attn_in['norm_w'], 'L0_attn_norm2_w': _L0_attn_in['norm2_w'], 'L0_attn_mlp_gate_w': _L0_attn_in['mlp_gate_w'], 'L0_attn_mlp_gate_b': _L0_attn_in['mlp_gate_b'], 'L0_attn_mlp_fc_w': _L0_attn_in['mlp_fc_w'], 'L0_attn_mlp_fc_b': _L0_attn_in['mlp_fc_b'], 'L0_attn_out_w': _L0_attn_in['out_w'], 'L0_attn_out_b': _L0_attn_in['out_b'], 'L0_ffn_fast_b': _L0_ffn_in['fast_b'], 'L0_ffn_w_fc': _L0_ffn_in['w_fc'], 'L0_ffn_w_proj': _L0_ffn_in['w_proj'], 'L0_ffn_u': _L0_ffn_in['u'], 'L0_ffn_v': _L0_ffn_in['v'], 'L0_ffn_gate': _L0_ffn_in['gate'], 'L1_attn_norm_w': _L1_attn_in['norm_w'], 'L1_attn_skip_w': _L1_attn_in['skip_w'], 'L1_attn_in_w': _L1_attn_in['in_w'], 'L1_attn_conv_w': _L1_attn_in['conv_w'], 'L1_attn_conv_b': _L1_attn_in['conv_b'], 'L1_attn_wd1': _L1_attn_in['wd1'], 'L1_attn_wd2': _L1_attn_in['wd2'], 'L1_attn_wd2_b': _L1_attn_in['wd2_b'], 'L1_attn_wB': _L1_attn_in['wB'], 'L1_attn_wC': _L1_attn_in['wC'], 'L1_attn_A_log': _L1_attn_in['A_log'], 'L1_attn_W_D': _L1_attn_in['W_D'], 'L1_attn_out_w': _L1_attn_in['out_w'], 'L1_ffn_gate_w': _L1_ffn_in['gate_w'], 'L1_ffn_gate_b': _L1_ffn_in['gate_b'], 'L1_ffn_w1': _L1_ffn_in['w1'], 'L1_ffn_b1': _L1_ffn_in['b1'], 'L1_ffn_w2': _L1_ffn_in['w2'], 'L1_ffn_b2': _L1_ffn_in['b2']}
    _x0 = _d['L0_attn_hidden_states']
    _d['L0_attn_hidden_states'] = jax.random.normal(jax.random.fold_in(jax.random.key(seed), 1), (4, 1024, 256), dtype=_x0.dtype)
    del _x0
    return _d

def reference(L0_attn_hidden_states, L0_attn_alpha, L0_attn_fc_w, L0_attn_fc_b, L0_attn_fc_r_w, L0_attn_fc_r_b, L0_attn_fc_i_w, L0_attn_fc_i_b, L0_attn_fc_gate_w, L0_attn_fc_gate_b, L0_attn_norm_w, L0_attn_norm2_w, L0_attn_mlp_gate_w, L0_attn_mlp_gate_b, L0_attn_mlp_fc_w, L0_attn_mlp_fc_b, L0_attn_out_w, L0_attn_out_b, L0_ffn_fast_b, L0_ffn_w_fc, L0_ffn_w_proj, L0_ffn_u, L0_ffn_v, L0_ffn_gate, L1_attn_norm_w, L1_attn_skip_w, L1_attn_in_w, L1_attn_conv_w, L1_attn_conv_b, L1_attn_wd1, L1_attn_wd2, L1_attn_wd2_b, L1_attn_wB, L1_attn_wC, L1_attn_A_log, L1_attn_W_D, L1_attn_out_w, L1_ffn_gate_w, L1_ffn_gate_b, L1_ffn_w1, L1_ffn_b1, L1_ffn_w2, L1_ffn_b2):

    def _L0_attn_ref(hidden_states, alpha, fc_w, fc_b, fc_r_w, fc_r_b, fc_i_w, fc_i_b, fc_gate_w, fc_gate_b, norm_w, norm2_w, mlp_gate_w, mlp_gate_b, mlp_fc_w, mlp_fc_b, out_w, out_b):
        import jax, jax.numpy as jnp
        import numpy as np
        D = 256
        B = 16
        L = 512

        def _lin_init(key, din, dout):
            kw, kb = jax.random.split(key)
            s = 1.0 / np.sqrt(din)
            w = jax.random.uniform(kw, (dout, din), minval=-s, maxval=s, dtype=jnp.float32)
            b = jax.random.uniform(kb, (dout,), minval=-s, maxval=s, dtype=jnp.float32)
            return (w, b)

        def _rms_norm(x, w, eps=1e-06):
            x32 = x.astype(jnp.float32)
            y = x32 * jax.lax.rsqrt(jnp.mean(x32 * x32, axis=-1, keepdims=True) + eps)
            return y.astype(x.dtype) * w
        residual = hidden_states
        h = _rms_norm(hidden_states, norm_w)
        gate = jax.nn.gelu(h @ fc_gate_w.T + fc_gate_b, approximate=False)
        hs = h @ fc_w.T + fc_b
        r = jax.nn.sigmoid(h @ fc_r_w.T + fc_r_b)
        i = jax.nn.sigmoid(h @ fc_i_w.T + fc_i_b)
        a = jnp.exp(-8.0 * jax.nn.softplus(alpha) * r)
        s = jnp.sqrt(1.0 - a * a) * hs * i

        def step(carry, xs):
            a_t, s_t = xs
            o = a_t * carry + s_t
            return (o, o)
        a_l = jnp.swapaxes(a, 0, 1)
        s_l = jnp.swapaxes(s, 0, 1)
        _, out_l = jax.lax.scan(step, jnp.zeros_like(s_l[0]), (a_l, s_l))
        out = jnp.swapaxes(out_l, 0, 1)
        hs2 = out * gate + residual
        h2 = _rms_norm(hs2, norm2_w)
        g2 = jax.nn.gelu(h2 @ mlp_gate_w.T + mlp_gate_b, approximate=False)
        f2 = h2 @ mlp_fc_w.T + mlp_fc_b
        return f2 * g2 @ out_w.T + out_b + hs2

    def _L0_ffn_ref(x, fast_b, w_fc, w_proj, u, v, gate):
        import jax, jax.numpy as jnp
        import numpy as np

        def _bitlinear(x, w_latent):
            scale = jax.lax.stop_gradient(jnp.clip(jnp.mean(jnp.abs(w_latent), axis=1, keepdims=True), 1e-05, None))
            tern = jnp.clip(jnp.round(w_latent / scale), -1.0, 1.0)
            w = w_latent + jax.lax.stop_gradient(tern - w_latent)
            return x @ (w * scale).T
        h = _bitlinear(x, w_fc) + gate * (x @ v.T @ fast_b.T @ u.T)
        r = jnp.maximum(h, 0.0)
        return _bitlinear(r * r, w_proj)

    def _L1_attn_ref(resid, norm_w, skip_w, in_w, conv_w, conv_b, wd1, wd2, wd2_b, wB, wC, A_log, W_D, out_w):
        import jax, jax.numpy as jnp
        import numpy as np
        B_, L_, D_, E_, N_, DR_, DC_ = (2, 512, 256, 512, 16, 64, 4)
        eps = 1e-05
        xn = resid * jax.lax.rsqrt(jnp.mean(resid * resid, axis=-1, keepdims=True) + eps) * norm_w
        skip = jnp.einsum('bld,ed->ble', xn, skip_w)
        x = jnp.einsum('bld,ed->ble', xn, in_w)
        Dc = conv_w.shape[1]
        L = x.shape[1]
        xp = jnp.pad(x, ((0, 0), (Dc - 1, 0), (0, 0)))
        xc = conv_b + sum((xp[:, k:k + L, :] * conv_w[:, k] for k in range(Dc)))
        x = jax.nn.silu(xc)
        delta = jax.nn.softplus(jnp.einsum('blr,er->ble', jnp.einsum('ble,re->blr', x, wd1), wd2) + wd2_b)
        Bm = jnp.einsum('ble,ne->bln', x, wB)
        Cm = jnp.einsum('ble,ne->bln', x, wC)
        A = -jnp.exp(A_log)

        def step(h, inp):
            xt, dt, bt, ct = inp
            h = jnp.exp(dt[:, :, None] * A) * h + (dt * xt)[:, :, None] * bt[:, None, :]
            y = jnp.einsum('ben,bn->be', h, ct)
            return (h, y)
        h0 = jnp.zeros((x.shape[0], A.shape[0], A.shape[1]), x.dtype)
        xs = (jnp.swapaxes(x, 0, 1), jnp.swapaxes(delta, 0, 1), jnp.swapaxes(Bm, 0, 1), jnp.swapaxes(Cm, 0, 1))
        _, ys = jax.lax.scan(step, h0, xs)
        y = jnp.swapaxes(ys, 0, 1) + W_D * x
        y = y * jax.nn.silu(skip)
        out = jnp.einsum('ble,de->bld', y, out_w)
        return resid + out

    def _L1_ffn_ref(x, gate_w, gate_b, w1, b1, w2, b2):
        import jax, jax.numpy as jnp
        import numpy as np
        D_MODEL = 256
        NUM_EXPERTS = 8
        TOP_K = 2
        B, S = (1, 512)
        gate_logits = jnp.einsum('bsd,de->bse', x, gate_w) + gate_b
        weights, indices = jax.lax.top_k(gate_logits, TOP_K)
        weights = jax.nn.softmax(weights, axis=-1)
        h = jnp.einsum('bsd,edh->ebsh', x, w1) + b1[:, None, None, :]
        xh, gh = jnp.split(h, 2, axis=-1)
        act = jax.nn.silu(gh) * xh
        out_e = jnp.einsum('ebsf,efd->ebsd', act, w2) + b2[:, None, None, :]
        out_e = jnp.transpose(out_e, (1, 2, 0, 3))
        sel = jnp.take_along_axis(out_e, indices[..., None], axis=2)
        return jnp.sum(sel * weights[..., None], axis=2)
    x = L0_attn_hidden_states
    xn = _layernorm(x, axis=-1)
    x = x + _L0_attn_ref(xn, L0_attn_alpha, L0_attn_fc_w, L0_attn_fc_b, L0_attn_fc_r_w, L0_attn_fc_r_b, L0_attn_fc_i_w, L0_attn_fc_i_b, L0_attn_fc_gate_w, L0_attn_fc_gate_b, L0_attn_norm_w, L0_attn_norm2_w, L0_attn_mlp_gate_w, L0_attn_mlp_gate_b, L0_attn_mlp_fc_w, L0_attn_mlp_fc_b, L0_attn_out_w, L0_attn_out_b) + _L0_ffn_ref(xn, L0_ffn_fast_b, L0_ffn_w_fc, L0_ffn_w_proj, L0_ffn_u, L0_ffn_v, L0_ffn_gate)
    xn = _layernorm(x, axis=-1)
    x = x + _L1_attn_ref(xn, L1_attn_norm_w, L1_attn_skip_w, L1_attn_in_w, L1_attn_conv_w, L1_attn_conv_b, L1_attn_wd1, L1_attn_wd2, L1_attn_wd2_b, L1_attn_wB, L1_attn_wC, L1_attn_A_log, L1_attn_W_D, L1_attn_out_w) + _L1_ffn_ref(xn, L1_ffn_gate_w, L1_ffn_gate_b, L1_ffn_w1, L1_ffn_b1, L1_ffn_w2, L1_ffn_b2)
    return x

_drawn_inputs = setup_inputs


def setup_inputs(seed=0):
    import zlib

    import numpy as np

    out = dict(_drawn_inputs(seed))
    spreads = {'L0_attn_norm_w': (1.0, 0.6),
     'L0_attn_norm2_w': (1.0, 0.6),
     'L1_attn_norm_w': (1.0, 0.2),
     'L1_attn_W_D': (1.0, 0.6),
     'L1_ffn_gate_b': (0.0, 0.8),
     'L1_ffn_b1': (0.0, 2.0),
     'L1_ffn_b2': (0.0, 2.0)}
    factors = {'L0_attn_alpha': 64.0,
     'L0_attn_fc_b': 7.929,
     'L0_attn_fc_r_w': 8.0,
     'L0_attn_fc_r_b': 49.349,
     'L0_attn_fc_i_w': 2.985,
     'L0_attn_fc_i_b': 24.291,
     'L0_attn_fc_gate_b': 7.731,
     'L0_attn_mlp_gate_b': 6.818,
     'L0_attn_mlp_fc_b': 8.0,
     'L0_attn_out_b': 3.9,
     'L0_ffn_fast_b': 8.0,
     'L0_ffn_u': 8.0,
     'L0_ffn_v': 8.0,
     'L1_attn_conv_b': 4.203,
     'L1_attn_wd1': 8.0,
     'L1_attn_wd2': 8.0,
     'L1_attn_wd2_b': 7.123,
     'L1_attn_wB': 4.307,
     'L1_attn_wC': 4.578,
     'L1_attn_A_log': 8.0,
     'L1_ffn_gate_w': 8.0,
     'L1_ffn_w1': 8.0,
     'L1_ffn_w2': 8.0}
    for name, (base, spread) in spreads.items():
        noise = np.random.default_rng([zlib.crc32(name.encode()), seed]).standard_normal(out[name].shape)
        drawn = base * np.exp(spread * noise) if base else spread * noise
        out[name] = jnp.asarray(drawn.astype(out[name].dtype))
    for name, factor in factors.items():
        out[name] = (out[name] * factor).astype(out[name].dtype)
    return out
```

```python
from contextlib import ExitStack

import concourse.bass as bass
from concourse import mybir

P = 128
F32 = mybir.dt.float32
BF16 = mybir.dt.bfloat16
I32 = mybir.dt.int32
U32 = mybir.dt.uint32
ALU = mybir.AluOpType
ACT = mybir.ActivationFunctionType
AX_X = mybir.AxisListType.X

NTOK = 4096
SEQ = 1024
D = 256
KD = D // P
T = 512
NCH = NTOK // T
CPS = SEQ // T
SUB = T // P
MLP = 768
KM = MLP // P
HID = 1024
KH = HID // P
RANK = 16
EPS_LN = 1e-5
EPS_RMS0 = 1e-6
EPS_RMS1 = 1e-5
BANKS = 8

V0 = {}
_at = 0
for _name, _n in (("r_b", KD), ("i_b", KD), ("hs_b", KD), ("gate_b", KD), ("mg_b", KM), ("mf_b", KM),
                  ("norm_w", KD), ("norm2_w", KD), ("alpha", KD)):
    V0[_name] = _at
    _at += _n
NV0 = _at


def identity(pool, tile, done):
    pool.memset(tile[:, :], 0.0).then_inc(done, 1)
    pool.wait_ge(done, 1)
    pool.affine_select(out=tile[:, :], in_=tile[:, :], compare_op=ALU.not_equal, fill=1.0, base=0,
                       pattern=[[-1, P]], channel_multiplier=1).then_inc(done, 1)


def layer0(nc, dram):
    order = ([f"F{m}" for m in range(KH)] + ["MS"]
             + [g for m in range(KM) for g in (f"MG{m}", f"MF{m}")] + ["O0", "O1"]
             + ["XT0", "XT1", "HT0", "HT1", "R0", "R1", "I0", "I1", "H0", "H1", "GA0", "GA1"]
             + ["N0", "N1", "Q0", "Q1", "L"])
    assert len(order) % BANKS == 0
    uses = len(order) // BANKS
    place = {g: (p % BANKS, p // BANKS) for p, g in enumerate(order)}

    with ExitStack() as ctx:
        def sb(name, shape, dt=F32):
            return ctx.enter_context(nc.sbuf_tensor(name, shape, dt))

        def sem(name):
            return ctx.enter_context(nc.semaphore(name))

        bank = [ctx.enter_context(nc.psum_tensor(f"bank{i}", [P, T], F32)) for i in range(BANKS)]
        w_p = sb("w_p", [P, KD, 4 * D])
        w_m = sb("w_m", [P, KD, 2 * MLP])
        w_o = sb("w_o", [P, KM, D])
        w_f = sb("w_f", [P, KD, HID])
        w_j = sb("w_j", [P, KH, D])
        vec = sb("vec", [P, NV0])
        brow = sb("brow", [1, D])
        gb = sb("gb", [P, 8])
        gw = sb("gw", [P, KD, 8])
        low_v = sb("low_v", [RANK, D])
        low_b = sb("low_b", [RANK, RANK])
        low_u = sb("low_u", [RANK, HID])
        low_g = sb("low_g", [RANK, 1])
        low_z = sb("low_z", [RANK, D])
        ident = sb("ident", [P, P])
        ones = sb("ones", [P, P])
        inv_d = sb("inv_d", [P, P])
        inv_h = sb("inv_h", [P, P])
        neghalf = sb("neghalf", [P, SUB])
        eps_ln, eps_rms0, eps_rms1 = (sb(f"eps_{n}", [P, SUB]) for n in ("ln", "rms0", "rms1"))
        sp = sb("sp", [P, 3, KD])
        eps0 = sb("eps0", [P, 1])
        ca = sb("ca", [P, KD])
        xt = sb("xt", [P, SUB, D])
        xres = sb("xres", [P, SUB, D])
        xn = sb("xn", [P, SUB, D])
        hn = sb("hn", [P, SUB, D])
        x1 = sb("x1", [P, SUB, D])
        xn1 = sb("xn1", [P, SUB, D])
        xr1 = sb("xr1", [P, SUB, D])
        x1p = sb("x1p", [P, SUB, D])
        stats = sb("stats", [P, SUB, 6])
        mv = sb("mv", [P, SUB, 2])
        stats1 = sb("stats1", [P, SUB, 6])
        seen = sb("seen", [P, SUB])
        mv1 = sb("mv1", [P, SUB, 2])
        small = sb("small", [P, 6, SUB])
        small1 = sb("small1", [P, 6, SUB])
        lg = sb("lg", [P, NCH * SUB, 8])
        xnT = sb("xnT", [P, KD, T])
        hT = sb("hT", [P, KD, T])
        rT = sb("rT", [P, KD, T])
        iT = sb("iT", [P, KD, T])
        gT = sb("gT", [P, KD, T])
        tT = sb("tT", [P, KD, T])
        aT = sb("aT", [P, KD, T])
        qT = sb("qT", [P, KD, T])
        oT = sb("oT", [P, KD, T])
        hs2 = sb("hs2", [P, KD, T])
        sq = sb("sq", [P, KD, T])
        rms = sb("rms", [P, T])
        rinv = sb("rinv", [P, T])
        h2 = sb("h2", [P, KD, T])
        fT = sb("fT", [P, KH, T])
        mg = sb("mg", [P, 2, T])
        mT = sb("mT", [P, KM, T])
        xn1T = sb("xn1T", [P, KD, T])
        xr1T = sb("xr1T", [P, KD, T])
        carry = sb("carry", [P, KD])
        keep = sb("keep", [P, 1])

        filled = [sem(f"filled{i}") for i in range(BANKS)]
        drained = [sem(f"drained{i}") for i in range(BANKS)]
        weights_in = sem("weights_in")
        x_in = sem("x_in")
        xres_in = sem("xres_in")
        x1p_out, xn1_out, xrT_out, lg_out = sem("x1p_out"), sem("xn1_out"), sem("xrT_out"), sem("lg_out")
        s_id = sem("s_id")
        s_const = sem("s_const")
        s_prep = sem("s_prep")
        s_prepa = sem("s_prepa")
        p_prep = sem("p_prep")
        s_st = sem("s_st")
        s_pw = sem("s_pw")
        s_ln = sem("s_ln")
        s_a = sem("s_a")
        s_a2 = sem("s_a2")
        s_q = sem("s_q")
        s_s = sem("s_s")
        s_scan = sem("s_scan")
        s_carry = sem("s_carry")
        s_og = sem("s_og")
        s_hs2 = sem("s_hs2")
        s_sq = sem("s_sq")
        s_rinv = sem("s_rinv")
        s_h2 = sem("s_h2")
        s_fsq = sem("s_fsq")
        s_st1 = sem("s_st1")
        s_pw1 = sem("s_pw1")
        s_l1 = sem("s_l1")
        block = ctx.enter_context(nc.Block())

        def wait_filled(eng, g, c):
            b, i = place[g]
            eng.wait_ge(filled[b], c * uses + (uses + i + 1))

        def wait_drained(eng, g, c):
            b, i = place[g]
            eng.wait_ge(drained[b], c * uses + (uses + i + 1))

        def wait_bank(pe, g, c):
            b, i = place[g]
            pe.wait_ge(drained[b], c * uses + (uses + i))

        def inc_filled(ins, g):
            ins.then_inc(filled[place[g][0]], 1)

        def inc_drained(ins, g):
            ins.then_inc(drained[place[g][0]], 1)

        def ps(g):
            return bank[place[g][0]]

        def rows(ap, c):
            return ap[bass.ds(c * T, T), :].rearrange("(s p) d -> p s d", p=P)

        w_loads = [(w_p, dram["w_p"]), (w_m, dram["w_m"]), (w_o, dram["w_o"]), (w_f, dram["w_f"]),
                   (w_j, dram["w_j"]), (vec, dram["vec0"]), (brow, dram["out_b"]),
                   (gb, dram["gate_b"].to_broadcast([P, 8])), (gw, dram["gate_w"]),
                   (low_v, dram["low_v"]), (low_b, dram["low_b"]), (low_u, dram["low_u"]),
                   (low_g, dram["low_g"].to_broadcast([RANK, 1]))]
        weights_all = 16 * len(w_loads)

        @block.sync
        def _(sp_):
            for dst, src in w_loads:
                sp_.dma_start(dst[:], src).then_inc(weights_in, 16)
            sp_.dma_start(xt[:], rows(dram["x"], 0)).then_inc(x_in, 16)
            with sp_.Fori(0, NCH) as c:
                wait_drained(sp_, "O1", c - 1)
                sp_.dma_start(xres[:], rows(dram["x"], c)).then_inc(xres_in, 16)
                sp_.wait_ge(s_ln, c * 8 + 8)
                sp_.dma_start(xt[:], rows(dram["x"], c + 1)).then_inc(x_in, 16)
                sp_.wait_ge(s_l1, c * 12 + 12)
                sp_.dma_start(rows(dram["x1p"], c), x1p[:]).then_inc(x1p_out, 16)
                sp_.dma_start(rows(dram["xn1"], c), xn1[:]).then_inc(xn1_out, 16)
                wait_drained(sp_, "Q1", c)
                wait_drained(sp_, "Q0", c)
                sp_.dma_start(dram["xrT"][bass.ds(c * P, P), :, :], xr1T[:]).then_inc(xrT_out, 16)
            wait_drained(sp_, "L", NCH - 1)
            sp_.dma_start(dram["logits"], lg[:]).then_inc(lg_out, 16)
            sp_.wait_ge(lg_out, 16)
            for s in (x1p_out, xn1_out, xrT_out):
                sp_.wait_ge(s, 16 * NCH + 16)

        @block.gpsimd
        def _(pool):
            identity(pool, ident, s_id)
            for tile, value in ((ones, 1.0), (inv_d, 1.0 / D), (inv_h, 1.0 / HID), (neghalf, -0.5),
                                (carry, 0.0), (keep, 1.0), (eps_ln, EPS_LN), (eps_rms0, EPS_RMS0),
                                (eps_rms1, EPS_RMS1)):
                pool.memset(tile[:], value).then_inc(s_const, 1)
            pool.wait_ge(s_const, 9)

            def row_scales(sm, mvt, done, base, eps_rms):
                var = mvt[:, :, 1]
                pool.tensor_tensor(sm[:, 0], var, eps_ln[:], ALU.add).then_inc(done, 1)
                pool.wait_ge(done, base + 1)
                pool.tensor_tensor(sm[:, 1], sm[:, 0], neghalf[:], ALU.pow).then_inc(done, 1)
                pool.wait_ge(done, base + 2)
                pool.tensor_tensor(sm[:, 2], sm[:, 1], sm[:, 1], ALU.mult).then_inc(done, 1)
                pool.wait_ge(done, base + 3)
                pool.tensor_tensor(sm[:, 3], sm[:, 2], var, ALU.mult).then_inc(done, 1)
                pool.wait_ge(done, base + 4)
                pool.tensor_tensor(sm[:, 2], sm[:, 3], eps_rms[:], ALU.add).then_inc(done, 1)
                pool.wait_ge(done, base + 5)
                pool.tensor_tensor(sm[:, 4], sm[:, 2], neghalf[:], ALU.pow).then_inc(done, 1)
                pool.wait_ge(done, base + 6)
                pool.tensor_tensor(sm[:, 5], sm[:, 4], sm[:, 1], ALU.mult).then_inc(done, 1)

            pool.wait_ge(s_st, 9)
            row_scales(small, mv, s_pw, 0, eps_rms0)
            with pool.Fori(0, NCH) as c:
                pool.wait_ge(s_st, c * 9 + 18)
                row_scales(small, mv, s_pw, c * 7 + 7, eps_rms0)
                for m in range(KH):
                    wait_drained(pool, f"F{m}", c)
                    pool.tensor_tensor(fT[:, m], fT[:, m], fT[:, m], ALU.mult).then_inc(s_fsq, 1)
                pool.wait_ge(s_st1, c * 9 + 9)
                row_scales(small1, mv1, s_pw1, c * 7, eps_rms1)

        @block.scalar
        def _(act):
            act.wait_ge(weights_in, weights_all)
            al = vec[:, V0["alpha"]:V0["alpha"] + KD]
            act.activation(sp[:, 0], al, ACT.Abs).then_inc(s_prepa, 1)
            act.wait_ge(s_prepa, 1)
            act.activation(sp[:, 1], sp[:, 0], ACT.Exp, scale=-1.0).then_inc(s_prepa, 1)
            act.wait_ge(s_prepa, 2)
            act.activation(sp[:, 2], sp[:, 1], ACT.Ln, bias=1.0).then_inc(s_prepa, 1)
            act.activation(mT[:, 0:2 * KD], w_f[:].rearrange("p k (a n) -> p (k a) n", n=T), ACT.Abs).then_inc(s_prepa, 1)
            act.activation(fT[:, 0:KH // 2], w_j[:].rearrange("p (k a) n -> p k (a n)", a=2), ACT.Abs).then_inc(s_prepa, 1)

            def project(c):
                for k in range(KD):
                    wait_filled(act, f"XT{k}", c)
                    inc_drained(act.activation(xnT[:, k], ps(f"XT{k}")[:], ACT.Copy), f"XT{k}")
                for name, dst, b, f in (("R", rT, "r_b", ACT.Sigmoid), ("I", iT, "i_b", ACT.Sigmoid),
                                        ("GA", gT, "gate_b", ACT.Gelu)):
                    for k in range(KD):
                        wait_filled(act, f"{name}{k}", c)
                        inc_drained(act.activation(dst[:, k], ps(f"{name}{k}")[:], f,
                                                   bias=vec[:, V0[b] + k:V0[b] + k + 1]), f"{name}{k}")

            act.wait_ge(s_prep, 1)
            project(-1)
            with act.Fori(0, NCH) as c:
                for k in range(KD):
                    wait_drained(act, f"R{k}", c - 1)
                    if k == 0:
                        act.wait_ge(s_scan, c * KD + KD)
                    act.activation(aT[:, k], rT[:, k], ACT.Exp, scale=ca[:, k:k + 1]).then_inc(s_a, 1)
                for m in range(2):
                    wait_filled(act, f"F{m}", c)
                    inc_drained(act.activation(fT[:, m], ps(f"F{m}")[:], ACT.Relu), f"F{m}")
                for k in range(KD):
                    act.wait_ge(s_a2, c * KD + (k + 1))
                    act.activation(qT[:, k], qT[:, k], ACT.Sqrt, bias=1.0, scale=-1.0).then_inc(s_q, 1)
                for m in range(2, KH):
                    wait_filled(act, f"F{m}", c)
                    inc_drained(act.activation(fT[:, m], ps(f"F{m}")[:], ACT.Relu), f"F{m}")
                for k in range(KD):
                    act.wait_ge(s_hs2, c * KD + (k + 1))
                    act.activation(sq[:, k], hs2[:, k], ACT.Square).then_inc(s_sq, 1)
                wait_filled(act, "MS", c)
                act.wait_ge(s_rinv, c + 1)
                inc_drained(act.activation(rms[:], ps("MS")[:], ACT.Sqrt, bias=eps0[:, 0:1]), "MS")
                for m in range(KM):
                    g = f"MG{m}"
                    wait_filled(act, g, c)
                    if m >= 2:
                        wait_drained(act, f"MF{m - 2}", c)
                    inc_drained(act.activation(mg[:, m % 2], ps(g)[:], ACT.Gelu,
                                               bias=vec[:, V0["mg_b"] + m:V0["mg_b"] + m + 1]), g)
                project(c)
                act.wait_ge(xrT_out, c * 16 + 16)
                for k in range(KD):
                    wait_filled(act, f"Q{k}", c)
                    inc_drained(act.activation(xr1T[:, k], ps(f"Q{k}")[:], ACT.Copy), f"Q{k}")

        @block.vector
        def _(dve):
            dve.memset(eps0[:], EPS_RMS0).then_inc(s_prep, 1)
            dve.wait_ge(weights_in, weights_all)
            n = [1]

            def step(ins, then_wait=True):
                ins.then_inc(s_prep, 1)
                n[0] += 1
                if then_wait:
                    dve.wait_ge(s_prep, n[0])

            for k in range(KD):
                step(dve.tensor_scalar(w_p[:, k], w_p[:, k], vec[:, V0["norm_w"] + k:V0["norm_w"] + k + 1], None, ALU.mult))
                step(dve.tensor_scalar(w_m[:, k], w_m[:, k], vec[:, V0["norm2_w"] + k:V0["norm2_w"] + k + 1], None, ALU.mult))
            dve.wait_ge(s_prepa, 3)
            al = vec[:, V0["alpha"]:V0["alpha"] + KD]
            step(dve.tensor_scalar(sp[:, 0], al, 0.0, None, ALU.max))
            step(dve.tensor_tensor(sp[:, 1], sp[:, 0], sp[:, 2], ALU.add))
            step(dve.tensor_scalar(ca[:], sp[:, 1], -8.0, None, ALU.mult))
            dve.wait_ge(p_prep, 1)
            step(dve.tensor_scalar(low_z[:], bank[0][0:RANK, 0:D], low_g[:, 0:1], None, ALU.mult))

            def ternary(w, w2, mean, scale, hi, lo, ready):
                dve.wait_ge(p_prep, ready)
                step(dve.tensor_scalar(scale, mean, 1e-5, None, ALU.max))
                step(dve.tensor_scalar(hi, scale, 0.5, None, ALU.mult))
                for wk, over, under in w2:
                    step(dve.tensor_tensor(over, wk, hi, ALU.is_gt))
                    step(dve.scalar_tensor_tensor(out=under, in0=wk, scalar=-1.0, in1=hi, op0=ALU.mult, op1=ALU.is_gt))
                    step(dve.tensor_tensor(over, over, under, ALU.subtract))
                    step(dve.tensor_tensor(wk, over, scale, ALU.mult))

            for a in range(2):
                half = slice(a * T, (a + 1) * T)
                ternary(None, [(w_f[:, k, half], xnT[:, k], hT[:, k]) for k in range(KD)], bank[1 + a][:],
                        rms[:], rinv[:], None, 2)
            ternary(None, [(w_j[:, k], xn[:, 0], xn[:, 1]) for k in range(KH)], bank[3][:, 0:D], rms[:, 0:D],
                    rinv[:, 0:D], None, 3)
            dve.wait_ge(p_prep, 4)
            for k in range(KD):
                for a in range(2):
                    half = slice(a * T, (a + 1) * T)
                    step(dve.tensor_tensor(w_f[:, k, half], w_f[:, k, half], bank[4 + 2 * k + a][:], ALU.add))
            assert n[0] == PREP_STEPS, n[0]

            def normalise(src, mvt, st, sm, c, s_stat, s_pow, s_out, dst_n, dst_r):
                for s in range(SUB):
                    dve.bn_stats(st[:, s], src[:, s]).then_inc(s_stat, 1)
                dve.wait_ge(s_stat, c * 9 + (9 + 4))
                dve.tensor_copy(seen[:], st[:, :, 0]).then_inc(s_stat, 1)
                for s in range(SUB):
                    dve.bn_aggr(mvt[:, s], st[:, s]).then_inc(s_stat, 1)
                return

            def centre(src, mvt, sm, s_out, dst_n, dst_r):
                for s in range(SUB):
                    dve.tensor_scalar(dst_n[:, s], src[:, s], mvt[:, s, 0:1], sm[:, 1, s:s + 1],
                                      ALU.subtract, ALU.mult).then_inc(s_out, 1)
                    dve.tensor_scalar(dst_r[:, s], src[:, s], mvt[:, s, 0:1], sm[:, 5, s:s + 1],
                                      ALU.subtract, ALU.mult).then_inc(s_out, 1)

            def next_rows(c):
                dve.wait_ge(x_in, c * 16 + 32)
                normalise(xt, mv, stats, small, c, s_st, s_pw, s_ln, xn, hn)
                dve.wait_ge(s_st, c * 9 + 18)
                dve.wait_ge(s_pw, c * 7 + 14)
                centre(xt, mv, small, s_ln, xn, hn)

            def project(c):
                for k in range(KD):
                    wait_filled(dve, f"HT{k}", c)
                    inc_drained(dve.tensor_copy(hT[:, k], ps(f"HT{k}")[:]), f"HT{k}")
                for k in range(KD):
                    wait_filled(dve, f"H{k}", c)
                    wait_drained(dve, f"I{k}", c)
                    inc_drained(dve.scalar_tensor_tensor(
                        out=tT[:, k], in0=ps(f"H{k}")[:], scalar=vec[:, V0["hs_b"] + k:V0["hs_b"] + k + 1],
                        in1=iT[:, k], op0=ALU.add, op1=ALU.mult), f"H{k}")

            next_rows(-1)
            dve.sem_inc(s_scan, KD)
            dve.sem_inc(s_rinv, 1)
            dve.sem_inc(s_carry, 3)
            dve.sem_inc(xrT_out, 16)
            dve.sem_inc(x1p_out, 16)
            dve.sem_inc(xn1_out, 16)
            project(-1)
            dve.wait_ge(s_const, 9)
            with dve.Fori(0, NCH) as c:
                for k in range(KD):
                    dve.wait_ge(s_a, c * KD + (k + 1))
                    dve.tensor_tensor(qT[:, k], aT[:, k], aT[:, k], ALU.mult).then_inc(s_a2, 1)
                for k in range(KD):
                    dve.wait_ge(s_q, c * KD + (k + 1))
                    wait_drained(dve, f"H{k}", c - 1)
                    dve.tensor_tensor(tT[:, k], tT[:, k], qT[:, k], ALU.mult).then_inc(s_s, 1)
                for k in range(KD):
                    dve.wait_ge(s_s, c * KD + (k + 1))
                    dve.wait_ge(s_carry, c * 3 + 3)
                    dve.tensor_tensor_scan(oT[:, k], aT[:, k], tT[:, k], carry[:, k:k + 1],
                                           ALU.mult, ALU.add).then_inc(s_scan, 1)
                for k in range(KD):
                    dve.wait_ge(s_scan, c * KD + (KD + k + 1))
                    dve.tensor_scalar(carry[:, k:k + 1], oT[:, k, T - 1:T], keep[:, 0:1], None, ALU.mult).then_inc(s_carry, 1)
                dve.wait_ge(s_carry, c * 3 + 5)
                dve.tensor_scalar(keep[:], keep[:], -1.0, 1.0, ALU.mult, ALU.add).then_inc(s_carry, 1)
                for k in range(KD):
                    wait_drained(dve, f"GA{k}", c - 1)
                    dve.tensor_tensor(oT[:, k], oT[:, k], gT[:, k], ALU.mult).then_inc(s_og, 1)
                for k in range(KD):
                    dve.wait_ge(s_og, c * KD + (k + 1))
                    wait_drained(dve, f"XT{k}", c - 1)
                    dve.tensor_tensor(hs2[:, k], oT[:, k], xnT[:, k], ALU.add).then_inc(s_hs2, 1)
                for s in range(SUB):
                    pass
                dve.wait_ge(x_in, c * 16 + 32)
                normalise(xt, mv, stats, small, c, s_st, s_pw, s_ln, xn, hn)
                wait_drained(dve, "MS", c)
                dve.reciprocal(rinv[:], rms[:]).then_inc(s_rinv, 1)
                dve.wait_ge(s_rinv, c + 2)
                for k in range(KD):
                    dve.tensor_tensor(h2[:, k], hs2[:, k], rinv[:], ALU.mult).then_inc(s_h2, 1)
                dve.wait_ge(s_st, c * 9 + 18)
                dve.wait_ge(s_pw, c * 7 + 14)
                centre(xt, mv, small, s_ln, xn, hn)
                for m in range(KM):
                    wait_filled(dve, f"MF{m}", c)
                    wait_drained(dve, f"MG{m}", c)
                    inc_drained(dve.scalar_tensor_tensor(
                        out=mT[:, m], in0=ps(f"MF{m}")[:], scalar=vec[:, V0["mf_b"] + m:V0["mf_b"] + m + 1],
                        in1=mg[:, m % 2], op0=ALU.add, op1=ALU.mult), f"MF{m}")
                dve.wait_ge(xres_in, c * 16 + 16)
                for j in range(2):
                    wait_filled(dve, f"O{j}", c)
                    inc_drained(dve.tensor_tensor(x1[:, 2 * j:2 * j + 2], ps(f"O{j}")[:].rearrange("p (s d) -> p s d", s=2),
                                                  xres[:, 2 * j:2 * j + 2], ALU.add), f"O{j}")
                wait_drained(dve, "O0", c)
                wait_drained(dve, "O1", c)
                normalise(x1, mv1, stats1, small1, c - 1, s_st1, s_pw1, s_l1, xn1, xr1)
                project(c)
                dve.wait_ge(s_st1, c * 9 + 9)
                dve.wait_ge(s_pw1, c * 7 + 7)
                dve.wait_ge(xn1_out, c * 16 + 16)
                dve.wait_ge(x1p_out, c * 16 + 16)
                centre(x1, mv1, small1, s_l1, xn1, xr1)
                dve.wait_ge(s_l1, c * 12 + 8)
                for s in range(SUB):
                    dve.tensor_tensor(x1p[:, s], x1[:, s], xn1[:, s], ALU.add).then_inc(s_l1, 1)
                for k in range(KD):
                    wait_filled(dve, f"N{k}", c)
                    inc_drained(dve.tensor_copy(xn1T[:, k], ps(f"N{k}")[:]), f"N{k}")
                wait_filled(dve, "L", c)
                inc_drained(dve.tensor_tensor(lg[:, bass.ds(c * SUB, SUB), :], ps("L")[:, 0:SUB * 8].rearrange("p (s e) -> p s e", e=8),
                                              gb[:].rearrange("p (o e) -> p o e", o=1).to_broadcast([P, SUB, 8]),
                                              ALU.add), "L")

        @block.tensor
        def _(pe):
            mm = pe.matmul
            pe.wait_ge(weights_in, weights_all)
            pe.wait_ge(s_const, 9)
            pe.wait_ge(s_id, 2)
            mm(bank[0][0:RANK, 0:D], low_b[:], low_v[:], start=True, stop=True).then_inc(p_prep, 1)
            pe.wait_ge(s_prepa, 5)
            wabs = mT[:, 0:2 * KD].rearrange("p (k a) n -> p k a n", a=2)
            for a in range(2):
                for k in range(KD):
                    last = mm(bank[1 + a][:], inv_d[:], wabs[:, k, a], start=(k == 0), stop=(k == KD - 1))
            last.then_inc(p_prep, 1)
            wabs = fT[:, 0:KH // 2].rearrange("p k (a n) -> p (k a) n", a=2)
            for k in range(KH):
                last = mm(bank[3][:, 0:D], inv_h[:], wabs[:, k], start=(k == 0), stop=(k == KH - 1))
            last.then_inc(p_prep, 1)
            pe.wait_ge(s_prep, LOWZ_STEP)
            for k in range(KD):
                for a in range(2):
                    last = mm(bank[4 + 2 * k + a][:], low_z[:, k * P:(k + 1) * P], low_u[:, a * T:(a + 1) * T],
                              start=True, stop=True)
            last.then_inc(p_prep, 1)
            pe.wait_ge(s_prep, PREP_STEPS)
            first = order.index("XT0")
            after = order.index("N0")
            for b in range(BANKS):
                skipped = sum(1 for p in range(first) if p % BANKS == b)
                pe.sem_inc(drained[b], skipped)
                pe.sem_inc(filled[b], skipped)

            def product(g, w, cols, rhs, nk, c, ready=None):
                wait_bank(pe, g, c)
                for k in range(nk):
                    if ready is not None:
                        ready(k)
                    last = mm(ps(g)[:], w[:, k, cols], rhs[:, k], start=(k == 0), stop=(k == nk - 1))
                inc_filled(last, g)

            def turn(g, src, k, c):
                wait_bank(pe, g, c)
                for s in range(SUB):
                    last = pe.transpose(ps(g)[:, s * P:(s + 1) * P], src[:, s, k * P:(k + 1) * P], ident[:])
                inc_filled(last, g)

            def project(c):
                pe.wait_ge(s_ln, c * 8 + 16)
                for k in range(KD):
                    turn(f"XT{k}", xn, k, c)
                for k in range(KD):
                    turn(f"HT{k}", hn, k, c)
                for j, name in enumerate(("R", "I", "H", "GA")):
                    for m in range(KD):
                        product(f"{name}{m}", w_p, slice(j * D + m * P, j * D + (m + 1) * P), hT, KD, c,
                                ready=(lambda k: wait_drained(pe, f"HT{k}", c)) if j + m == 0 else None)

            project(-1)
            for p in range(after, len(order)):
                b = p % BANKS
                pe.wait_ge(drained[b], p // BANKS)
                pe.sem_inc(filled[b], 1)
                pe.sem_inc(drained[b], 1)
            with pe.Fori(0, NCH) as c:
                for m in range(KH):
                    product(f"F{m}", w_f, slice(m * P, (m + 1) * P), xnT, KD, c,
                            ready=(lambda k: wait_drained(pe, f"XT{k}", c - 1)) if m == 0 else None)
                wait_bank(pe, "MS", c)
                for k in range(KD):
                    pe.wait_ge(s_sq, c * KD + (k + 1))
                    last = mm(ps("MS")[:], inv_d[:], sq[:, k], start=(k == 0), stop=(k == KD - 1))
                inc_filled(last, "MS")
                for m in range(KM):
                    for j, name in enumerate(("MG", "MF")):
                        product(f"{name}{m}", w_m, slice(j * MLP + m * P, j * MLP + (m + 1) * P), h2, KD, c,
                                ready=(lambda k: pe.wait_ge(s_h2, c * KD + (k + 1))) if m + j == 0 else None)
                pe.wait_ge(s_hs2, c * KD + KD)
                for j in range(2):
                    wait_bank(pe, f"O{j}", c)
                    for s in (2 * j, 2 * j + 1):
                        cols = slice(s * P, (s + 1) * P)
                        out = ps(f"O{j}")[:, (s % 2) * D:(s % 2 + 1) * D]
                        mm(out, ones[0:1, :], brow[:], start=(s % 2 == 0), stop=False, skip_group_check=True)
                        for k in range(KD):
                            mm(out[:, k * P:(k + 1) * P], hs2[:, k, cols], ident[:], start=False, stop=False,
                               skip_group_check=True)
                        for m in range(KH):
                            if s == 0:
                                pe.wait_ge(s_fsq, c * KH + (m + 1))
                            mm(out, fT[:, m, cols], w_j[:, m], start=False, stop=False, skip_group_check=True)
                        for m in range(KM):
                            if s == 0:
                                wait_drained(pe, f"MF{m}", c)
                            last = mm(out, mT[:, m, cols], w_o[:, m], start=False, stop=(s % 2 == 1 and m == KM - 1),
                                      skip_group_check=True)
                    inc_filled(last, f"O{j}")
                project(c)
                pe.wait_ge(s_l1, c * 12 + 8)
                for k in range(KD):
                    turn(f"N{k}", xn1, k, c)
                for k in range(KD):
                    turn(f"Q{k}", xr1, k, c)
                wait_bank(pe, "L", c)
                for s in range(SUB):
                    for k in range(KD):
                        if s == 0:
                            wait_drained(pe, f"N{k}", c)
                        last = mm(ps("L")[:, s * 8:(s + 1) * 8], xn1T[:, k, s * P:(s + 1) * P], gw[:, k],
                                  start=(k == 0), stop=(k == KD - 1))
                inc_filled(last, "L")


LOWZ_STEP = 1 + 2 * KD + 3 + 1
PREP_STEPS = LOWZ_STEP + 2 * (2 + 4 * KD) + 2 + 4 * KH + 2 * KD


E_IN = 512
KE = E_IN // P
NST = 16
DR = 64
TAPS = 4
PAD = TAPS - 1
NSEQ = NTOK // SEQ
V1 = {}
_at = 0
for _name, _n in (("norm_w", KD), ("conv_w", KE * TAPS), ("conv_b", KE), ("dt_b", KE), ("A_log", KE * NST),
                  ("W_D", KE)):
    V1[_name] = _at
    _at += _n
NV1 = _at


def mamba(nc, dram):
    RING = 4
    ahead = {n: [] for n in range(NST)}
    for e in range(KE):
        ahead[e].append(f"IN{e}")
        ahead[5].append(f"SK{e}")
    ahead[7] = ["BC", "DR"]
    ahead[9] = [f"DT{e}" for e in range(KE)]

    def spread_at(n):
        return [(f"B{(n + 2) % NST}", n + 2 >= NST), (f"C{(n + 1) % NST}", n + 1 >= NST)]

    def listing(last):
        order = []
        for n in range(NST):
            if not last:
                order += ahead[n]
            order += [g for g, of_next in spread_at(n) if not (last and of_next)]
        return order + ["O0", "O1"]

    first = [g for n in range(NST) for g in ahead[n]] + ["B0", "C15", "B1", "C0", "O0", "O1"]
    place = {"first": {g: p for p, g in enumerate(first)}, "body": {g: p for p, g in enumerate(listing(False))},
             "last": {g: p for p, g in enumerate(listing(True))}}
    lead, per = len(first), len(listing(False))
    assert per % RING == 0 and (lead + place["body"]["O1"] - per) == place["first"]["O1"]

    with ExitStack() as ctx:
        def sb(name, shape, dt=F32):
            return ctx.enter_context(nc.sbuf_tensor("m_" + name, shape, dt))

        def sem(name):
            return ctx.enter_context(nc.semaphore("m_" + name))

        ybank = [ctx.enter_context(nc.psum_tensor(f"m_y{e}", [P, T], F32)) for e in range(KE)]
        ring = [ctx.enter_context(nc.psum_tensor(f"m_ring{i}", [P, T], F32)) for i in range(RING)]
        w_si = sb("w_si", [P, KD, 2 * E_IN])
        w_x = sb("w_x", [P, KE, DR + 2 * NST])
        w_dt = sb("w_dt", [DR, E_IN])
        w_out = sb("w_out", [P, KE, D])
        vec = sb("vec", [P, NV1])
        A = sb("A", [P, KE * NST])
        ident = sb("ident", [P, P])
        sel = sb("sel", [3 * 2 * NST, 2 * NST, P], BF16)
        xr = sb("xr", [P, KD, T])
        xpad = [sb(f"xpad{h}", [P, KE, PAD + T]) for h in range(2)]
        cv = sb("cv", [P, KE, T])
        xs = [sb(f"xs{h}", [P, KE, T]) for h in range(2)]
        sk = [sb(f"sk{h}", [P, KE, T]) for h in range(2)]
        dl = [sb(f"dl{h}", [P, KE, T]) for h in range(2)]
        ux = [sb(f"ux{h}", [P, KE, T]) for h in range(2)]
        bc3 = [sb(f"bc3{h}", [3 * 2 * NST, T], BF16) for h in range(2)]
        bcr = sb("bcr", [2 * NST, T])
        bc2 = sb("bc2", [2 * NST, T], BF16)
        dr = sb("dr", [DR, T])
        z = sb("z", [P, KE, T])
        ez = sb("ez", [P, KE, T])
        dA = sb("dA", [P, 2, KE, T])
        bb = sb("bb", [P, 2, T])
        bx = sb("bx", [P, 2, KE, T])
        hh = sb("hh", [P, 1, KE, T])
        hc = sb("hc", [P, 2, KE, T])
        carry = sb("carry", [P, NST, KE])
        y1 = ez
        mo = sb("mo", [P, SUB, D])

        filled = [sem(f"filled{i}") for i in range(RING)]
        drained = [sem(f"drained{i}") for i in range(RING)]
        w_in, xr_in, mo_out = sem("w_in"), sem("xr_in"), sem("mo_out")
        s_id, s_sel, s_pad, s_prep, s_A = sem("s_id"), sem("s_sel"), sem("s_pad"), sem("s_prep"), sem("s_A")
        s_conv, s_xs, s_bca, s_bcd = sem("s_conv"), sem("s_xs"), sem("s_bca"), sem("s_bcd")
        s_abs, s_ez, s_w, s_ln, s_dl, s_ux = (sem("s_abs"), sem("s_ez"), sem("s_w"), sem("s_ln"), sem("s_dl"),
                                              sem("s_ux"))
        s_exp, s_bx, s_scan, s_carry, s_y = sem("s_exp"), sem("s_bx"), sem("s_scan"), sem("s_carry"), sem("s_y")
        s_yf, s_y2 = sem("s_yf"), sem("s_y2")
        block = ctx.enter_context(nc.Block())

        def spot(g, at):
            kind, i, h = at
            p = place[kind][g]
            if kind == "first":
                return p % RING, p // RING
            return (lead + p) % RING, i * (per // RING) + (lead + p) // RING

        def bank_of(g, at):
            return (place[at[0]][g] + (0 if at[0] == "first" else lead)) % RING

        def wait_filled(eng, g, at):
            b, k = spot(g, at)
            eng.wait_ge(filled[b], k + 1)

        def wait_drained(eng, g, at):
            b, k = spot(g, at)
            eng.wait_ge(drained[b], k + 1)

        def wait_bank(pe, g, at):
            b, k = spot(g, at)
            if not (isinstance(k, int) and k == 0):
                pe.wait_ge(drained[b], k)

        def inc(ins, sems, g, at):
            ins.then_inc(sems[bank_of(g, at)], 1)

        def tile_of(g, at):
            return ring[bank_of(g, at)]

        START = ("first", -1, 1)

        def at_of(at, g):
            kind, i, h = at
            if g not in ("B0", "B1", "C0"):
                return at
            if isinstance(i, int) and i == 0:
                return START
            return ("body", i - 1, 1 - h)

        def program(eng, ahead_of, step, end):
            ahead_of(START, 0, 0, range(NST))

            def chunk(i, h, last):
                at = ("last" if last else "body", i, h)
                nxt = None if last else (i + 1, 1 - h)
                for n in range(NST):
                    if nxt:
                        ahead_of(at, nxt[0], nxt[1], [n])
                    step(at, i, h, n, last)
                end(at, i, h)

            with eng.Fori(0, NSEQ - 1) as b:
                chunk(b * 2, 0, False)
                chunk(b * 2 + 1, 1, False)
            chunk(2 * NSEQ - 2, 0, False)
            chunk(2 * NSEQ - 1, 1, True)

        w_loads = [(w_si, dram["w_si"]), (w_x, dram["w_x"]), (w_dt, dram["w_dt"]), (w_out, dram["w_out"]),
                   (vec, dram["vec1"])]

        @block.sync
        def _(sp):
            sp.dma_start(xr[:], dram["xrT"][0:P]).then_inc(xr_in, 16)
            for dst, src in w_loads:
                sp.dma_start(dst[:], src).then_inc(w_in, 16)

            def ahead_of(at, q, h, slots):
                if 6 in slots:
                    if not (isinstance(q, int) and q == 2 * NSEQ - 1):
                        wait_filled(sp, "SK3", at)
                        sp.dma_start(xr[:], dram["xrT"][bass.ds((q + 1) * P, P), :, :]).then_inc(xr_in, 16)

            def end(at, i, h):
                wait_drained(sp, "O0", at)
                wait_drained(sp, "O1", at)
                sp.dma_start(dram["mo"][bass.ds(i * T, T), :].rearrange("(s p) d -> p s d", p=P), mo[:]).then_inc(mo_out, 16)

            program(sp, ahead_of, lambda *_: None, end)
            sp.wait_ge(mo_out, 16 * NCH + 16)

        @block.gpsimd
        def _(pool):
            identity(pool, ident, s_id)
            pool.memset(sel[:], 0.0).then_inc(s_sel, 1)
            pool.memset(xpad[0][:, :, 0:PAD], 0.0).then_inc(s_pad, 1)
            for j in range(3):
                pool.wait_ge(s_sel, j + 1)
                pool.affine_select(out=sel[:], in_=sel[:], compare_op=ALU.not_equal, fill=1.0, base=-2 * NST * j,
                                   pattern=[[-1, 2 * NST], [0, P]], channel_multiplier=1).then_inc(s_sel, 1)
            pool.sem_inc(s_bx, 2)

            def step(at, i, h, n, last):
                wait_drained(pool, f"B{n}", at_of(at, f"B{n}"))
                if n == 0:
                    pool.wait_ge(s_ux, i * 1 + 1)
                pool.wait_ge(s_scan, i * (NST * KE) + (8 + KE * (n - 1)))
                pool.tensor_tensor(bx[:, n % 2], ux[h][:], bb[:, n % 2:n % 2 + 1, :].to_broadcast([P, KE, T]),
                                   ALU.mult).then_inc(s_bx, 1)

            program(pool, lambda *_: None, step, lambda *_: None)

        @block.scalar
        def _(act):
            act.wait_ge(w_in, 16 * len(w_loads))
            act.activation(A[:], vec[:, V1["A_log"]:V1["A_log"] + KE * NST], ACT.Exp).then_inc(s_prep, 1)
            act.sem_inc(mo_out, 16)

            def b_row(i, n, at):
                wait_filled(act, f"B{n}", at)
                act.wait_ge(s_bx, i * NST + (n + 1))
                inc(act.activation(bb[:, n % 2], tile_of(f"B{n}", at)[:], ACT.Copy), drained, f"B{n}", at)

            def decays(i, h, n):
                if n == 0:
                    act.wait_ge(s_dl, i * 3 + 3)
                    act.wait_ge(s_A, 1)
                act.wait_ge(s_scan, i * (NST * KE) + (8 + KE * (n - 1)))
                for e in range(KE):
                    act.activation(dA[:, n % 2, e], dl[h][:, e], ACT.Exp,
                                   scale=A[:, e * NST + n:e * NST + n + 1]).then_inc(s_exp, 1)

            def ahead_of(at, q, h, slots):
                for n in slots:
                    if n < KE:
                        e = n
                        wait_filled(act, f"IN{e}", at)
                        inc(act.activation(xpad[h][:, e, PAD:PAD + T], tile_of(f"IN{e}", at)[:], ACT.Copy), drained, f"IN{e}", at)
                    if n == 5:
                        for e in range(KE):
                            act.wait_ge(s_conv, q * (KE * TAPS) + ((e + 1) * TAPS))
                            act.activation(xs[h][:, e], cv[:, e], ACT.Silu).then_inc(s_xs, 1)
                        for e in range(KE):
                            wait_filled(act, f"SK{e}", at)
                            inc(act.activation(sk[h][:, e], tile_of(f"SK{e}", at)[:], ACT.Silu), drained, f"SK{e}", at)
                    if n == 7:
                        wait_filled(act, "BC", at)
                        act.activation(bc3[h][0:2 * NST, :], tile_of("BC", at)[0:2 * NST, :], ACT.Copy).then_inc(s_bca, 1)
                        wait_filled(act, "DR", at)
                        inc(act.activation(dr[:], tile_of("DR", at)[0:DR, :], ACT.Copy), drained, "DR", at)
                    if n == 8:
                        act.wait_ge(s_bcd, q * 3 + 2)
                        act.activation(bc3[h][2 * NST:4 * NST, :], bc2[:], ACT.Copy).then_inc(s_bca, 1)
                    if n == 9:
                        for e in range(KE):
                            wait_filled(act, f"DT{e}", at)
                            inc(act.activation(z[:, e], tile_of(f"DT{e}", at)[:], ACT.Identity,
                                               bias=vec[:, V1["dt_b"] + e:V1["dt_b"] + e + 1]), drained, f"DT{e}", at)
                    if n == 10:
                        wait_drained(act, f"DT{KE - 1}", at)
                        act.activation(ez[:], z[:], ACT.Abs).then_inc(s_abs, 1)
                        act.wait_ge(s_abs, q + 1)
                        act.activation(ez[:], ez[:], ACT.Exp, scale=-1.0).then_inc(s_ez, 1)
                    if n == 12:
                        act.wait_ge(s_dl, q * 3 + 1)
                        act.activation(cv[:], cv[:], ACT.Ln).then_inc(s_ln, 1)

            def step(at, i, h, n, last):
                for g, of_next in spread_at(n):
                    if g[0] == "B" and not (last and of_next):
                        b_row(i + 1 if of_next else i, int(g[1:]), at)
                if n < NST - 1:
                    decays(i, h, n + 1)
                elif not last:
                    decays(i + 1, 1 - h, 0)

            def end(at, i, h):
                act.wait_ge(mo_out, i * 16 + 16)
                for j in range(2):
                    wait_filled(act, f"O{j}", at)
                    inc(act.activation(mo[:, 2 * j:2 * j + 2], tile_of(f"O{j}", at)[:].rearrange("p (s d) -> p s d", s=2),
                                       ACT.Copy), drained, f"O{j}", at)

            ahead0 = ahead_of

            def ahead_first(at, q, h, slots):
                ahead0(at, q, h, slots)
                if at[0] == "first":
                    b_row(0, 0, START)
                    b_row(0, 1, START)
                    decays(0, 0, 0)

            program(act, ahead_first, step, end)

        @block.vector
        def _(dve):
            dve.wait_ge(s_prep, 1)
            dve.tensor_scalar(A[:], A[:], -1.0, None, ALU.mult).then_inc(s_A, 1)
            for k in range(KD):
                dve.tensor_scalar(w_si[:, k], w_si[:, k], vec[:, V1["norm_w"] + k:V1["norm_w"] + k + 1], None,
                                  ALU.mult).then_inc(s_prep, 1)
            dve.sem_inc(s_scan, 8)
            dve.sem_inc(s_yf, KE)
            dve.wait_ge(s_pad, 1)

            def ahead_of(at, q, h, slots):
                for n in slots:
                    if 1 <= n < KE + 1:
                        e = n - 1
                        w = [vec[:, V1["conv_w"] + e * TAPS + k:V1["conv_w"] + e * TAPS + k + 1] for k in range(TAPS)]
                        base = q * (KE * TAPS) + e * TAPS
                        if h == 1:
                            dve.tensor_copy(xpad[1][:, e, 0:PAD], xpad[0][:, e, T:T + PAD]).then_inc(s_pad, 1)
                            dve.wait_ge(s_pad, (q - 1) * 2 + (e + 2))
                        wait_drained(dve, f"IN{e}", at)
                        dve.tensor_scalar(cv[:, e], xpad[h][:, e, 0:T], w[0], vec[:, V1["conv_b"] + e:V1["conv_b"] + e + 1],
                                          ALU.mult, ALU.add).then_inc(s_conv, 1)
                        for k in range(1, TAPS):
                            dve.wait_ge(s_conv, base + k)
                            dve.scalar_tensor_tensor(out=cv[:, e], in0=xpad[h][:, e, k:k + T], scalar=w[k], in1=cv[:, e],
                                                     op0=ALU.mult, op1=ALU.add).then_inc(s_conv, 1)
                    if n == 7:
                        dve.wait_ge(s_bca, q * 2 + 1)
                        inc(dve.tensor_tensor(bcr[:], tile_of("BC", at)[0:2 * NST, :], bc3[h][0:2 * NST, :], ALU.subtract),
                            drained, "BC", at)
                        dve.sem_inc(s_bcd, 1)
                        wait_drained(dve, "BC", at)
                        dve.tensor_copy(bc2[:], bcr[:]).then_inc(s_bcd, 1)
                        dve.wait_ge(s_bcd, q * 3 + 2)
                        dve.tensor_tensor(bc3[h][4 * NST:6 * NST, :], bcr[:], bc2[:], ALU.subtract).then_inc(s_bcd, 1)
                    if n == 11:
                        dve.wait_ge(s_ez, q + 1)
                        dve.tensor_scalar(cv[:], ez[:], 1.0, None, ALU.add).then_inc(s_w, 1)
                        dve.wait_ge(s_w, q + 1)
                        dve.scalar_tensor_tensor(out=ez[:], in0=cv[:], scalar=-1.0, in1=ez[:], op0=ALU.add,
                                                 op1=ALU.subtract).then_inc(s_dl, 1)
                    if n == 13:
                        dve.wait_ge(s_ln, q + 1)
                        dve.tensor_tensor(ez[:], cv[:], ez[:], ALU.subtract).then_inc(s_dl, 1)
                        dve.wait_ge(s_dl, q * 3 + 2)
                        dve.scalar_tensor_tensor(out=dl[h][:], in0=z[:], scalar=0.0, in1=ez[:], op0=ALU.max,
                                                 op1=ALU.add).then_inc(s_dl, 1)
                    if n == 14:
                        dve.wait_ge(s_dl, q * 3 + 3)
                        dve.wait_ge(s_xs, q * KE + KE)
                        dve.tensor_tensor(ux[h][:], dl[h][:], xs[h][:], ALU.mult).then_inc(s_ux, 1)

            def step(at, i, h, n, last):
                here = at_of(at, f"C{n}")
                if n == 0:
                    dve.wait_ge(s_yf, i * KE + KE)
                else:
                    wait_drained(dve, f"C{n - 1}", at_of(at, f"C{n - 1}"))
                if h == 0 and n > 0:
                    dve.wait_ge(s_carry, i * (NST // 2) + n)
                dve.wait_ge(s_bx, i * NST + (2 + n + 1))
                for e in range(KE):
                    dve.wait_ge(s_exp, i * (NST * KE) + (KE * n + e + 1))
                    if h == 1 and e == 0:
                        dve.wait_ge(s_carry, (i - 1) * (NST // 2) + (n + 1))
                    dve.tensor_tensor_scan(hh[:, 0, e], dA[:, n % 2, e], bx[:, n % 2, e],
                                           0.0 if h == 0 else carry[:, n, e:e + 1], ALU.mult, ALU.add).then_inc(s_scan, 1)
                wait_filled(dve, f"C{n}", here)
                dve.wait_ge(s_scan, i * (NST * KE) + (8 + KE * (n + 1)))
                dve.wait_ge(s_y, i * NST + (n + 1))
                inc(dve.tensor_tensor(hc[:, n % 2], hh[:, 0],
                                      tile_of(f"C{n}", here)[:].rearrange("p (o t) -> p o t", o=1).to_broadcast([P, KE, T]),
                                      ALU.mult), drained, f"C{n}", here)
                if h == 0:
                    dve.tensor_copy(carry[:, n, :], hh[:, 0, :, T - 1]).then_inc(s_carry, 1)

            def end(at, i, h):
                dve.wait_ge(s_y, i * NST + (2 + NST))
                wait_filled(dve, "O1", at_of(at, "C0"))
                for e in range(KE):
                    dve.scalar_tensor_tensor(out=y1[:, e], in0=xs[h][:, e], scalar=vec[:, V1["W_D"] + e:V1["W_D"] + e + 1],
                                             in1=ybank[e][:], op0=ALU.mult, op1=ALU.add).then_inc(s_yf, 1)
                for e in range(KE):
                    dve.wait_ge(s_yf, i * KE + (KE + e + 1))
                    dve.tensor_tensor(y1[:, e], y1[:, e], sk[h][:, e], ALU.mult).then_inc(s_y2, 1)

            program(dve, ahead_of, step, end)

        @block.tensor
        def _(pe):
            mm = pe.matmul
            pe.wait_ge(w_in, 16 * len(w_loads))
            pe.wait_ge(s_prep, 1 + KD)
            pe.wait_ge(s_id, 2)
            pe.wait_ge(s_sel, 4)
            pe.sem_inc(s_y, 2)

            def spread(g, q, h, at):
                n = int(g[1:]) + (NST if g[0] == "C" else 0)
                wait_bank(pe, g, at)
                if g == "B0":
                    pe.wait_ge(s_bca, q * 2 + 2)
                    pe.wait_ge(s_bcd, q * 3 + 3)
                inc(mm(tile_of(g, at)[:], sel[:, n, :], bc3[h][:], start=True, stop=True), filled, g, at)

            def ahead_of(at, q, h, slots):
                for n in slots:
                    for g in ahead[n]:
                        wait_bank(pe, g, at)
                        out = tile_of(g, at)
                        if g[:2] in ("IN", "SK"):
                            e = int(g[2:])
                            if g == "IN0":
                                pe.wait_ge(xr_in, q * 16 + 16)
                            col = (E_IN if g[:2] == "IN" else 0) + e * P
                            for k in range(KD):
                                last = mm(out[:], w_si[:, k, col:col + P], xr[:, k], start=(k == 0), stop=(k == KD - 1))
                        elif g in ("BC", "DR"):
                            pe.wait_ge(s_xs, q * KE + KE)
                            cols = slice(0, 2 * NST) if g == "BC" else slice(2 * NST, 2 * NST + DR)
                            for e in range(KE):
                                last = mm(out[0:cols.stop - cols.start, :], w_x[:, e, cols], xs[h][:, e],
                                          start=(e == 0), stop=(e == KE - 1))
                        else:
                            e = int(g[2:])
                            wait_drained(pe, "DR", at)
                            last = mm(out[:], w_dt[:, e * P:(e + 1) * P], dr[:], start=True, stop=True)
                        inc(last, filled, g, at)
                if at[0] == "first":
                    for g in first[-6:]:
                        if g in ("B0", "B1", "C0"):
                            spread(g, q, h, at)
                            continue
                        wait_bank(pe, g, at)
                        pe.sem_inc(filled[bank_of(g, at)], 1)
                        pe.sem_inc(drained[bank_of(g, at)], 1)

            def step(at, i, h, n, last):
                for g, of_next in spread_at(n):
                    if not of_next:
                        spread(g, i, h, at)
                    elif not last:
                        spread(g, i + 1, 1 - h, at)
                here = at_of(at, f"C{n}")
                wait_drained(pe, f"C{n}", here)
                if n == 0:
                    pe.wait_ge(s_yf, i * KE + KE)
                for e in range(KE):
                    last_mm = mm(ybank[e][:], ident[:], hc[:, n % 2, e], start=(n == 0), stop=(n == NST - 1))
                last_mm.then_inc(s_y, 1)

            def end(at, i, h):
                pe.wait_ge(s_y2, i * KE + KE)
                for j in range(2):
                    wait_bank(pe, f"O{j}", at)
                    for s in (2 * j, 2 * j + 1):
                        for e in range(KE):
                            last = mm(tile_of(f"O{j}", at)[:, (s % 2) * D:(s % 2 + 1) * D], y1[:, e, s * P:(s + 1) * P],
                                      w_out[:, e], start=(e == 0 and s % 2 == 0), stop=(e == KE - 1 and s % 2 == 1),
                                      skip_group_check=True)
                    inc(last, filled, f"O{j}", at)

            program(pe, ahead_of, step, end)


NE = 8
TOPK = 2
FF = 1024
KF = FF // P
NJ = NTOK // P
NPICK = TOPK * NJ
S = 256
NT_NEED = (NTOK * TOPK + NE * (S - 1)) // S
NT = NT_NEED + NT_NEED % 2
NSLOT = NT * S
TMAX = NTOK // S


def routing(nc, dram):
    with ExitStack() as ctx:
        def sb(name, shape, dt=F32):
            return ctx.enter_context(nc.sbuf_tensor("r_" + name, shape, dt))

        def sem(name):
            return ctx.enter_context(nc.semaphore("r_" + name))

        ps_before = ctx.enter_context(nc.psum_tensor("r_ps_before", [P, NPICK * NE], F32))
        ps_total = ctx.enter_context(nc.psum_tensor("r_ps_total", [P, NPICK * NE], F32))
        rows = sb("rows", [P, NJ, D])
        zero = sb("zero", [P, 8 * D])
        lg = sb("lg", [P, NJ, NE])
        m8 = sb("m8", [P, NJ, 8])
        i8 = sb("i8", [P, NJ, 8], U32)
        pick = sb("pick", [P, TOPK, NJ])
        oh = sb("oh", [P, NPICK, NE])
        wts = sb("wts", [P, TOPK, NJ])
        ex = sb("ex", [P, 3, NJ])
        upper = sb("upper", [P, P])
        ones = sb("ones", [P, P])
        io_e = sb("io_e", [P, NE])
        io_m = sb("io_m", [P, TMAX])
        io_t = sb("io_t", [1, NT])
        tot = sb("tot", [P, NE, NPICK])
        incl = sb("incl", [P, NE, NPICK])
        cmp = sb("cmp", [P, NE, TMAX])
        nt = sb("nt", [P, NE])
        tend = sb("tend", [P, NE])
        base = sb("base", [P, NE])
        onesrow = ones[:, 0:NPICK]
        before = sb("before", [P, NPICK, NE])
        dstf = sb("dstf", [P, NPICK])
        dst = sb("dst", [P, NPICK], I32)
        cmpt = sb("cmpt", [1, NT, NE])
        texf = sb("texf", [1, NT])
        tex = sb("tex", [1, NT], I32)
        lg_in, rows_in, zero_out = sem("lg_in"), sem("rows_in"), sem("zero_out")
        s_c, s_z, s_d, s_ex, s_mm, s_sc, s_out = (sem("c"), sem("z"), sem("d"), sem("ex"), sem("mm"), sem("sc"),
                                                  sem("out"))
        block = ctx.enter_context(nc.Block())

        @block.gpsimd
        def _(pool):
            pool.memset(zero[:], 0.0).then_inc(s_z, 1)
            pool.memset(ones[:], 1.0).then_inc(s_c, 1)
            pool.wait_ge(s_c, 1)
            pool.affine_select(out=upper[:], in_=ones[:], compare_op=ALU.is_gt, fill=0.0, base=0, pattern=[[1, P]],
                               channel_multiplier=-1).then_inc(s_c, 1)
            pool.iota(io_e[:], pattern=[[1, NE]], base=0, channel_multiplier=0,
                      allow_small_or_imprecise_dtypes=True).then_inc(s_c, 1)
            pool.iota(io_m[:], pattern=[[S, TMAX]], base=0, channel_multiplier=0,
                      allow_small_or_imprecise_dtypes=True).then_inc(s_c, 1)
            pool.iota(io_t[:], pattern=[[1, NT]], base=0, channel_multiplier=0,
                      allow_small_or_imprecise_dtypes=True).then_inc(s_c, 1)
            pool.wait_ge(zero_out, 16 * (NSLOT // (8 * P)))
            pool.wait_ge(rows_in, 16)
            pool.wait_ge(s_d, D_STEPS)
            for a in range(NPICK):
                pool.indirect_dma_start(dram["xg"][:, :], bass.IndirectOffsetOnAxis(ap=dst[:, a:a + 1], axis=0),
                                        rows[:, a % NJ, :], None).then_inc(s_sc, 16)
            pool.wait_ge(s_sc, 16 * NPICK)

        @block.sync
        def _(sp):
            sp.dma_start(lg[:], dram["logits"]).then_inc(lg_in, 16)
            sp.dma_start(rows[:], dram["xn1"].rearrange("(j p) d -> p j d", p=P)).then_inc(rows_in, 16)
            sp.wait_ge(s_z, 1)
            for i in range(NSLOT // (8 * P)):
                sp.dma_start(dram["xg"][i * 8 * P:(i + 1) * 8 * P, :].rearrange("(p a) d -> p (a d)", a=8),
                             zero[:]).then_inc(zero_out, 16)
            sp.wait_ge(s_d, D_STEPS)
            sp.dma_start(dram["dst"], dst[:]).then_inc(s_out, 16)
            sp.dma_start(dram["tex"], tex[:]).then_inc(s_out, 16)
            sp.dma_start(dram["wts"], wts[:].rearrange("p k j -> p (k j)")).then_inc(s_out, 16)
            sp.wait_ge(s_out, 48)

        @block.scalar
        def _(act):
            act.wait_ge(s_d, 2 * NJ + 1)
            act.activation(ex[:, 1], ex[:, 0], ACT.Exp).then_inc(s_ex, 1)

        @block.tensor
        def _(pe):
            pe.wait_ge(s_c, 5)
            pe.wait_ge(s_d, 2 * NJ + 1 + 1 + 1)
            r = oh[:].rearrange("p a e -> p (a e)")
            pe.matmul(ps_before[:], upper[:], r, start=True, stop=True).then_inc(s_mm, 1)
            pe.matmul(ps_total[:], ones[:], r, start=True, stop=True).then_inc(s_mm, 1)

        @block.vector
        def _(dve):
            n = [0]

            def step(ins, wait=True):
                ins.then_inc(s_d, 1)
                n[0] += 1
                if wait:
                    dve.wait_ge(s_d, n[0])

            def over(row, k):
                return row.rearrange("p (o n) -> p o n", o=1).to_broadcast([row.shape[0], k, row.shape[1]])

            dve.wait_ge(lg_in, 16)
            for j in range(NJ):
                step(dve.max(m8[:, j], lg[:, j]), False)
            dve.wait_ge(s_d, NJ)
            for j in range(NJ):
                step(dve.max_index(i8[:, j], m8[:, j], lg[:, j]), False)
            step(dve.tensor_tensor(ex[:, 0], m8[:, :, 1], m8[:, :, 0], ALU.subtract))
            step(dve.tensor_copy(pick[:], i8[:, :, 0:TOPK].rearrange("p j k -> p k j")))
            dve.wait_ge(s_c, 5)
            picks = pick[:].rearrange("p k (j o) -> p (k j) o", o=1).to_broadcast([P, NPICK, NE])
            step(dve.tensor_tensor(oh[:], picks, over(io_e[:], NPICK), ALU.is_equal))
            dve.wait_ge(s_ex, 1)
            step(dve.tensor_scalar(ex[:, 2], ex[:, 1], 1.0, None, ALU.add))
            step(dve.reciprocal(wts[:, 0], ex[:, 2]))
            step(dve.tensor_tensor(wts[:, 1], ex[:, 1], wts[:, 0], ALU.mult))
            dve.wait_ge(s_mm, 2)
            step(dve.tensor_copy(tot[:], ps_total[:].rearrange("p (a e) -> p e a", e=NE)))
            for e in range(NE):
                step(dve.tensor_tensor_scan(incl[:, e], onesrow, tot[:, e], 0.0, ALU.mult, ALU.add), False)
            dve.wait_ge(s_d, n[0])
            step(dve.tensor_tensor(cmp[:], over(io_m[:], NE), incl[:, :, NPICK - 1:NPICK].to_broadcast([P, NE, TMAX]), ALU.is_lt))
            step(dve.tensor_reduce(nt[:], cmp[:], AX_X, ALU.add))
            step(dve.tensor_tensor_scan(tend[:], ones[:, 0:NE], nt[:], 0.0, ALU.mult, ALU.add))
            step(dve.tensor_tensor(base[:], tend[:], nt[:], ALU.subtract))
            step(dve.tensor_scalar(base[:], base[:], float(S), None, ALU.mult))
            step(dve.tensor_tensor(incl[:], incl[:], tot[:], ALU.subtract))
            step(dve.tensor_tensor(before[:], ps_before[:].rearrange("p (a e) -> p a e", e=NE),
                                   incl[:].rearrange("p e a -> p a e"), ALU.add))
            step(dve.tensor_tensor(before[:], before[:], over(base[:], NPICK), ALU.add))
            step(dve.tensor_tensor(before[:], before[:], oh[:], ALU.mult))
            step(dve.tensor_reduce(dstf[:], before[:], AX_X, ALU.add))
            step(dve.tensor_copy(dst[:], dstf[:]))
            step(dve.tensor_tensor(cmpt[:], io_t[:].rearrange("p (t o) -> p t o", o=1).to_broadcast([1, NT, NE]),
                                   over(tend[0:1, :], NT), ALU.is_ge))
            step(dve.tensor_reduce(texf[:], cmpt[:], AX_X, ALU.add))
            step(dve.tensor_scalar(texf[:], texf[:], float(NE - 1), None, ALU.min))
            step(dve.tensor_copy(tex[:], texf[:]))
            assert n[0] == D_STEPS, n[0]


D_STEPS = 2 * NJ + 3 + 3 + 1 + NE + 15


def experts(nc, dram):
    with ExitStack() as ctx:
        def sb(name, shape, dt=F32):
            return ctx.enter_context(nc.sbuf_tensor("e_" + name, shape, dt))

        def sem(name):
            return ctx.enter_context(nc.semaphore("e_" + name))

        NS = S // P
        HR = 4
        turned = [ctx.enter_context(nc.psum_tensor(f"e_turned{i}", [P, KD, S], F32)) for i in range(2)]
        hbank = [ctx.enter_context(nc.psum_tensor(f"e_h{i}", [P, 2, S], F32)) for i in range(HR)]
        obank = [ctx.enter_context(nc.psum_tensor(f"e_o{i}", [P, NS, D], F32)) for i in range(2)]
        ident = sb("ident", [P, P])
        ones = sb("ones", [1, P])
        tex = sb("tex", [1, NT], I32)
        w1 = [sb(f"w1{i}", [P, KD, 2 * FF]) for i in range(2)]
        w2 = [sb(f"w2{i}", [P, KF, D]) for i in range(2)]
        b1 = [sb(f"b1{i}", [P, 2 * KF]) for i in range(2)]
        b2 = [sb(f"b2{i}", [1, D]) for i in range(2)]
        xg = [sb(f"xg{i}", [P, NS, D]) for i in range(2)]
        xT = [sb(f"xT{i}", [P, KD, S]) for i in range(2)]
        sg = sb("sg", [P, 2, S])
        ac = [sb(f"ac{i}", [P, KF, S]) for i in range(2)]
        yo = [sb(f"yo{i}", [P, NS, D]) for i in range(2)]
        tex_in, s_id = sem("tex_in"), sem("id")
        w_in = [sem(f"w_in{i}") for i in range(2)]
        x_in = [sem(f"x_in{i}") for i in range(2)]
        y_out = [sem(f"y_out{i}") for i in range(2)]
        s_turn, s_xT, s_h, s_sg, s_ac, s_o, s_y = (sem("turn"), sem("xT"), sem("h"), sem("sg"), sem("ac"), sem("o"),
                                                   sem("y"))
        block = ctx.enter_context(nc.Block())

        @block.gpsimd
        def _(pool):
            identity(pool, ident, s_id)
            pool.memset(ones[:], 1.0).then_inc(s_id, 1)

        @block.sync
        def _(sp):
            sp.dma_start(tex[:], dram["tex"]).then_inc(tex_in, 16)
            sp.wait_ge(tex_in, 16)

            def load(t, i):
                e = sp.value_load(tex[0:1, bass.ds(t, 1)], min_val=0, max_val=NE - 1)
                sp.wait_ge(s_o, t + 1)
                sp.wait_ge(tex_in, 16)
                sp.dma_start(xg[i][:], dram["xg"][bass.ds(t * S, S), :].rearrange("(s p) d -> p s d", p=P)).then_inc(x_in[i], 16)
                sp.dma_start(w1[i][:], dram["w1"][bass.ds(e * P, P), :, :]).then_inc(w_in[i], 16)
                sp.dma_start(b1[i][:], dram["b1"][bass.ds(e * P, P), :]).then_inc(w_in[i], 16)
                sp.dma_start(b2[i][:], dram["b2"][bass.ds(e, 1), :]).then_inc(w_in[i], 16)
                sp.dma_start(w2[i][:], dram["w2"][bass.ds(e * P, P), :, :]).then_inc(w_in[i], 16)

            def store(t, i):
                sp.wait_ge(s_y, t + 3)
                sp.dma_start(dram["yg"][bass.ds(t * S, S), :].rearrange("(s p) d -> p s d", p=P), yo[i][:]).then_inc(y_out[i], 16)

            load(0, 0)
            load(1, 1)
            with sp.Fori(0, NT // 2 - 1) as g:
                for i in range(2):
                    load(g * 2 + (2 + i), i)
                    store(g * 2 + i, i)
            for i in range(2):
                store(NT - 2 + i, i)
            for i in range(2):
                sp.wait_ge(y_out[i], 16 * (NT // 2 + 1))

        @block.scalar
        def _(act):
            for i in range(2):
                act.sem_inc(y_out[i], 16)
            with act.Fori(0, NT // 2) as g:
                for i in range(2):
                    t = g * 2 + i
                    act.wait_ge(s_turn, t + 1)
                    act.activation(xT[i][:], turned[i][:], ACT.Copy).then_inc(s_xT, 1)
                    for m in range(KF):
                        act.wait_ge(s_h, t * KF + (m + 1))
                        if m == 0:
                            act.wait_ge(w_in[i], g * 64 + 64)
                        act.wait_ge(s_ac, t * KF + (m + 1))
                        act.activation(sg[:, m % 2], hbank[m % HR][:, 1], ACT.Silu,
                                       bias=b1[i][:, KF + m:KF + m + 1]).then_inc(s_sg, 1)
                    act.wait_ge(s_o, t + 3)
                    act.wait_ge(y_out[i], g * 16 + 16)
                    act.activation(yo[i][:], obank[i][:], ACT.Copy).then_inc(s_y, 1)

        @block.vector
        def _(dve):
            dve.sem_inc(s_ac, 2)
            dve.sem_inc(s_o, 2)
            dve.sem_inc(s_y, 2)
            with dve.Fori(0, NT // 2) as g:
                for i in range(2):
                    t = g * 2 + i
                    for m in range(KF):
                        dve.wait_ge(s_sg, t * KF + (m + 1))
                        if m == 0:
                            dve.wait_ge(s_o, t + 1)
                        dve.scalar_tensor_tensor(out=ac[i][:, m], in0=hbank[m % HR][:, 0], scalar=b1[i][:, m:m + 1],
                                                 in1=sg[:, m % 2], op0=ALU.add, op1=ALU.mult).then_inc(s_ac, 1)

        @block.tensor
        def _(pe):
            mm = pe.matmul
            pe.wait_ge(s_id, 3)

            def turn(t, g, i):
                pe.wait_ge(x_in[i], g * 16 + 16)
                for k in range(KD):
                    for s in range(NS):
                        last = pe.transpose(turned[i][:, k, s * P:(s + 1) * P], xg[i][:, s, k * P:(k + 1) * P], ident[:])
                last.then_inc(s_turn, 1)

            def tile(t, g, i, nxt):
                pe.wait_ge(s_xT, t + 1)
                pe.wait_ge(w_in[i], g * 64 + 64)
                for m in range(KF):
                    if m >= HR or not isinstance(t, int) or t > 0:
                        pe.wait_ge(s_ac, t * KF + (2 + m + 1 - HR))
                    for j in range(2):
                        for k in range(KD):
                            last = mm(hbank[m % HR][:, j], w1[i][:, k, j * FF + m * P:j * FF + (m + 1) * P], xT[i][:, k],
                                      start=(k == 0 and j == 0), stop=(k == KD - 1 and j == 1), skip_group_check=True)
                    last.then_inc(s_h, 1)
                if nxt is not None:
                    turn(*nxt)
                pe.wait_ge(s_y, t + 1)
                for s in range(NS):
                    mm(obank[i][:, s], ones[:], b2[i][:], start=(s == 0), stop=False, skip_group_check=True)
                for m in range(KF):
                    pe.wait_ge(s_ac, t * KF + (2 + m + 1))
                    for s in range(NS):
                        last = mm(obank[i][:, s], ac[i][:, m, s * P:(s + 1) * P], w2[i][:, m], start=False,
                                  stop=(m == KF - 1 and s == NS - 1), skip_group_check=True)
                last.then_inc(s_o, 1)

            turn(0, 0, 0)
            tile(0, 0, 0, (1, 0, 1))
            with pe.Fori(0, NT // 2 - 1) as g:
                tile(g * 2 + 1, g, 1, (g * 2 + 2, g + 1, 0))
                tile(g * 2 + 2, g + 1, 0, (g * 2 + 3, g + 1, 1))
            tile(NT - 1, NT // 2 - 1, 1, None)


def combine(nc, dram, out):
    with ExitStack() as ctx:
        def sb(name, shape, dt=F32):
            return ctx.enter_context(nc.sbuf_tensor("c_" + name, shape, dt))

        def sem(name):
            return ctx.enter_context(nc.semaphore("c_" + name))

        dst = sb("dst", [P, NPICK], I32)
        wts = sb("wts", [P, NPICK])
        ya = sb("ya", [P, NPICK, D])
        xa = sb("xa", [P, NJ, D])
        mo = sb("mo", [P, NJ, D])
        small_in, y_in, out_done = sem("small_in"), sem("y_in"), sem("out_done")
        x_in = [sem(f"x_in{i}") for i in range(NCH)]
        s_add, s_y1, s_y2 = sem("add"), sem("y1"), sem("y2")
        yj = [sem(f"yj{i}") for i in range(NCH)]
        block = ctx.enter_context(nc.Block())

        @block.sync
        def _(sp):
            sp.dma_start(dst[:], dram["dst"]).then_inc(small_in, 16)
            sp.dma_start(wts[:], dram["wts"]).then_inc(small_in, 16)
            for c in range(NCH):
                for tile, src in ((xa, dram["x1p"]), (mo, dram["mo"])):
                    sp.dma_start(tile[:, c * SUB:(c + 1) * SUB], src[c * T:(c + 1) * T, :].rearrange("(s p) d -> p s d", p=P)).then_inc(x_in[c], 16)
            for c in range(NCH):
                sp.wait_ge(s_y2, (c + 1) * SUB)
                sp.dma_start(out[c * T:(c + 1) * T, :].rearrange("(s p) d -> p s d", p=P), xa[:, c * SUB:(c + 1) * SUB]).then_inc(out_done, 16)
            sp.wait_ge(out_done, 16 * NCH)

        @block.gpsimd
        def _(pool):
            pool.wait_ge(small_in, 32)
            for c in range(NCH):
                for j in range(c * SUB, (c + 1) * SUB):
                    for k in range(TOPK):
                        a = k * NJ + j
                        pool.indirect_dma_start(ya[:, a, :], None, dram["yg"][:, :],
                                                bass.IndirectOffsetOnAxis(ap=dst[:, a:a + 1], axis=0)).then_inc(yj[c], 16)

        @block.vector
        def _(dve):
            dve.wait_ge(small_in, 32)
            for c in range(NCH):
                cs = slice(c * SUB, (c + 1) * SUB)
                dve.wait_ge(x_in[c], 32)
                dve.tensor_tensor(xa[:, cs], xa[:, cs], mo[:, cs], ALU.add).then_inc(s_add, 1)
                dve.wait_ge(s_add, c + 1)
                dve.wait_ge(yj[c], 16 * SUB * TOPK)
                for k, done in ((0, s_y1), (1, s_y2)):
                    for j in range(c * SUB, (c + 1) * SUB):
                        a = k * NJ + j
                        if k == 1:
                            dve.wait_ge(s_y1, j + 1)
                        dve.scalar_tensor_tensor(out=xa[:, j], in0=ya[:, a], scalar=wts[:, a:a + 1], in1=xa[:, j],
                                                 op0=ALU.mult, op1=ALU.add).then_inc(done, 1)


def kernel(**inputs):
    import numpy as np
    import concourse.bacc as bacc
    from concourse.bass_utils import run_bass_kernel_spmd

    a = {k: np.ascontiguousarray(v) for k, v in inputs.items()}
    g = lambda n: a["L0_attn_" + n]
    f = lambda n: a["L0_ffn_" + n]
    m = lambda n: a["L1_attn_" + n]
    x = lambda n: a["L1_ffn_" + n]

    def blocks(w):
        return np.ascontiguousarray(w.reshape(-1, P, w.shape[1]).transpose(1, 0, 2))

    def cols(v):
        return np.ascontiguousarray(v.reshape(-1, P, v[0].size).transpose(1, 0, 2).reshape(P, -1))

    arrays = {
        "x": np.concatenate([g("hidden_states").reshape(NTOK, D), np.zeros((T, D), np.float32)]),
        "w_p": blocks(np.concatenate([g("fc_r_w"), g("fc_i_w"), g("fc_w"), g("fc_gate_w")]).T),
        "w_m": blocks(np.concatenate([g("mlp_gate_w"), g("mlp_fc_w")]).T),
        "w_o": blocks(g("out_w").T),
        "w_f": blocks(f("w_fc").T),
        "w_j": blocks(f("w_proj").T),
        "vec0": np.concatenate([cols(v) for v in (g("fc_r_b"), g("fc_i_b"), g("fc_b"), g("fc_gate_b"), g("mlp_gate_b"),
                                                  g("mlp_fc_b"), g("norm_w"), g("norm2_w"), g("alpha").reshape(-1))], axis=1),
        "out_b": g("out_b").reshape(1, D),
        "gate_b": x("gate_b").reshape(1, NE),
        "gate_w": blocks(x("gate_w")),
        "low_v": f("v"),
        "low_b": np.ascontiguousarray(f("fast_b").T),
        "low_u": np.ascontiguousarray(f("u").T),
        "low_g": f("gate").reshape(1, 1),
        "w_si": blocks(np.concatenate([m("skip_w"), m("in_w")]).T),
        "w_x": blocks(np.concatenate([m("wB"), m("wC"), m("wd1")]).T),
        "w_dt": np.ascontiguousarray(m("wd2").T),
        "w_out": blocks(m("out_w").T),
        "vec1": np.concatenate([cols(v) for v in (m("norm_w"), m("conv_w"), m("conv_b"), m("wd2_b"), m("A_log"), m("W_D"))], axis=1),
        "w1": np.ascontiguousarray(x("w1").reshape(NE, KD, P, 2 * FF).transpose(0, 2, 1, 3).reshape(NE * P, KD, 2 * FF)),
        "w2": np.ascontiguousarray(x("w2").reshape(NE, KF, P, D).transpose(0, 2, 1, 3).reshape(NE * P, KF, D)),
        "b1": np.ascontiguousarray(x("b1").reshape(NE, 2 * KF, P).transpose(0, 2, 1).reshape(NE * P, 2 * KF)),
        "b2": x("b2"),
    }
    nc = bacc.Bacc("TRN2", target_bir_lowering=False, num_devices=1)
    dram = {n: nc.dram_tensor("in_" + n, v.shape, F32, kind="ExternalInput").ap() for n, v in arrays.items()}
    out = nc.dram_tensor("out", (NTOK, D), F32, kind="ExternalOutput").ap()
    program(nc, dram, out)
    r = run_bass_kernel_spmd(nc, [{"in_" + n: v for n, v in arrays.items()}], core_ids=[0])
    return r.results[0]["out"].reshape(NTOK // SEQ, SEQ, D)


def program(nc, dram, out):
    dram = dict(dram)
    for name, shape, dt in (("x1p", (NTOK, D), F32), ("xn1", (NTOK, D), F32), ("xrT", (NCH * P, KD, T), F32),
                            ("logits", (P, NJ, NE), F32), ("mo", (NTOK, D), F32), ("xg", (NSLOT, D), F32),
                            ("yg", (NSLOT, D), F32), ("dst", (P, NPICK), I32), ("tex", (1, NT), I32),
                            ("wts", (P, NPICK), F32)):
        dram[name] = nc.dram_tensor("scratch_" + name, shape, dt, kind="Internal").ap()
    layer0(nc, dram)
    routing(nc, dram)
    mamba(nc, dram)
    experts(nc, dram)
    combine(nc, dram, out)
```

```python
from contextlib import ExitStack

import concourse.bass as bass
from concourse import mybir

P = 128
F32 = mybir.dt.float32
F32R = mybir.dt.float32r
BF16 = mybir.dt.bfloat16
I32 = mybir.dt.int32
U32 = mybir.dt.uint32
ALU = mybir.AluOpType
ACT = mybir.ActivationFunctionType
AX_X = mybir.AxisListType.X

NTOK = 4096
SEQ = 1024
D = 256
KD = D // P
T = 512
NCH = NTOK // T
CPS = SEQ // T
SUB = T // P
MLP = 768
KM = MLP // P
HID = 1024
KH = HID // P
RANK = 16
EPS_LN = 1e-5
EPS_RMS0 = 1e-6
EPS_RMS1 = 1e-5
BANKS = 8

V0 = {}
_at = 0
for _name, _n in (("r_b", KD), ("i_b", KD), ("hs_b", KD), ("gate_b", KD), ("mg_b", KM), ("mf_b", KM),
                  ("norm_w", KD), ("norm2_w", KD), ("alpha", KD)):
    V0[_name] = _at
    _at += _n
NV0 = _at


def identity(pool, tile, done):
    pool.memset(tile[:, :], 0.0).then_inc(done, 1)
    pool.wait_ge(done, 1)
    pool.affine_select(out=tile[:, :], in_=tile[:, :], compare_op=ALU.not_equal, fill=1.0, base=0,
                       pattern=[[-1, P]], channel_multiplier=1).then_inc(done, 1)


NE = 8
TOPK = 2
FF = 1024
KF = FF // P
NJ = NTOK // P
NPICK = TOPK * NJ
S = 256
NT_NEED = (NTOK * TOPK + NE * (S - 1)) // S
NT = NT_NEED + NT_NEED % 2
NSLOT = NT * S
TMAX = NTOK // S

FMS = 6


def layer0(nc, dram):
    order = ([f"F{m}" for m in range(FMS)] + ["MS"] + [f"F{m}" for m in range(FMS, KH)]
             + [g for m in range(KM) for g in (f"MG{m}", f"MF{m}")] + ["O0", "O1"]
             + ["XT0", "XT1", "HT0", "HT1", "R0", "R1", "I0", "I1", "H0", "H1", "GA0", "GA1"]
             + ["N0", "N1", "Q0", "Q1", "L"])
    assert len(order) % BANKS == 0
    uses = len(order) // BANKS
    place = {g: (p % BANKS, p // BANKS) for p, g in enumerate(order)}

    with ExitStack() as ctx:
        def sb(name, shape, dt=F32):
            return ctx.enter_context(nc.sbuf_tensor(name, shape, dt))

        def sem(name):
            return ctx.enter_context(nc.semaphore(name))

        bank = [ctx.enter_context(nc.psum_tensor(f"bank{i}", [P, T], F32)) for i in range(BANKS)]
        w_p = sb("w_p", [P, KD, 4 * D])
        w_m = sb("w_m", [P, KD, 2 * MLP])
        w_o = sb("w_o", [P, KM, D])
        w_f = sb("w_f", [P, KD, HID])
        w_j = sb("w_j", [P, KH, D])
        vec = sb("vec", [P, NV0])
        brow = sb("brow", [1, D])
        gb = sb("gb", [P, 8])
        gw = sb("gw", [P, KD, 8])
        low_v = sb("low_v", [RANK, D])
        low_b = sb("low_b", [RANK, RANK])
        low_u = sb("low_u", [RANK, HID])
        low_g = sb("low_g", [RANK, 1])
        low_z = sb("low_z", [RANK, D])
        ident = sb("ident", [P, P])
        ones = sb("ones", [P, P])
        inv_d = sb("inv_d", [P, P])
        inv_h = sb("inv_h", [P, P])
        neghalf = sb("neghalf", [P, SUB])
        eps_ln, eps_rms0, eps_rms1 = (sb(f"eps_{n}", [P, SUB]) for n in ("ln", "rms0", "rms1"))
        sp = sb("sp", [P, 3, KD])
        eps0 = sb("eps0", [P, 1])
        ca = sb("ca", [P, KD])
        xt = sb("xt", [P, SUB, D])
        xres = sb("xres", [P, SUB, D])
        xn = sb("xn", [P, SUB, D])
        hn = sb("hn", [P, SUB, D])
        x1 = sb("x1", [P, SUB, D])
        xn1 = sb("xn1", [P, SUB, D])
        xr1 = sb("xr1", [P, SUB, D])
        x1p = sb("x1p", [P, SUB, D])
        stats = sb("stats", [P, SUB, 6])
        mv = sb("mv", [P, SUB, 2])
        stats1 = sb("stats1", [P, SUB, 6])
        seen = sb("seen", [P, SUB])
        mv1 = sb("mv1", [P, SUB, 2])
        small = sb("small", [P, 6, SUB])
        small1 = sb("small1", [P, 6, SUB])
        lg = sb("lg", [P, NCH * SUB, 8])
        xnT = sb("xnT", [P, KD, T])
        hT = sb("hT", [P, KD, T])
        rT = sb("rT", [P, KD, T])
        iT = sb("iT", [P, KD, T])
        gT = sb("gT", [P, KD, T])
        tT = sb("tT", [P, KD, T])
        aT = sb("aT", [P, KD, T])
        qT = sb("qT", [P, KD, T])
        oT = sb("oT", [P, KD, T])
        hs2 = sb("hs2", [P, KD, T])
        sq = sb("sq", [P, KD, T])
        rms = sb("rms", [P, T])
        rinv = sb("rinv", [P, T])
        h2 = sb("h2", [P, KD, T])
        fT = sb("fT", [P, KH, T])
        mg = sb("mg", [P, 2, T])
        mT = sb("mT", [P, KM, T])
        xn1T = sb("xn1T", [P, KD, T])
        xr1T = sb("xr1T", [P, KD, T])
        zero = sb("zero", [P, 8 * D])
        carry = sb("carry", [P, KD])
        keep = sb("keep", [P, 1])

        filled = [sem(f"filled{i}") for i in range(BANKS)]
        drained = [sem(f"drained{i}") for i in range(BANKS)]
        weights_in = sem("weights_in")
        x_in = sem("x_in")
        xres_in = sem("xres_in")
        x1p_out, xn1_out, xrT_out, lg_out = sem("x1p_out"), sem("xn1_out"), sem("xrT_out"), sem("lg_out")
        s_id = sem("s_id")
        s_const = sem("s_const")
        s_zero, zero_out = sem("s_zero"), sem("zero_out")
        s_prep = sem("s_prep")
        s_prepa = sem("s_prepa")
        p_prep = sem("p_prep")
        s_st = sem("s_st")
        s_pw = sem("s_pw")
        s_ln = sem("s_ln")
        s_a = sem("s_a")
        s_a2 = sem("s_a2")
        s_q = sem("s_q")
        s_s = sem("s_s")
        s_scan = sem("s_scan")
        s_carry = sem("s_carry")
        s_og = sem("s_og")
        s_hs2 = sem("s_hs2")
        s_sq = sem("s_sq")
        s_rinv = sem("s_rinv")
        s_h2 = sem("s_h2")
        s_fsq = sem("s_fsq")
        s_st1 = sem("s_st1")
        s_pw1 = sem("s_pw1")
        s_l1 = sem("s_l1")
        block = ctx.enter_context(nc.Block())

        def wait_filled(eng, g, c):
            b, i = place[g]
            eng.wait_ge(filled[b], c * uses + (uses + i + 1))

        def wait_drained(eng, g, c):
            b, i = place[g]
            eng.wait_ge(drained[b], c * uses + (uses + i + 1))

        def wait_bank(pe, g, c):
            b, i = place[g]
            pe.wait_ge(drained[b], c * uses + (uses + i))

        def inc_filled(ins, g):
            ins.then_inc(filled[place[g][0]], 1)

        def inc_drained(ins, g):
            ins.then_inc(drained[place[g][0]], 1)

        def ps(g):
            return bank[place[g][0]]

        def rows(ap, c):
            return ap[bass.ds(c * T, T), :].rearrange("(s p) d -> p s d", p=P)

        w_loads = [(w_p, dram["w_p"]), (w_m, dram["w_m"]), (w_o, dram["w_o"]), (w_f, dram["w_f"]),
                   (w_j, dram["w_j"]), (vec, dram["vec0"]), (brow, dram["out_b"]),
                   (gb, dram["gate_b"].to_broadcast([P, 8])), (gw, dram["gate_w"]),
                   (low_v, dram["low_v"]), (low_b, dram["low_b"]), (low_u, dram["low_u"]),
                   (low_g, dram["low_g"].to_broadcast([RANK, 1]))]
        weights_all = 16 * len(w_loads)

        @block.sync
        def _(sp_):
            for dst, src in w_loads:
                sp_.dma_start(dst[:], src).then_inc(weights_in, 16)
            sp_.dma_start(xt[:], rows(dram["x"], 0)).then_inc(x_in, 16)
            sp_.wait_ge(s_zero, 1)
            for i in range(NSLOT // (8 * P)):
                sp_.dma_start(dram["xg"][i * 8 * P:(i + 1) * 8 * P, :].rearrange("(p a) d -> p (a d)", a=8),
                              zero[:]).then_inc(zero_out, 16)
            with sp_.Fori(0, NCH) as c:
                wait_drained(sp_, "O1", c - 1)
                sp_.dma_start(xres[:], rows(dram["x"], c)).then_inc(xres_in, 16)
                sp_.wait_ge(s_ln, c * 8 + 8)
                sp_.dma_start(xt[:], rows(dram["x"], c + 1)).then_inc(x_in, 16)
                sp_.wait_ge(s_l1, c * 12 + 12)
                sp_.dma_start(rows(dram["x1p"], c), x1p[:]).then_inc(x1p_out, 16)
                sp_.dma_start(rows(dram["xn1"], c), xn1[:]).then_inc(xn1_out, 16)
                wait_drained(sp_, "Q1", c)
                wait_drained(sp_, "Q0", c)
                sp_.dma_start(dram["xrT"][bass.ds(c * P, P), :, :], xr1T[:]).then_inc(xrT_out, 16)
            wait_drained(sp_, "L", NCH - 1)
            sp_.dma_start(dram["logits"], lg[:]).then_inc(lg_out, 16)
            sp_.wait_ge(lg_out, 16)
            sp_.wait_ge(zero_out, 16 * (NSLOT // (8 * P)))
            for s in (x1p_out, xn1_out, xrT_out):
                sp_.wait_ge(s, 16 * NCH + 16)

        @block.gpsimd
        def _(pool):
            identity(pool, ident, s_id)
            for tile, value in ((ones, 1.0), (inv_d, 1.0 / D), (inv_h, 1.0 / HID), (neghalf, -0.5),
                                (carry, 0.0), (keep, 1.0), (eps_ln, EPS_LN), (eps_rms0, EPS_RMS0),
                                (eps_rms1, EPS_RMS1)):
                pool.memset(tile[:], value).then_inc(s_const, 1)
            pool.memset(zero[:], 0.0).then_inc(s_zero, 1)
            pool.wait_ge(s_const, 9)

            def row_scales(sm, mvt, done, base, eps_rms):
                var = mvt[:, :, 1]
                pool.tensor_tensor(sm[:, 0], var, eps_ln[:], ALU.add).then_inc(done, 1)
                pool.wait_ge(done, base + 1)
                pool.tensor_tensor(sm[:, 1], sm[:, 0], neghalf[:], ALU.pow).then_inc(done, 1)
                pool.wait_ge(done, base + 2)
                pool.tensor_tensor(sm[:, 2], sm[:, 1], sm[:, 1], ALU.mult).then_inc(done, 1)
                pool.wait_ge(done, base + 3)
                pool.tensor_tensor(sm[:, 3], sm[:, 2], var, ALU.mult).then_inc(done, 1)
                pool.wait_ge(done, base + 4)
                pool.tensor_tensor(sm[:, 2], sm[:, 3], eps_rms[:], ALU.add).then_inc(done, 1)
                pool.wait_ge(done, base + 5)
                pool.tensor_tensor(sm[:, 4], sm[:, 2], neghalf[:], ALU.pow).then_inc(done, 1)
                pool.wait_ge(done, base + 6)
                pool.tensor_tensor(sm[:, 5], sm[:, 4], sm[:, 1], ALU.mult).then_inc(done, 1)

            pool.wait_ge(s_st, 9)
            row_scales(small, mv, s_pw, 0, eps_rms0)
            with pool.Fori(0, NCH) as c:
                pool.wait_ge(s_st, c * 9 + 18)
                row_scales(small, mv, s_pw, c * 7 + 7, eps_rms0)
                for m in range(KH):
                    wait_drained(pool, f"F{m}", c)
                    pool.tensor_tensor(fT[:, m], fT[:, m], fT[:, m], ALU.mult).then_inc(s_fsq, 1)
                pool.wait_ge(s_st1, c * 9 + 9)
                row_scales(small1, mv1, s_pw1, c * 7, eps_rms1)

        @block.scalar
        def _(act):
            act.wait_ge(weights_in, weights_all)
            al = vec[:, V0["alpha"]:V0["alpha"] + KD]
            act.activation(sp[:, 0], al, ACT.Abs).then_inc(s_prepa, 1)
            act.wait_ge(s_prepa, 1)
            act.activation(sp[:, 1], sp[:, 0], ACT.Exp, scale=-1.0).then_inc(s_prepa, 1)
            act.wait_ge(s_prepa, 2)
            act.activation(sp[:, 2], sp[:, 1], ACT.Ln, bias=1.0).then_inc(s_prepa, 1)
            act.activation(mT[:, 0:2 * KD], w_f[:].rearrange("p k (a n) -> p (k a) n", n=T), ACT.Abs).then_inc(s_prepa, 1)
            act.activation(fT[:, 0:KH // 2], w_j[:].rearrange("p (k a) n -> p k (a n)", a=2), ACT.Abs).then_inc(s_prepa, 1)

            def project(c):
                for k in range(KD):
                    wait_filled(act, f"XT{k}", c)
                    inc_drained(act.activation(xnT[:, k], ps(f"XT{k}")[:], ACT.Copy), f"XT{k}")
                for name, dst, b, f in (("R", rT, "r_b", ACT.Sigmoid), ("I", iT, "i_b", ACT.Sigmoid),
                                        ("GA", gT, "gate_b", ACT.Gelu)):
                    for k in range(KD):
                        wait_filled(act, f"{name}{k}", c)
                        inc_drained(act.activation(dst[:, k], ps(f"{name}{k}")[:], f,
                                                   bias=vec[:, V0[b] + k:V0[b] + k + 1]), f"{name}{k}")

            act.wait_ge(s_prep, 1)

            def relu(ms, c):
                for m in ms:
                    wait_filled(act, f"F{m}", c)
                    inc_drained(act.activation(fT[:, m], ps(f"F{m}")[:], ACT.Relu), f"F{m}")

            def decay(c):
                for k in range(KD):
                    wait_drained(act, f"R{k}", c)
                    if k == 0:
                        act.wait_ge(s_scan, (c + 1) * KD + KD)
                    act.activation(aT[:, k], rT[:, k], ACT.Exp, scale=ca[:, k:k + 1]).then_inc(s_a, 1)

            project(-1)
            decay(-1)
            with act.Fori(0, NCH) as c:
                for k in range(KD):
                    act.wait_ge(s_a2, c * KD + (k + 1))
                    act.activation(qT[:, k], qT[:, k], ACT.Sqrt, bias=1.0, scale=-1.0).then_inc(s_q, 1)
                relu(range(FMS - 2), c)
                for k in range(KD):
                    act.wait_ge(s_hs2, c * KD + (k + 1))
                    act.activation(sq[:, k], hs2[:, k], ACT.Square).then_inc(s_sq, 1)
                relu(range(FMS - 2, FMS), c)
                wait_filled(act, "MS", c)
                act.wait_ge(s_rinv, c + 1)
                inc_drained(act.activation(rms[:], ps("MS")[:], ACT.Sqrt, bias=eps0[:, 0:1]), "MS")
                relu(range(FMS, KH), c)
                for m in range(KM):
                    g = f"MG{m}"
                    wait_filled(act, g, c)
                    if m >= 2:
                        wait_drained(act, f"MF{m - 2}", c)
                    inc_drained(act.activation(mg[:, m % 2], ps(g)[:], ACT.Gelu,
                                               bias=vec[:, V0["mg_b"] + m:V0["mg_b"] + m + 1]), g)
                project(c)
                decay(c)
                act.wait_ge(xrT_out, c * 16 + 16)
                for k in range(KD):
                    wait_filled(act, f"Q{k}", c)
                    inc_drained(act.activation(xr1T[:, k], ps(f"Q{k}")[:], ACT.Copy), f"Q{k}")

        @block.vector
        def _(dve):
            dve.memset(eps0[:], EPS_RMS0).then_inc(s_prep, 1)
            dve.wait_ge(weights_in, weights_all)
            n = [1]

            def step(ins, then_wait=True):
                ins.then_inc(s_prep, 1)
                n[0] += 1
                if then_wait:
                    dve.wait_ge(s_prep, n[0])

            for k in range(KD):
                step(dve.tensor_scalar(w_p[:, k], w_p[:, k], vec[:, V0["norm_w"] + k:V0["norm_w"] + k + 1], None, ALU.mult))
                step(dve.tensor_scalar(w_m[:, k], w_m[:, k], vec[:, V0["norm2_w"] + k:V0["norm2_w"] + k + 1], None, ALU.mult))
            dve.wait_ge(s_prepa, 3)
            al = vec[:, V0["alpha"]:V0["alpha"] + KD]
            step(dve.tensor_scalar(sp[:, 0], al, 0.0, None, ALU.max))
            step(dve.tensor_tensor(sp[:, 1], sp[:, 0], sp[:, 2], ALU.add))
            step(dve.tensor_scalar(ca[:], sp[:, 1], -8.0, None, ALU.mult))
            dve.wait_ge(p_prep, 1)
            step(dve.tensor_scalar(low_z[:], bank[0][0:RANK, 0:D], low_g[:, 0:1], None, ALU.mult))

            def ternary(w, w2, mean, scale, hi, lo, ready):
                dve.wait_ge(p_prep, ready)
                step(dve.tensor_scalar(scale, mean, 1e-5, None, ALU.max))
                step(dve.tensor_scalar(hi, scale, 0.5, None, ALU.mult))
                for wk, over, under in w2:
                    step(dve.tensor_tensor(over, wk, hi, ALU.is_gt))
                    step(dve.scalar_tensor_tensor(out=under, in0=wk, scalar=-1.0, in1=hi, op0=ALU.mult, op1=ALU.is_gt))
                    step(dve.tensor_tensor(over, over, under, ALU.subtract))
                    step(dve.tensor_tensor(wk, over, scale, ALU.mult))

            for a in range(2):
                half = slice(a * T, (a + 1) * T)
                ternary(None, [(w_f[:, k, half], xnT[:, k], hT[:, k]) for k in range(KD)], bank[1 + a][:],
                        rms[:], rinv[:], None, 2)
            ternary(None, [(w_j[:, k], xn[:, 0], xn[:, 1]) for k in range(KH)], bank[3][:, 0:D], rms[:, 0:D],
                    rinv[:, 0:D], None, 3)
            dve.wait_ge(p_prep, 4)
            for k in range(KD):
                for a in range(2):
                    half = slice(a * T, (a + 1) * T)
                    step(dve.tensor_tensor(w_f[:, k, half], w_f[:, k, half], bank[4 + 2 * k + a][:], ALU.add))
            assert n[0] == PREP_STEPS, n[0]

            def normalise(src, mvt, st, sm, c, s_stat, s_pow, s_out, dst_n, dst_r):
                for s in range(SUB):
                    dve.bn_stats(st[:, s], src[:, s]).then_inc(s_stat, 1)
                dve.wait_ge(s_stat, c * 9 + (9 + 4))
                dve.tensor_copy(seen[:], st[:, :, 0]).then_inc(s_stat, 1)
                for s in range(SUB):
                    dve.bn_aggr(mvt[:, s], st[:, s]).then_inc(s_stat, 1)
                return

            def centre(src, mvt, sm, s_out, dst_n, dst_r):
                for s in range(SUB):
                    dve.tensor_scalar(dst_n[:, s], src[:, s], mvt[:, s, 0:1], sm[:, 1, s:s + 1],
                                      ALU.subtract, ALU.mult).then_inc(s_out, 1)
                    dve.tensor_scalar(dst_r[:, s], src[:, s], mvt[:, s, 0:1], sm[:, 5, s:s + 1],
                                      ALU.subtract, ALU.mult).then_inc(s_out, 1)

            def next_rows(c):
                dve.wait_ge(x_in, c * 16 + 32)
                normalise(xt, mv, stats, small, c, s_st, s_pw, s_ln, xn, hn)
                dve.wait_ge(s_st, c * 9 + 18)
                dve.wait_ge(s_pw, c * 7 + 14)
                centre(xt, mv, small, s_ln, xn, hn)

            def project(c):
                for k in range(KD):
                    wait_filled(dve, f"HT{k}", c)
                    inc_drained(dve.tensor_copy(hT[:, k], ps(f"HT{k}")[:]), f"HT{k}")
                for k in range(KD):
                    wait_filled(dve, f"H{k}", c)
                    wait_drained(dve, f"I{k}", c)
                    inc_drained(dve.scalar_tensor_tensor(
                        out=tT[:, k], in0=ps(f"H{k}")[:], scalar=vec[:, V0["hs_b"] + k:V0["hs_b"] + k + 1],
                        in1=iT[:, k], op0=ALU.add, op1=ALU.mult), f"H{k}")

            next_rows(-1)
            dve.sem_inc(s_scan, KD)
            dve.sem_inc(s_rinv, 1)
            dve.sem_inc(s_carry, 3)
            dve.sem_inc(xrT_out, 16)
            dve.sem_inc(x1p_out, 16)
            dve.sem_inc(xn1_out, 16)
            project(-1)
            dve.wait_ge(s_const, 9)
            with dve.Fori(0, NCH) as c:
                for k in range(KD):
                    dve.wait_ge(s_a, c * KD + (k + 1))
                    dve.tensor_tensor(qT[:, k], aT[:, k], aT[:, k], ALU.mult).then_inc(s_a2, 1)
                for k in range(KD):
                    dve.wait_ge(s_q, c * KD + (k + 1))
                    wait_drained(dve, f"H{k}", c - 1)
                    dve.tensor_tensor(tT[:, k], tT[:, k], qT[:, k], ALU.mult).then_inc(s_s, 1)
                for k in range(KD):
                    dve.wait_ge(s_s, c * KD + (k + 1))
                    dve.wait_ge(s_carry, c * 3 + 3)
                    dve.tensor_tensor_scan(oT[:, k], aT[:, k], tT[:, k], carry[:, k:k + 1],
                                           ALU.mult, ALU.add).then_inc(s_scan, 1)
                for k in range(KD):
                    dve.wait_ge(s_scan, c * KD + (KD + k + 1))
                    dve.tensor_scalar(carry[:, k:k + 1], oT[:, k, T - 1:T], keep[:, 0:1], None, ALU.mult).then_inc(s_carry, 1)
                dve.wait_ge(s_carry, c * 3 + 5)
                dve.tensor_scalar(keep[:], keep[:], -1.0, 1.0, ALU.mult, ALU.add).then_inc(s_carry, 1)
                for k in range(KD):
                    wait_drained(dve, f"GA{k}", c - 1)
                    dve.tensor_tensor(oT[:, k], oT[:, k], gT[:, k], ALU.mult).then_inc(s_og, 1)
                for k in range(KD):
                    dve.wait_ge(s_og, c * KD + (k + 1))
                    wait_drained(dve, f"XT{k}", c - 1)
                    dve.tensor_tensor(hs2[:, k], oT[:, k], xnT[:, k], ALU.add).then_inc(s_hs2, 1)
                wait_drained(dve, "MS", c)
                dve.reciprocal(rinv[:], rms[:]).then_inc(s_rinv, 1)
                dve.wait_ge(s_rinv, c + 2)
                for k in range(KD):
                    dve.tensor_tensor(h2[:, k], hs2[:, k], rinv[:], ALU.mult).then_inc(s_h2, 1)
                dve.wait_ge(x_in, c * 16 + 32)
                normalise(xt, mv, stats, small, c, s_st, s_pw, s_ln, xn, hn)
                dve.wait_ge(s_st, c * 9 + 18)
                dve.wait_ge(s_pw, c * 7 + 14)
                centre(xt, mv, small, s_ln, xn, hn)
                for m in range(KM):
                    wait_filled(dve, f"MF{m}", c)
                    wait_drained(dve, f"MG{m}", c)
                    inc_drained(dve.scalar_tensor_tensor(
                        out=mT[:, m], in0=ps(f"MF{m}")[:], scalar=vec[:, V0["mf_b"] + m:V0["mf_b"] + m + 1],
                        in1=mg[:, m % 2], op0=ALU.add, op1=ALU.mult), f"MF{m}")
                dve.wait_ge(xres_in, c * 16 + 16)
                for j in range(2):
                    wait_filled(dve, f"O{j}", c)
                    inc_drained(dve.tensor_tensor(x1[:, 2 * j:2 * j + 2], ps(f"O{j}")[:].rearrange("p (s d) -> p s d", s=2),
                                                  xres[:, 2 * j:2 * j + 2], ALU.add), f"O{j}")
                wait_drained(dve, "O0", c)
                wait_drained(dve, "O1", c)
                normalise(x1, mv1, stats1, small1, c - 1, s_st1, s_pw1, s_l1, xn1, xr1)
                project(c)
                dve.wait_ge(s_st1, c * 9 + 9)
                dve.wait_ge(s_pw1, c * 7 + 7)
                dve.wait_ge(xn1_out, c * 16 + 16)
                dve.wait_ge(x1p_out, c * 16 + 16)
                centre(x1, mv1, small1, s_l1, xn1, xr1)
                dve.wait_ge(s_l1, c * 12 + 8)
                for s in range(SUB):
                    dve.tensor_tensor(x1p[:, s], x1[:, s], xn1[:, s], ALU.add).then_inc(s_l1, 1)
                for k in range(KD):
                    wait_filled(dve, f"N{k}", c)
                    inc_drained(dve.tensor_copy(xn1T[:, k], ps(f"N{k}")[:]), f"N{k}")
                wait_filled(dve, "L", c)
                inc_drained(dve.tensor_tensor(lg[:, bass.ds(c * SUB, SUB), :], ps("L")[:, 0:SUB * 8].rearrange("p (s e) -> p s e", e=8),
                                              gb[:].rearrange("p (o e) -> p o e", o=1).to_broadcast([P, SUB, 8]),
                                              ALU.add), "L")

        @block.tensor
        def _(pe):
            mm = pe.matmul
            pe.wait_ge(weights_in, weights_all)
            pe.wait_ge(s_const, 9)
            pe.wait_ge(s_id, 2)
            mm(bank[0][0:RANK, 0:D], low_b[:], low_v[:], start=True, stop=True).then_inc(p_prep, 1)
            pe.wait_ge(s_prepa, 5)
            wabs = mT[:, 0:2 * KD].rearrange("p (k a) n -> p k a n", a=2)
            for a in range(2):
                for k in range(KD):
                    last = mm(bank[1 + a][:], inv_d[:], wabs[:, k, a], start=(k == 0), stop=(k == KD - 1))
            last.then_inc(p_prep, 1)
            wabs = fT[:, 0:KH // 2].rearrange("p k (a n) -> p (k a) n", a=2)
            for k in range(KH):
                last = mm(bank[3][:, 0:D], inv_h[:], wabs[:, k], start=(k == 0), stop=(k == KH - 1))
            last.then_inc(p_prep, 1)
            pe.wait_ge(s_prep, LOWZ_STEP)
            for k in range(KD):
                for a in range(2):
                    last = mm(bank[4 + 2 * k + a][:], low_z[:, k * P:(k + 1) * P], low_u[:, a * T:(a + 1) * T],
                              start=True, stop=True)
            last.then_inc(p_prep, 1)
            pe.wait_ge(s_prep, PREP_STEPS)
            first = order.index("XT0")
            after = order.index("N0")
            for b in range(BANKS):
                skipped = sum(1 for p in range(first) if p % BANKS == b)
                pe.sem_inc(drained[b], skipped)
                pe.sem_inc(filled[b], skipped)

            def product(g, w, cols, rhs, nk, c, ready=None):
                wait_bank(pe, g, c)
                for k in range(nk):
                    if ready is not None:
                        ready(k)
                    last = mm(ps(g)[:], w[:, k, cols], rhs[:, k], start=(k == 0), stop=(k == nk - 1))
                inc_filled(last, g)

            def turn(g, src, k, c):
                wait_bank(pe, g, c)
                for s in range(SUB):
                    last = pe.transpose(ps(g)[:, s * P:(s + 1) * P], src[:, s, k * P:(k + 1) * P], ident[:])
                inc_filled(last, g)

            def project(c):
                pe.wait_ge(s_ln, c * 8 + 16)
                for k in range(KD):
                    turn(f"XT{k}", xn, k, c)
                for k in range(KD):
                    turn(f"HT{k}", hn, k, c)
                for j, name in enumerate(("R", "I", "H", "GA")):
                    for m in range(KD):
                        product(f"{name}{m}", w_p, slice(j * D + m * P, j * D + (m + 1) * P), hT, KD, c,
                                ready=(lambda k: wait_drained(pe, f"HT{k}", c)) if j + m == 0 else None)

            project(-1)
            for p in range(after, len(order)):
                b = p % BANKS
                pe.wait_ge(drained[b], p // BANKS)
                pe.sem_inc(filled[b], 1)
                pe.sem_inc(drained[b], 1)
            with pe.Fori(0, NCH) as c:
                for m in range(KH):
                    if m == FMS:
                        wait_bank(pe, "MS", c)
                        for k in range(KD):
                            pe.wait_ge(s_sq, c * KD + (k + 1))
                            last = mm(ps("MS")[:], inv_d[:], sq[:, k], start=(k == 0), stop=(k == KD - 1))
                        inc_filled(last, "MS")
                    product(f"F{m}", w_f, slice(m * P, (m + 1) * P), xnT, KD, c,
                            ready=(lambda k: wait_drained(pe, f"XT{k}", c - 1)) if m == 0 else None)
                for m in range(KM):
                    for j, name in enumerate(("MG", "MF")):
                        product(f"{name}{m}", w_m, slice(j * MLP + m * P, j * MLP + (m + 1) * P), h2, KD, c,
                                ready=(lambda k: pe.wait_ge(s_h2, c * KD + (k + 1))) if m + j == 0 else None)
                pe.wait_ge(s_hs2, c * KD + KD)
                for j in range(2):
                    wait_bank(pe, f"O{j}", c)
                    for s in (2 * j, 2 * j + 1):
                        cols = slice(s * P, (s + 1) * P)
                        out = ps(f"O{j}")[:, (s % 2) * D:(s % 2 + 1) * D]
                        mm(out, ones[0:1, :], brow[:], start=(s % 2 == 0), stop=False, skip_group_check=True)
                        for k in range(KD):
                            mm(out[:, k * P:(k + 1) * P], hs2[:, k, cols], ident[:], start=False, stop=False,
                               skip_group_check=True)
                        for m in range(KH):
                            if s == 0:
                                pe.wait_ge(s_fsq, c * KH + (m + 1))
                            mm(out, fT[:, m, cols], w_j[:, m], start=False, stop=False, skip_group_check=True)
                        for m in range(KM):
                            if s == 0:
                                wait_drained(pe, f"MF{m}", c)
                            last = mm(out, mT[:, m, cols], w_o[:, m], start=False, stop=(s % 2 == 1 and m == KM - 1),
                                      skip_group_check=True)
                    inc_filled(last, f"O{j}")
                project(c)
                pe.wait_ge(s_l1, c * 12 + 8)
                for k in range(KD):
                    turn(f"N{k}", xn1, k, c)
                for k in range(KD):
                    turn(f"Q{k}", xr1, k, c)
                wait_bank(pe, "L", c)
                for s in range(SUB):
                    for k in range(KD):
                        if s == 0:
                            wait_drained(pe, f"N{k}", c)
                        last = mm(ps("L")[:, s * 8:(s + 1) * 8], xn1T[:, k, s * P:(s + 1) * P], gw[:, k],
                                  start=(k == 0), stop=(k == KD - 1))
                inc_filled(last, "L")


LOWZ_STEP = 1 + 2 * KD + 3 + 1
PREP_STEPS = LOWZ_STEP + 2 * (2 + 4 * KD) + 2 + 4 * KH + 2 * KD


E_IN = 512
KE = E_IN // P
NST = 16
DR = 64
TAPS = 4
PAD = TAPS - 1
NSEQ = NTOK // SEQ
V1 = {}
_at = 0
for _name, _n in (("norm_w", KD), ("conv_w", KE * TAPS), ("conv_b", KE), ("dt_b", KE), ("A_log", KE * NST),
                  ("W_D", KE)):
    V1[_name] = _at
    _at += _n
NV1 = _at


def mamba(nc, dram):
    RING = 4
    NA = 4
    SCAN0 = NA * KE
    ahead = {n: [] for n in range(NST)}
    for e in range(KE):
        ahead[2 + e].append(f"IN{e}")
        ahead[3 + e].append(f"SK{e}")
        ahead[10 + e // 2].append(f"DT{e}")
    ahead[8] = ["BC"]
    ahead[9] = ["DR"]

    def spread_at(n):
        return [(f"B{(n + 2) % NST}", n + 2 >= NST), (f"C{(n + 1) % NST}", n + 1 >= NST)]

    def listing(last):
        order = []
        for n in range(NST):
            order += [g for g, of_next in spread_at(n) if not (last and of_next)]
            if n < 2:
                order += [f"O{n}"]
            if not last:
                order += ahead[n]
        return order + (["Z0", "Z1"] if last else [])

    first = [g for n in range(NST) for g in ahead[n]] + ["B0", "C15", "B1", "C0"]
    place = {"first": {g: p for p, g in enumerate(first)}, "body": {g: p for p, g in enumerate(listing(False))},
             "last": {g: p for p, g in enumerate(listing(True))}}
    lead, per = len(first), len(listing(False))
    assert per % RING == 0 and all(lead + place["body"][g] - per == place["first"][g] for g in ("B0", "C15", "B1", "C0"))

    with ExitStack() as ctx:
        def sb(name, shape, dt=F32):
            return ctx.enter_context(nc.sbuf_tensor("m_" + name, shape, dt))

        def sem(name):
            return ctx.enter_context(nc.semaphore("m_" + name))

        ybank = [ctx.enter_context(nc.psum_tensor(f"m_y{e}", [P, T], F32)) for e in range(KE)]
        ring = [ctx.enter_context(nc.psum_tensor(f"m_ring{i}", [P, T], F32)) for i in range(RING)]
        w_si = sb("w_si", [P, KD, 2 * E_IN])
        w_x = sb("w_x", [P, KE, DR + 2 * NST])
        w_dt = sb("w_dt", [DR, E_IN])
        w_out = sb("w_out", [P, KE, D])
        vec = sb("vec", [P, NV1])
        A = sb("A", [P, KE * NST])
        ident = sb("ident", [P, P])
        sel = sb("sel", [3 * 2 * NST, 2 * NST], BF16)
        xr = sb("xr", [P, KD, T])
        xpad = [sb(f"xpad{h}", [P, KE, PAD + T]) for h in range(2)]
        cv = sb("cv", [P, KE, T])
        xs = [sb(f"xs{h}", [P, KE, T]) for h in range(2)]
        sk = [sb(f"sk{h}", [P, KE, T]) for h in range(2)]
        dl = [sb(f"dl{h}", [P, KE, T]) for h in range(2)]
        ux = [sb(f"ux{h}", [P, KE, T]) for h in range(2)]
        bc3 = [sb(f"bc3{h}", [3 * 2 * NST, T], BF16) for h in range(2)]
        bc2 = sb("bc2", [2 * NST, T], BF16)
        dr = sb("dr", [DR, T])
        z = sb("z", [P, KE, T])
        ez = sb("ez", [P, KE, T])
        bcr = ez[0:2 * NST, 0]
        dA = sb("dA", [P, NA, KE, T])
        bb = sb("bb", [P, 2, T])
        bx_hc = sb("bx_hc", [P, 4, KE, T])
        bx, hc = bx_hc[:, 0:2], bx_hc[:, 2:4]
        hh = sb("hh", [P, 1, KE, T])
        rows = bx_hc[:].rearrange("p a e t -> p (a e t)").rearrange("p (j d) -> p j d", d=D)
        dst = sb("dst", [P, NPICK], I32)
        carry = sb("carry", [P, NST, KE])
        y1 = ez
        mo = z[:, 0:SUB * D // T].rearrange("p e t -> p (e t)").rearrange("p (s d) -> p s d", d=D)

        filled = [sem(f"filled{i}") for i in range(RING)]
        drained = [sem(f"drained{i}") for i in range(RING)]
        w_in, xr_in, mo_out = sem("w_in"), sem("xr_in"), sem("mo_out")
        rows_in, picks_out = [sem(f"rows_in{c}") for c in range(NCH)], sem("picks_out")
        s_id, s_sel, s_pad, s_prep, s_A = sem("s_id"), sem("s_sel"), sem("s_pad"), sem("s_prep"), sem("s_A")
        s_conv, s_xs, s_sk, s_bca, s_bcd = sem("s_conv"), sem("s_xs"), sem("s_sk"), sem("s_bca"), sem("s_bcd")
        s_abs, s_ez, s_w, s_ln, s_dl, s_ux = (sem("s_abs"), sem("s_ez"), sem("s_w"), sem("s_ln"), sem("s_dl"),
                                              sem("s_ux"))
        s_exp, s_bx, s_scan, s_carry, s_y = sem("s_exp"), sem("s_bx"), sem("s_scan"), sem("s_carry"), sem("s_y")
        s_yf, s_y2, s_zero = sem("s_yf"), sem("s_y2"), sem("s_zero")
        block = ctx.enter_context(nc.Block())

        def spot(g, at):
            kind, i, h = at
            p = place[kind][g]
            if kind == "first":
                return p % RING, p // RING
            return (lead + p) % RING, i * (per // RING) + (lead + p) // RING

        def bank_of(g, at):
            return (place[at[0]][g] + (0 if at[0] == "first" else lead)) % RING

        def wait_filled(eng, g, at):
            b, k = spot(g, at)
            eng.wait_ge(filled[b], k + 1)

        def wait_drained(eng, g, at):
            b, k = spot(g, at)
            eng.wait_ge(drained[b], k + 1)

        def wait_bank(pe, g, at):
            b, k = spot(g, at)
            if not (isinstance(k, int) and k == 0):
                pe.wait_ge(drained[b], k)

        def inc(ins, sems, g, at):
            ins.then_inc(sems[bank_of(g, at)], 1)

        def tile_of(g, at):
            return ring[bank_of(g, at)]

        START = ("first", -1, 1)

        def before(at):
            return ("body", at[1] - 1, 1 - at[2])

        def at_of(at, g):
            return before(at) if g in ("B0", "B1", "C0") else at

        def program(eng, ahead_of, step, end):
            ahead_of(START, 0, 0, range(NST))

            def chunk(i, h, last):
                at = ("last" if last else "body", i, h)
                for n in range(NST):
                    step(at, i, h, n, last)
                    if n < 2:
                        end(at, i, 1 - h, f"O{n}")
                    if not last:
                        ahead_of(at, i + 1, 1 - h, [n])

            with eng.Fori(0, NSEQ - 1) as b:
                chunk(b * 2, 0, False)
                chunk(b * 2 + 1, 1, False)
            chunk(2 * NSEQ - 2, 0, False)
            chunk(2 * NSEQ - 1, 1, True)
            for g in ("Z0", "Z1"):
                end(("last", 2 * NSEQ - 1, 1), 2 * NSEQ, 1, g)

        w_loads = [(w_si, dram["w_si"]), (w_x, dram["w_x"]), (w_dt, dram["w_dt"]), (w_out, dram["w_out"]),
                   (vec, dram["vec1"])]

        @block.sync
        def _(sp):
            sp.dma_start(xr[:], dram["xrT"][0:P]).then_inc(xr_in, 16)
            for tile, src in w_loads:
                sp.dma_start(tile[:], src).then_inc(w_in, 16)
            sp.dma_start(dst[:], dram["dst"]).then_inc(rows_in[0], 16)
            for c in range(NCH):
                sp.dma_start(rows[:, c * SUB:(c + 1) * SUB],
                             dram["xn1"][c * T:(c + 1) * T, :].rearrange("(s p) d -> p s d", p=P)).then_inc(rows_in[c], 16)

            def ahead_of(at, q, h, slots):
                if 6 in slots:
                    if not (isinstance(q, int) and q == 2 * NSEQ - 1):
                        wait_filled(sp, "SK3", at)
                        sp.dma_start(xr[:], dram["xrT"][bass.ds((q + 1) * P, P), :, :]).then_inc(xr_in, 16)

            def end(at, i, h, g):
                if g[1] == "0":
                    return
                wait_drained(sp, g[0] + "0", at)
                wait_drained(sp, g, at)
                sp.dma_start(dram["mo"][bass.ds(i * T, T), :].rearrange("(s p) d -> p s d", p=P), mo).then_inc(mo_out, 16)

            program(sp, ahead_of, lambda *_: None, end)
            sp.wait_ge(mo_out, 16 * (NCH + 1) + 16)

        @block.gpsimd
        def _(pool):
            identity(pool, ident, s_id)
            pool.memset(sel[:], 0.0).then_inc(s_sel, 1)
            pool.memset(xpad[0][:, :, 0:PAD], 0.0).then_inc(s_pad, 1)
            for j in range(3):
                pool.wait_ge(s_sel, j + 1)
                pool.affine_select(out=sel[:], in_=sel[:], compare_op=ALU.not_equal, fill=1.0, base=-2 * NST * j,
                                   pattern=[[-1, 2 * NST]], channel_multiplier=1).then_inc(s_sel, 1)
            pool.sem_inc(s_bx, 2)
            pool.memset(xs[1][:], 0.0).then_inc(s_zero, 1)
            pool.memset(sk[1][:], 0.0).then_inc(s_zero, 1)

            for c in range(NCH):
                pool.wait_ge(rows_in[c], 32 if c == 0 else 16)
                for j in range(c * SUB, (c + 1) * SUB):
                    for k in range(TOPK):
                        a = k * NJ + j
                        pool.indirect_dma_start(dram["xg"][:, :], bass.IndirectOffsetOnAxis(ap=dst[:, a:a + 1], axis=0),
                                                rows[:, j, :], None).then_inc(picks_out, 16)
            pool.wait_ge(picks_out, 16 * NPICK)

            def step(at, i, h, n, last):
                wait_drained(pool, f"B{n}", at_of(at, f"B{n}"))
                if n == 0:
                    pool.wait_ge(s_ux, i * 1 + 1)
                pool.wait_ge(s_scan, i * (NST * KE) + (SCAN0 + KE * (n - 1)))
                pool.tensor_tensor(bx[:, n % 2], ux[h][:], bb[:, n % 2:n % 2 + 1, :].to_broadcast([P, KE, T]),
                                   ALU.mult).then_inc(s_bx, 1)

            program(pool, lambda *_: None, step, lambda *_: None)

        @block.scalar
        def _(act):
            act.wait_ge(w_in, 16 * len(w_loads))
            act.activation(A[:], vec[:, V1["A_log"]:V1["A_log"] + KE * NST], ACT.Exp).then_inc(s_prep, 1)
            act.sem_inc(mo_out, 16)
            act.sem_inc(s_sk, 1)

            def b_row(i, n, at):
                wait_filled(act, f"B{n}", at)
                act.wait_ge(s_bx, i * NST + (n + 1))
                inc(act.activation(bb[:, n % 2], tile_of(f"B{n}", at)[:], ACT.Copy), drained, f"B{n}", at)

            def decays(i, h, n):
                if n == 0:
                    act.wait_ge(s_dl, i * 3 + 3)
                    act.wait_ge(s_A, 1)
                act.wait_ge(s_scan, i * (NST * KE) + (SCAN0 + KE * (n + 1 - NA)))
                for e in range(KE):
                    act.activation(dA[:, n % NA, e], dl[h][:, e], ACT.Exp,
                                   scale=A[:, e * NST + n:e * NST + n + 1]).then_inc(s_exp, 1)

            def ahead_of(at, q, h, slots):
                for n in slots:
                    for g in ahead[n]:
                        if g in ("BC", "DR"):
                            continue
                        e = int(g[2:])
                        wait_filled(act, g, at)
                        if g[:2] == "IN":
                            ins = act.activation(xpad[h][:, e, PAD:PAD + T], tile_of(g, at)[:], ACT.Copy)
                        elif g[:2] == "SK":
                            if e == 0 and at[0] != "first":
                                act.wait_ge(s_y2, q)
                            ins = act.activation(sk[h][:, e], tile_of(g, at)[:], ACT.Copy)
                        else:
                            if e == 0:
                                act.wait_ge(mo_out, q * 16 + 16)
                            ins = act.activation(z[:, e], tile_of(g, at)[:], ACT.Identity,
                                                 bias=vec[:, V1["dt_b"] + e:V1["dt_b"] + e + 1])
                        inc(ins, drained, g, at)
                    if n == 7:
                        wait_drained(act, "SK3", at)
                        act.wait_ge(s_conv, q * (KE * TAPS) + (KE * TAPS))
                        act.activation(xs[h][:], cv[:], ACT.Silu).then_inc(s_xs, 1)
                        act.activation(sk[h][:], sk[h][:], ACT.Silu).then_inc(s_sk, 1)
                    if n == 8:
                        wait_filled(act, "BC", at)
                        act.activation(bc3[h][0:2 * NST, :], tile_of("BC", at)[0:2 * NST, :], ACT.Copy).then_inc(s_bca, 1)
                    if n == 9:
                        wait_filled(act, "DR", at)
                        inc(act.activation(dr[:], tile_of("DR", at)[0:DR, :], ACT.Copy), drained, "DR", at)
                    if n == 10:
                        act.wait_ge(s_bcd, q * 3 + 3)
                        act.activation(bc3[h][2 * NST:4 * NST, :], bc2[:], ACT.Copy).then_inc(s_bca, 1)
                    if n == 11:
                        wait_drained(act, f"DT{KE - 1}", at)
                        act.activation(ez[:], z[:], ACT.Abs).then_inc(s_abs, 1)
                        act.wait_ge(s_abs, q + 1)
                        act.activation(ez[:], ez[:], ACT.Exp, scale=-1.0).then_inc(s_ez, 1)
                    if n == 12:
                        act.wait_ge(s_dl, q * 3 + 1)
                        act.activation(cv[:], cv[:], ACT.Ln).then_inc(s_ln, 1)

            def step(at, i, h, n, last):
                if n < NST - 2:
                    decays(i, h, n + 2)
                elif not last:
                    decays(i + 1, 1 - h, n + 2 - NST)
                for g, of_next in spread_at(n):
                    if g[0] == "B" and not (last and of_next):
                        b_row(i + 1 if of_next else i, int(g[1:]), at)

            def end(at, i, h, g):
                j = int(g[1])
                if j == 0:
                    act.wait_ge(mo_out, i * 16 + 16)
                    act.wait_ge(s_dl, i * 3 + (0 if g == "Z0" else 3))
                wait_filled(act, g, at)
                inc(act.activation(mo[:, 2 * j:2 * j + 2], tile_of(g, at)[:].rearrange("p (s d) -> p s d", s=2),
                                   ACT.Copy), drained, g, at)

            ahead0 = ahead_of

            def ahead_first(at, q, h, slots):
                ahead0(at, q, h, slots)
                if at[0] == "first":
                    b_row(0, 0, START)
                    b_row(0, 1, START)
                    decays(0, 0, 0)
                    decays(0, 0, 1)

            program(act, ahead_first, step, end)

        @block.vector
        def _(dve):
            dve.wait_ge(s_prep, 1)
            dve.tensor_scalar(A[:], A[:], -1.0, None, ALU.mult).then_inc(s_A, 1)
            for k in range(KD):
                dve.tensor_scalar(w_si[:, k], w_si[:, k], vec[:, V1["norm_w"] + k:V1["norm_w"] + k + 1], None,
                                  ALU.mult).then_inc(s_prep, 1)
            dve.sem_inc(s_scan, SCAN0)
            for e in range(KE):
                dve.memset(ybank[e][:], 0.0).then_inc(s_zero, 1)
            dve.wait_ge(s_zero, 2 + KE)
            dve.wait_ge(s_pad, 1)

            def ahead_of(at, q, h, slots):
                for n in slots:
                    if 3 <= n < KE + 3:
                        e = n - 3
                        w = [vec[:, V1["conv_w"] + e * TAPS + k:V1["conv_w"] + e * TAPS + k + 1] for k in range(TAPS)]
                        base = q * (KE * TAPS) + e * TAPS
                        if h == 1:
                            dve.tensor_copy(xpad[1][:, e, 0:PAD], xpad[0][:, e, T:T + PAD]).then_inc(s_pad, 1)
                            dve.wait_ge(s_pad, (q - 1) * 2 + (e + 2))
                        wait_drained(dve, f"IN{e}", at)
                        dve.tensor_scalar(cv[:, e], xpad[h][:, e, 0:T], w[0], vec[:, V1["conv_b"] + e:V1["conv_b"] + e + 1],
                                          ALU.mult, ALU.add).then_inc(s_conv, 1)
                        for k in range(1, TAPS):
                            dve.wait_ge(s_conv, base + k)
                            dve.scalar_tensor_tensor(out=cv[:, e], in0=xpad[h][:, e, k:k + T], scalar=w[k], in1=cv[:, e],
                                                     op0=ALU.mult, op1=ALU.add).then_inc(s_conv, 1)
                    if n == 9:
                        dve.wait_ge(s_bca, q * 2 + 1)
                        inc(dve.tensor_tensor(bcr, tile_of("BC", at)[0:2 * NST, :], bc3[h][0:2 * NST, :], ALU.subtract),
                            drained, "BC", at)
                        dve.sem_inc(s_bcd, 1)
                        wait_drained(dve, "BC", at)
                        dve.tensor_copy(bc2[:], bcr).then_inc(s_bcd, 1)
                        dve.wait_ge(s_bcd, q * 3 + 2)
                        dve.tensor_tensor(bc3[h][4 * NST:6 * NST, :], bcr, bc2[:], ALU.subtract).then_inc(s_bcd, 1)
                    if n == 12:
                        dve.wait_ge(s_ez, q + 1)
                        dve.tensor_scalar(cv[:], ez[:], 1.0, None, ALU.add).then_inc(s_w, 1)
                        dve.wait_ge(s_w, q + 1)
                        dve.scalar_tensor_tensor(out=ez[:], in0=cv[:], scalar=-1.0, in1=ez[:], op0=ALU.add,
                                                 op1=ALU.subtract).then_inc(s_dl, 1)
                    if n == 13:
                        dve.wait_ge(s_ln, q + 1)
                        dve.tensor_tensor(ez[:], cv[:], ez[:], ALU.subtract).then_inc(s_dl, 1)
                        dve.wait_ge(s_dl, q * 3 + 2)
                        dve.scalar_tensor_tensor(out=dl[h][:], in0=z[:], scalar=0.0, in1=ez[:], op0=ALU.max,
                                                 op1=ALU.add).then_inc(s_dl, 1)
                    if n == 14:
                        dve.wait_ge(s_dl, q * 3 + 3)
                        dve.wait_ge(s_xs, q + 1)
                        dve.tensor_tensor(ux[h][:], dl[h][:], xs[h][:], ALU.mult).then_inc(s_ux, 1)

            def finish(i, h):
                dve.wait_ge(s_y, i * NST + 2)
                for e in range(KE):
                    dve.scalar_tensor_tensor(out=y1[:, e], in0=xs[h][:, e], scalar=vec[:, V1["W_D"] + e:V1["W_D"] + e + 1],
                                             in1=ybank[e][:], op0=ALU.mult, op1=ALU.add).then_inc(s_yf, 1)
                dve.wait_ge(s_yf, i * KE + KE)
                dve.wait_ge(s_sk, i + 1)
                dve.tensor_tensor(y1[:], y1[:], sk[h][:], ALU.mult).then_inc(s_y2, 1)

            def step(at, i, h, n, last):
                here = at_of(at, f"C{n}")
                if n == 0:
                    wait_drained(dve, f"C{NST - 1}", before(at))
                else:
                    wait_drained(dve, f"C{n - 1}", at_of(at, f"C{n - 1}"))
                if h == 0 and n > 0:
                    dve.wait_ge(s_carry, i * (NST // 2) + n)
                dve.wait_ge(s_bx, i * NST + (2 + n + 1))
                for e in range(KE):
                    dve.wait_ge(s_exp, i * (NST * KE) + (KE * n + e + 1))
                    if h == 1 and n == 0 and e == 0:
                        dve.wait_ge(s_carry, (i - 1) * (NST // 2) + NST)
                    dve.tensor_tensor_scan(hh[:, 0, e], dA[:, n % NA, e], bx[:, n % 2, e],
                                           0.0 if h == 0 else carry[:, n, e:e + 1], ALU.mult, ALU.add).then_inc(s_scan, 1)
                if n == 0:
                    finish(i, 1 - h)
                wait_filled(dve, f"C{n}", here)
                dve.wait_ge(s_scan, i * (NST * KE) + (SCAN0 + KE * (n + 1)))
                dve.wait_ge(s_y, i * NST + (n + 1))
                inc(dve.tensor_tensor(hc[:, n % 2], hh[:, 0],
                                      tile_of(f"C{n}", here)[:].rearrange("p (o t) -> p o t", o=1).to_broadcast([P, KE, T]),
                                      ALU.mult), drained, f"C{n}", here)
                if h == 0:
                    dve.tensor_copy(carry[:, n, :], hh[:, 0, :, T - 1]).then_inc(s_carry, 1)

            def end(at, i, h, g):
                if g == "Z0":
                    finish(i, h)

            program(dve, ahead_of, step, end)

        @block.tensor
        def _(pe):
            mm = pe.matmul
            pe.wait_ge(w_in, 16 * len(w_loads))
            pe.wait_ge(s_prep, 1 + KD)
            pe.wait_ge(s_id, 2)
            pe.wait_ge(s_sel, 4)
            pe.sem_inc(s_y, 2)

            def spread(g, q, h, at):
                n = int(g[1:]) + (NST if g[0] == "C" else 0)
                wait_bank(pe, g, at)
                if g == "B0":
                    pe.wait_ge(s_bca, q * 2 + 2)
                    pe.wait_ge(s_bcd, q * 3 + 3)
                inc(mm(tile_of(g, at)[:], sel[:, n:n + 1].to_broadcast([3 * 2 * NST, P]), bc3[h][:], start=True, stop=True), filled, g, at)

            def pieces(at, q, h, slots):
                for n in slots:
                    for g in ahead[n]:
                        wait_bank(pe, g, at)
                        out = tile_of(g, at)
                        if g[:2] in ("IN", "SK"):
                            e = int(g[2:])
                            if g == "IN0":
                                pe.wait_ge(xr_in, q * 16 + 16)
                            col = (E_IN if g[:2] == "IN" else 0) + e * P
                            for k in range(KD):
                                last = mm(out[:], w_si[:, k, col:col + P], xr[:, k], start=(k == 0), stop=(k == KD - 1))
                        elif g in ("BC", "DR"):
                            pe.wait_ge(s_xs, q + 1)
                            cols = slice(0, 2 * NST) if g == "BC" else slice(2 * NST, 2 * NST + DR)
                            for e in range(KE):
                                last = mm(out[0:cols.stop - cols.start, :], w_x[:, e, cols], xs[h][:, e],
                                          start=(e == 0), stop=(e == KE - 1))
                        else:
                            e = int(g[2:])
                            wait_drained(pe, "DR", at)
                            last = mm(out[:], w_dt[:, e * P:(e + 1) * P], dr[:], start=True, stop=True)
                        inc(last, filled, g, at)
            def ahead_of(at, q, h, slots):
                if at[0] == "first":
                    pieces(at, q, h, slots)
                    for g in first[-4:]:
                        if g in ("B0", "B1", "C0"):
                            spread(g, q, h, at)
                            continue
                        wait_bank(pe, g, at)
                        pe.sem_inc(filled[bank_of(g, at)], 1)
                        pe.sem_inc(drained[bank_of(g, at)], 1)

            def step(at, i, h, n, last):
                for g, of_next in spread_at(n):
                    if not of_next:
                        spread(g, i, h, at)
                    elif not last:
                        spread(g, i + 1, 1 - h, at)
                if n < 2:
                    out_rows(at, i, f"O{n}")
                if not last:
                    pieces(at, i + 1, 1 - h, [n])
                here = at_of(at, f"C{n}")
                wait_drained(pe, f"C{n}", here)
                if n == 0:
                    pe.wait_ge(s_yf, i * KE + KE)
                for e in range(KE):
                    last_mm = mm(ybank[e][:], ident[:], hc[:, n % 2, e], start=(n == 0), stop=(n == NST - 1))
                last_mm.then_inc(s_y, 1)

            def out_rows(at, i, g):
                j = int(g[1])
                if j == 0:
                    pe.wait_ge(s_y2, i + 1)
                wait_bank(pe, g, at)
                for s in (2 * j, 2 * j + 1):
                    for e in range(KE):
                        last = mm(tile_of(g, at)[:, (s % 2) * D:(s % 2 + 1) * D], y1[:, e, s * P:(s + 1) * P],
                                  w_out[:, e], start=(e == 0 and s % 2 == 0), stop=(e == KE - 1 and s % 2 == 1),
                                  skip_group_check=True)
                inc(last, filled, g, at)

            def end(at, i, h, g):
                if g[0] == "Z":
                    out_rows(at, i, g)

            program(pe, ahead_of, step, end)



def routing(nc, dram):
    with ExitStack() as ctx:
        def sb(name, shape, dt=F32):
            return ctx.enter_context(nc.sbuf_tensor("r_" + name, shape, dt))

        def sem(name):
            return ctx.enter_context(nc.semaphore("r_" + name))

        ps_before = ctx.enter_context(nc.psum_tensor("r_ps_before", [P, NPICK * NE], F32))
        ps_total = ctx.enter_context(nc.psum_tensor("r_ps_total", [P, NPICK * NE], F32))
        lg = sb("lg", [P, NJ, NE])
        m8 = sb("m8", [P, NJ, 8])
        i8 = sb("i8", [P, NJ, 8], U32)
        pick = sb("pick", [P, TOPK, NJ])
        oh = sb("oh", [P, NPICK, NE])
        wts = sb("wts", [P, TOPK, NJ])
        ex = sb("ex", [P, 3, NJ])
        upper = sb("upper", [P, P])
        ones = sb("ones", [P, P])
        io_e = sb("io_e", [P, NE])
        io_m = sb("io_m", [P, TMAX])
        io_t = sb("io_t", [1, NT])
        tot = sb("tot", [P, NE, NPICK])
        incl = sb("incl", [P, NE, NPICK])
        cmp = sb("cmp", [P, NE, TMAX])
        nt = sb("nt", [P, NE])
        tend = sb("tend", [P, NE])
        base = sb("base", [P, NE])
        onesrow = ones[:, 0:NPICK]
        before = sb("before", [P, NPICK, NE])
        dstf = sb("dstf", [P, NPICK])
        dst = sb("dst", [P, NPICK], I32)
        cmpt = sb("cmpt", [1, NT, NE])
        texf = sb("texf", [1, NT])
        tex = sb("tex", [1, NT], I32)
        lg_in, s_c, s_d, s_ex, s_mm, s_out = sem("lg_in"), sem("c"), sem("d"), sem("ex"), sem("mm"), sem("out")
        block = ctx.enter_context(nc.Block())

        @block.gpsimd
        def _(pool):
            pool.memset(ones[:], 1.0).then_inc(s_c, 1)
            pool.wait_ge(s_c, 1)
            pool.affine_select(out=upper[:], in_=ones[:], compare_op=ALU.is_gt, fill=0.0, base=0, pattern=[[1, P]],
                               channel_multiplier=-1).then_inc(s_c, 1)
            pool.iota(io_e[:], pattern=[[1, NE]], base=0, channel_multiplier=0,
                      allow_small_or_imprecise_dtypes=True).then_inc(s_c, 1)
            pool.iota(io_m[:], pattern=[[S, TMAX]], base=0, channel_multiplier=0,
                      allow_small_or_imprecise_dtypes=True).then_inc(s_c, 1)
            pool.iota(io_t[:], pattern=[[1, NT]], base=0, channel_multiplier=0,
                      allow_small_or_imprecise_dtypes=True).then_inc(s_c, 1)

        @block.sync
        def _(sp):
            sp.dma_start(lg[:], dram["logits"]).then_inc(lg_in, 16)
            sp.wait_ge(s_d, D_STEPS)
            sp.dma_start(dram["dst"], dst[:]).then_inc(s_out, 16)
            sp.dma_start(dram["tex"], tex[:]).then_inc(s_out, 16)
            sp.dma_start(dram["wts"], wts[:].rearrange("p k j -> p (k j)")).then_inc(s_out, 16)
            sp.wait_ge(s_out, 48)

        @block.scalar
        def _(act):
            act.wait_ge(s_d, 2 * NJ + 1)
            act.activation(ex[:, 1], ex[:, 0], ACT.Exp).then_inc(s_ex, 1)

        @block.tensor
        def _(pe):
            pe.wait_ge(s_c, 5)
            pe.wait_ge(s_d, 2 * NJ + 1 + 1 + 1)
            r = oh[:].rearrange("p a e -> p (a e)")
            pe.matmul(ps_before[:], upper[:], r, start=True, stop=True).then_inc(s_mm, 1)
            pe.matmul(ps_total[:], ones[:], r, start=True, stop=True).then_inc(s_mm, 1)

        @block.vector
        def _(dve):
            n = [0]

            def step(ins, wait=True):
                ins.then_inc(s_d, 1)
                n[0] += 1
                if wait:
                    dve.wait_ge(s_d, n[0])

            def over(row, k):
                return row.rearrange("p (o n) -> p o n", o=1).to_broadcast([row.shape[0], k, row.shape[1]])

            dve.wait_ge(lg_in, 16)
            for j in range(NJ):
                step(dve.max(m8[:, j], lg[:, j]), False)
            dve.wait_ge(s_d, NJ)
            for j in range(NJ):
                step(dve.max_index(i8[:, j], m8[:, j], lg[:, j]), False)
            step(dve.tensor_tensor(ex[:, 0], m8[:, :, 1], m8[:, :, 0], ALU.subtract))
            step(dve.tensor_copy(pick[:], i8[:, :, 0:TOPK].rearrange("p j k -> p k j")))
            dve.wait_ge(s_c, 5)
            picks = pick[:].rearrange("p k (j o) -> p (k j) o", o=1).to_broadcast([P, NPICK, NE])
            step(dve.tensor_tensor(oh[:], picks, over(io_e[:], NPICK), ALU.is_equal))
            dve.wait_ge(s_ex, 1)
            step(dve.tensor_scalar(ex[:, 2], ex[:, 1], 1.0, None, ALU.add))
            step(dve.reciprocal(wts[:, 0], ex[:, 2]))
            step(dve.tensor_tensor(wts[:, 1], ex[:, 1], wts[:, 0], ALU.mult))
            dve.wait_ge(s_mm, 2)
            step(dve.tensor_copy(tot[:], ps_total[:].rearrange("p (a e) -> p e a", e=NE)))
            for e in range(NE):
                step(dve.tensor_tensor_scan(incl[:, e], onesrow, tot[:, e], 0.0, ALU.mult, ALU.add), False)
            dve.wait_ge(s_d, n[0])
            step(dve.tensor_tensor(cmp[:], over(io_m[:], NE), incl[:, :, NPICK - 1:NPICK].to_broadcast([P, NE, TMAX]), ALU.is_lt))
            step(dve.tensor_reduce(nt[:], cmp[:], AX_X, ALU.add))
            step(dve.tensor_tensor_scan(tend[:], ones[:, 0:NE], nt[:], 0.0, ALU.mult, ALU.add))
            step(dve.tensor_tensor(base[:], tend[:], nt[:], ALU.subtract))
            step(dve.tensor_scalar(base[:], base[:], float(S), None, ALU.mult))
            step(dve.tensor_tensor(incl[:], incl[:], tot[:], ALU.subtract))
            step(dve.tensor_tensor(before[:], ps_before[:].rearrange("p (a e) -> p a e", e=NE),
                                   incl[:].rearrange("p e a -> p a e"), ALU.add))
            step(dve.tensor_tensor(before[:], before[:], over(base[:], NPICK), ALU.add))
            step(dve.tensor_tensor(before[:], before[:], oh[:], ALU.mult))
            step(dve.tensor_reduce(dstf[:], before[:], AX_X, ALU.add))
            step(dve.tensor_copy(dst[:], dstf[:]))
            step(dve.tensor_tensor(cmpt[:], io_t[:].rearrange("p (t o) -> p t o", o=1).to_broadcast([1, NT, NE]),
                                   over(tend[0:1, :], NT), ALU.is_ge))
            step(dve.tensor_reduce(texf[:], cmpt[:], AX_X, ALU.add))
            step(dve.tensor_scalar(texf[:], texf[:], float(NE - 1), None, ALU.min))
            step(dve.tensor_copy(tex[:], texf[:]))
            assert n[0] == D_STEPS, n[0]


SPLITS = 2 * KF
D_STEPS = 2 * NJ + 3 + 3 + 1 + NE + 15


def experts(nc, dram):
    with ExitStack() as ctx:
        def sb(name, shape, dt=F32):
            return ctx.enter_context(nc.sbuf_tensor("e_" + name, shape, dt))

        def sem(name):
            return ctx.enter_context(nc.semaphore("e_" + name))

        NS = S // P
        HR = 4
        turned = [ctx.enter_context(nc.psum_tensor(f"e_turned{i}", [P, KD, S], F32)) for i in range(2)]
        hbank = [ctx.enter_context(nc.psum_tensor(f"e_h{i}", [P, 2, S], F32)) for i in range(HR)]
        obank = [ctx.enter_context(nc.psum_tensor(f"e_o{i}", [P, NS, D], F32)) for i in range(2)]
        ident = sb("ident", [P, P])
        ones = sb("ones", [1, P])
        tex = sb("tex", [1, NT], I32)
        w1 = [sb(f"w1{i}", [P, KD, 2 * FF]) for i in range(2)]
        w2 = [sb(f"w2{i}", [P, KF, D]) for i in range(2)]
        w1h, w1l, w2h, w2l = ([sb(f"{n}{i}", shape, F32R) for i in range(2)] for n, shape in
                              (("w1h", [P, KD, 2 * FF]), ("w1l", [P, KD, 2 * FF]), ("w2h", [P, KF, D]), ("w2l", [P, KF, D])))
        b1 = [sb(f"b1{i}", [P, 2 * KF]) for i in range(2)]
        b2 = [sb(f"b2{i}", [1, D]) for i in range(2)]
        xg = [sb(f"xg{i}", [P, NS, D]) for i in range(2)]
        xTh, xTl = ([sb(f"{n}{i}", [P, KD, S], F32R) for i in range(2)] for n in ("xTh", "xTl"))
        sg = sb("sg", [P, 2, S])
        ac = sb("ac", [P, 2, S])
        ach, acl = ([sb(f"{n}{i}", [P, KF, S], F32R) for i in range(2)] for n in ("ach", "acl"))
        yo = [sb(f"yo{i}", [P, NS, D]) for i in range(2)]
        tex_in, s_id = sem("tex_in"), sem("id")
        w_in = [sem(f"w_in{i}") for i in range(2)]
        x_in = [sem(f"x_in{i}") for i in range(2)]
        y_out = [sem(f"y_out{i}") for i in range(2)]
        small_in = [sem(f"small_in{i}") for i in range(2)]
        s_wh, s_wl, s_xTl, s_ah, s_al = sem("wh"), sem("wl"), sem("xTl"), sem("ah"), sem("al")
        s_turn, s_xT, s_h, s_sg, s_ac, s_o, s_y = (sem("turn"), sem("xT"), sem("h"), sem("sg"), sem("ac"), sem("o"),
                                                   sem("y"))
        block = ctx.enter_context(nc.Block())

        def f32(ap):
            return ap.bitcast(F32)

        def pairs(eng, tile):
            with eng.Fori(0, NT // 2 - 1) as g:
                tile(g * 2, g, 0, True)
                tile(g * 2 + 1, g, 1, True)
            tile(NT - 2, NT // 2 - 1, 0, True)
            tile(NT - 1, NT // 2 - 1, 1, False)

        def after(t, g, i):
            return t + 1, g + i, 1 - i

        def piece(w, m):
            n = 2 * FF // KF
            return w[:, :, m * n:(m + 1) * n]

        @block.gpsimd
        def _(pool):
            identity(pool, ident, s_id)
            pool.memset(ones[:], 1.0).then_inc(s_id, 1)
            pool.sem_inc(s_al, 2)

            def tile(t, g, i, follows):
                for m in range(KF):
                    pool.wait_ge(s_ah, t * KF + (m + 1))
                    pool.tensor_tensor(acl[i][:, m], ac[:, m % 2], f32(ach[i][:, m]), ALU.subtract).then_inc(s_al, 1)

            pairs(pool, tile)

        @block.sync
        def _(sp):
            sp.dma_start(tex[:], dram["tex"]).then_inc(tex_in, 16)
            sp.wait_ge(tex_in, 16)

            def load_weights(t, i):
                e = sp.value_load(tex[0:1, bass.ds(t, 1)], min_val=0, max_val=NE - 1)
                sp.wait_ge(s_wl, t * SPLITS + SPLITS)
                sp.wait_ge(tex_in, 16)
                sp.dma_start(w1[i][:], dram["w1"][bass.ds(e * P, P), :, :]).then_inc(w_in[i], 16)
                sp.dma_start(w2[i][:], dram["w2"][bass.ds(e * P, P), :, :]).then_inc(w_in[i], 16)

            def load_rows(t, i):
                e = sp.value_load(tex[0:1, bass.ds(t, 1)], min_val=0, max_val=NE - 1)
                sp.wait_ge(s_o, t + 1)
                sp.wait_ge(tex_in, 16)
                sp.dma_start(xg[i][:], dram["xg"][bass.ds(t * S, S), :].rearrange("(s p) d -> p s d", p=P)).then_inc(x_in[i], 16)
                sp.dma_start(b1[i][:], dram["b1"][bass.ds(e * P, P), :]).then_inc(small_in[i], 16)
                sp.dma_start(b2[i][:], dram["b2"][bass.ds(e, 1), :]).then_inc(small_in[i], 16)

            def store(t, i):
                sp.wait_ge(s_y, t + 3)
                sp.dma_start(dram["yg"][bass.ds(t * S, S), :].rearrange("(s p) d -> p s d", p=P), yo[i][:]).then_inc(y_out[i], 16)

            load_weights(0, 0)
            load_rows(0, 0)
            load_weights(1, 1)
            load_rows(1, 1)
            with sp.Fori(0, NT // 2 - 1) as g:
                for i in range(2):
                    load_weights(g * 2 + (2 + i), i)
                    load_rows(g * 2 + (2 + i), i)
                    store(g * 2 + i, i)
            for i in range(2):
                store(NT - 2 + i, i)
            for i in range(2):
                sp.wait_ge(y_out[i], 16 * (NT // 2 + 1))

        @block.scalar
        def _(act):
            for i in range(2):
                act.sem_inc(y_out[i], 16)

            def high(t, g, i, m):
                if m == 0:
                    act.wait_ge(w_in[i], g * 32 + 32)
                    act.wait_ge(s_o, t + 1)
                act.activation(piece(w1h[i], m), piece(w1[i], m), ACT.Copy).then_inc(s_wh, 1)
                act.activation(w2h[i][:, m], w2[i][:, m], ACT.Copy).then_inc(s_wh, 1)

            def high_rows(t, i):
                act.wait_ge(s_turn, t + 1)
                act.activation(xTh[i][:], turned[i][:], ACT.Copy).then_inc(s_xT, 1)

            def tile(t, g, i, follows):
                for m in range(KF):
                    act.wait_ge(s_h, t * KF + (m + 1))
                    if m == 0:
                        act.wait_ge(small_in[i], g * 32 + 32)
                    act.wait_ge(s_ac, t * KF + (m + 1))
                    act.activation(sg[:, m % 2], hbank[m % HR][:, 1], ACT.Silu,
                                   bias=b1[i][:, KF + m:KF + m + 1]).then_inc(s_sg, 1)
                    if follows:
                        high(*after(t, g, i), m)
                if follows:
                    high_rows(t + 1, 1 - i)
                act.wait_ge(s_o, t + 3)
                act.wait_ge(y_out[i], g * 16 + 16)
                act.activation(yo[i][:], obank[i][:], ACT.Copy).then_inc(s_y, 1)

            for m in range(KF):
                high(0, 0, 0, m)
            high_rows(0, 0)
            pairs(act, tile)

        @block.vector
        def _(dve):
            dve.sem_inc(s_ac, 2)
            dve.sem_inc(s_o, 2)
            dve.sem_inc(s_y, 2)
            dve.sem_inc(s_wl, 2 * SPLITS)

            def low(t, i, m):
                dve.wait_ge(s_wh, t * SPLITS + 2 * (m + 1))
                dve.tensor_tensor(piece(w1l[i], m), piece(w1[i], m), f32(piece(w1h[i], m)), ALU.subtract).then_inc(s_wl, 1)
                dve.tensor_tensor(w2l[i][:, m], w2[i][:, m], f32(w2h[i][:, m]), ALU.subtract).then_inc(s_wl, 1)

            def low_rows(t, i):
                dve.wait_ge(s_xT, t + 1)
                dve.tensor_tensor(xTl[i][:], turned[i][:], f32(xTh[i][:]), ALU.subtract).then_inc(s_xTl, 1)

            def tile(t, g, i, follows):
                for m in range(KF):
                    dve.wait_ge(s_sg, t * KF + (m + 1))
                    dve.wait_ge(s_al, t * KF + (m + 1))
                    dve.scalar_tensor_tensor(out=ac[:, m % 2], in0=hbank[m % HR][:, 0], scalar=b1[i][:, m:m + 1],
                                             in1=sg[:, m % 2], op0=ALU.add, op1=ALU.mult).then_inc(s_ac, 1)
                    dve.wait_ge(s_ac, t * KF + (2 + m + 1))
                    if m == 0:
                        dve.wait_ge(s_o, t + 1)
                    dve.tensor_copy(ach[i][:, m], ac[:, m % 2]).then_inc(s_ah, 1)
                    if follows:
                        low(t + 1, 1 - i, m)
                if follows:
                    low_rows(t + 1, 1 - i)

            for m in range(KF):
                low(0, 0, m)
            low_rows(0, 0)
            pairs(dve, tile)

        @block.tensor
        def _(pe):
            mm = pe.matmul
            pe.wait_ge(s_id, 3)

            def turn(t, g, i):
                pe.wait_ge(x_in[i], g * 16 + 16)
                if not (isinstance(t, int) and t < 2):
                    pe.wait_ge(s_xTl, t - 1)
                for k in range(KD):
                    for s in range(NS):
                        last = pe.transpose(turned[i][:, k, s * P:(s + 1) * P], xg[i][:, s, k * P:(k + 1) * P], ident[:])
                last.then_inc(s_turn, 1)

            def tile(t, g, i, nxt):
                pe.wait_ge(s_xTl, t + 1)
                pe.wait_ge(s_wl, t * SPLITS + 3 * SPLITS)
                for m in range(KF):
                    if m >= HR or not isinstance(t, int) or t > 0:
                        pe.wait_ge(s_ac, t * KF + (2 + m + 1 - HR))
                    for j in range(2):
                        cols = slice(j * FF + m * P, j * FF + (m + 1) * P)
                        for k in range(KD):
                            for p, (w, x) in enumerate(((w1h, xTh), (w1h, xTl), (w1l, xTh))):
                                last = mm(hbank[m % HR][:, j], w[i][:, k, cols], x[i][:, k],
                                          start=(p == 0 and k == 0 and j == 0), stop=(p == 2 and k == KD - 1 and j == 1),
                                          skip_group_check=True)
                    last.then_inc(s_h, 1)
                if nxt is not None:
                    turn(*nxt)
                pe.wait_ge(s_y, t + 1)
                pe.wait_ge(small_in[i], g * 32 + 32)
                for s in range(NS):
                    mm(obank[i][:, s], ones[:], b2[i][:], start=(s == 0), stop=False, skip_group_check=True)
                for m in range(KF):
                    pe.wait_ge(s_al, t * KF + (2 + m + 1))
                    for s in range(NS):
                        for p, (a, w) in enumerate(((ach, w2h), (ach, w2l), (acl, w2h))):
                            last = mm(obank[i][:, s], a[i][:, m, s * P:(s + 1) * P], w[i][:, m], start=False,
                                      stop=(p == 2 and m == KF - 1 and s == NS - 1), skip_group_check=True)
                last.then_inc(s_o, 1)

            turn(0, 0, 0)
            tile(0, 0, 0, (1, 0, 1))
            with pe.Fori(0, NT // 2 - 1) as g:
                tile(g * 2 + 1, g, 1, (g * 2 + 2, g + 1, 0))
                tile(g * 2 + 2, g + 1, 0, (g * 2 + 3, g + 1, 1))
            tile(NT - 1, NT // 2 - 1, 1, None)


def combine(nc, dram, out):
    with ExitStack() as ctx:
        def sb(name, shape, dt=F32):
            return ctx.enter_context(nc.sbuf_tensor("c_" + name, shape, dt))

        def sem(name):
            return ctx.enter_context(nc.semaphore("c_" + name))

        dst = sb("dst", [P, NPICK], I32)
        wts = sb("wts", [P, NPICK])
        ya = sb("ya", [P, NPICK, D])
        xa = sb("xa", [P, NJ, D])
        mo = sb("mo", [P, NJ, D])
        small_in, y_in, out_done = sem("small_in"), sem("y_in"), sem("out_done")
        x_in = [sem(f"x_in{i}") for i in range(NCH)]
        s_add, s_y1, s_y2 = sem("add"), sem("y1"), sem("y2")
        yj = [sem(f"yj{i}") for i in range(NCH)]
        block = ctx.enter_context(nc.Block())

        @block.sync
        def _(sp):
            sp.dma_start(dst[:], dram["dst"]).then_inc(small_in, 16)
            sp.dma_start(wts[:], dram["wts"]).then_inc(small_in, 16)
            for c in range(NCH):
                for tile, src in ((xa, dram["x1p"]), (mo, dram["mo"][T:, :])):
                    sp.dma_start(tile[:, c * SUB:(c + 1) * SUB], src[c * T:(c + 1) * T, :].rearrange("(s p) d -> p s d", p=P)).then_inc(x_in[c], 16)
            for c in range(NCH):
                sp.wait_ge(s_y2, (c + 1) * SUB)
                sp.dma_start(out[c * T:(c + 1) * T, :].rearrange("(s p) d -> p s d", p=P), xa[:, c * SUB:(c + 1) * SUB]).then_inc(out_done, 16)
            sp.wait_ge(out_done, 16 * NCH)

        @block.gpsimd
        def _(pool):
            pool.wait_ge(small_in, 32)
            for c in range(NCH):
                for j in range(c * SUB, (c + 1) * SUB):
                    for k in range(TOPK):
                        a = k * NJ + j
                        pool.indirect_dma_start(ya[:, a, :], None, dram["yg"][:, :],
                                                bass.IndirectOffsetOnAxis(ap=dst[:, a:a + 1], axis=0)).then_inc(yj[c], 16)

        @block.vector
        def _(dve):
            dve.wait_ge(small_in, 32)
            for c in range(NCH):
                cs = slice(c * SUB, (c + 1) * SUB)
                dve.wait_ge(x_in[c], 32)
                dve.tensor_tensor(xa[:, cs], xa[:, cs], mo[:, cs], ALU.add).then_inc(s_add, 1)
                dve.wait_ge(s_add, c + 1)
                dve.wait_ge(yj[c], 16 * SUB * TOPK)
                for k, done in ((0, s_y1), (1, s_y2)):
                    for j in range(c * SUB, (c + 1) * SUB):
                        a = k * NJ + j
                        if k == 1:
                            dve.wait_ge(s_y1, j + 1)
                        dve.scalar_tensor_tensor(out=xa[:, j], in0=ya[:, a], scalar=wts[:, a:a + 1], in1=xa[:, j],
                                                 op0=ALU.mult, op1=ALU.add).then_inc(done, 1)


def kernel(**inputs):
    import numpy as np
    import concourse.bacc as bacc
    from concourse.bass_utils import run_bass_kernel_spmd

    a = {k: np.ascontiguousarray(v) for k, v in inputs.items()}
    g = lambda n: a["L0_attn_" + n]
    f = lambda n: a["L0_ffn_" + n]
    m = lambda n: a["L1_attn_" + n]
    x = lambda n: a["L1_ffn_" + n]

    def blocks(w):
        return np.ascontiguousarray(w.reshape(-1, P, w.shape[1]).transpose(1, 0, 2))

    def cols(v):
        return np.ascontiguousarray(v.reshape(-1, P, v[0].size).transpose(1, 0, 2).reshape(P, -1))

    arrays = {
        "x": np.concatenate([g("hidden_states").reshape(NTOK, D), np.zeros((T, D), np.float32)]),
        "w_p": blocks(np.concatenate([g("fc_r_w"), g("fc_i_w"), g("fc_w"), g("fc_gate_w")]).T),
        "w_m": blocks(np.concatenate([g("mlp_gate_w"), g("mlp_fc_w")]).T),
        "w_o": blocks(g("out_w").T),
        "w_f": blocks(f("w_fc").T),
        "w_j": blocks(f("w_proj").T),
        "vec0": np.concatenate([cols(v) for v in (g("fc_r_b"), g("fc_i_b"), g("fc_b"), g("fc_gate_b"), g("mlp_gate_b"),
                                                  g("mlp_fc_b"), g("norm_w"), g("norm2_w"), g("alpha").reshape(-1))], axis=1),
        "out_b": g("out_b").reshape(1, D),
        "gate_b": x("gate_b").reshape(1, NE),
        "gate_w": blocks(x("gate_w")),
        "low_v": f("v"),
        "low_b": np.ascontiguousarray(f("fast_b").T),
        "low_u": np.ascontiguousarray(f("u").T),
        "low_g": f("gate").reshape(1, 1),
        "w_si": blocks(np.concatenate([m("skip_w"), m("in_w")]).T),
        "w_x": blocks(np.concatenate([m("wB"), m("wC"), m("wd1")]).T),
        "w_dt": np.ascontiguousarray(m("wd2").T),
        "w_out": blocks(m("out_w").T),
        "vec1": np.concatenate([cols(v) for v in (m("norm_w"), m("conv_w"), m("conv_b"), m("wd2_b"), m("A_log"), m("W_D"))], axis=1),
        "w1": np.ascontiguousarray(x("w1").reshape(NE, KD, P, 2 * FF).transpose(0, 2, 1, 3).reshape(NE * P, KD, 2 * FF)),
        "w2": np.ascontiguousarray(x("w2").reshape(NE, KF, P, D).transpose(0, 2, 1, 3).reshape(NE * P, KF, D)),
        "b1": np.ascontiguousarray(x("b1").reshape(NE, 2 * KF, P).transpose(0, 2, 1).reshape(NE * P, 2 * KF)),
        "b2": x("b2"),
    }
    nc = bacc.Bacc("TRN2", target_bir_lowering=False, num_devices=1)
    dram = {n: nc.dram_tensor("in_" + n, v.shape, F32, kind="ExternalInput").ap() for n, v in arrays.items()}
    out = nc.dram_tensor("out", (NTOK, D), F32, kind="ExternalOutput").ap()
    program(nc, dram, out)
    r = run_bass_kernel_spmd(nc, [{"in_" + n: v for n, v in arrays.items()}], core_ids=[0])
    return r.results[0]["out"].reshape(NTOK // SEQ, SEQ, D)


def program(nc, dram, out):
    dram = dict(dram)
    for name, shape, dt in (("x1p", (NTOK, D), F32), ("xn1", (NTOK, D), F32), ("xrT", (NCH * P, KD, T), F32),
                            ("logits", (P, NJ, NE), F32), ("mo", (T + NTOK, D), F32), ("xg", (NSLOT, D), F32),
                            ("yg", (NSLOT, D), F32), ("dst", (P, NPICK), I32), ("tex", (1, NT), I32),
                            ("wts", (P, NPICK), F32)):
        dram[name] = nc.dram_tensor("scratch_" + name, shape, dt, kind="Internal").ap()
    layer0(nc, dram)
    routing(nc, dram)
    mamba(nc, dram)
    experts(nc, dram)
    combine(nc, dram, out)
```

```python
from contextlib import ExitStack

import concourse.bass as bass
from concourse import mybir

P = 128
F32 = mybir.dt.float32
F32R = mybir.dt.float32r
BF16 = mybir.dt.bfloat16
I32 = mybir.dt.int32
U32 = mybir.dt.uint32
ALU = mybir.AluOpType
ACT = mybir.ActivationFunctionType
AX_X = mybir.AxisListType.X

NTOK = 4096
SEQ = 1024
D = 256
KD = D // P
T = 512
NCH = NTOK // T
CPS = SEQ // T
SUB = T // P
MLP = 768
KM = MLP // P
HID = 1024
KH = HID // P
RANK = 16
EPS_LN = 1e-5
EPS_RMS0 = 1e-6
EPS_RMS1 = 1e-5
BANKS = 8

V0 = {}
_at = 0
for _name, _n in (("r_b", KD), ("i_b", KD), ("hs_b", KD), ("gate_b", KD), ("mg_b", KM), ("mf_b", KM),
                  ("norm_w", KD), ("norm2_w", KD), ("alpha", KD)):
    V0[_name] = _at
    _at += _n
NV0 = _at


def identity(pool, tile, done):
    pool.memset(tile[:, :], 0.0).then_inc(done, 1)
    pool.wait_ge(done, 1)
    pool.affine_select(out=tile[:, :], in_=tile[:, :], compare_op=ALU.not_equal, fill=1.0, base=0,
                       pattern=[[-1, P]], channel_multiplier=1).then_inc(done, 1)


NE = 8
TOPK = 2
FF = 1024
KF = FF // P
NJ = NTOK // P
NPICK = TOPK * NJ
S = 256
NT = (NTOK * TOPK + NE * (S - 1)) // S
assert NT % 2 == 1
NSLOT = NT * S
TMAX = NTOK // S

FMS = 4


def layer0(nc, dram):
    order = ([f"F{m}" for m in range(FMS)] + ["MS"] + [f"F{m}" for m in range(FMS, KH)]
             + [g for m in range(KM) for g in (f"MG{m}", f"MF{m}")] + ["O0", "O1"]
             + ["XT0", "XT1", "HT0", "HT1", "R0", "R1", "I0", "I1", "H0", "H1", "GA0", "GA1"]
             + ["N0", "N1", "Q0", "Q1", "L"])
    assert len(order) % BANKS == 0
    uses = len(order) // BANKS
    place = {g: (p % BANKS, p // BANKS) for p, g in enumerate(order)}

    with ExitStack() as ctx:
        def sb(name, shape, dt=F32):
            return ctx.enter_context(nc.sbuf_tensor(name, shape, dt))

        def sem(name):
            return ctx.enter_context(nc.semaphore(name))

        bank = [ctx.enter_context(nc.psum_tensor(f"bank{i}", [P, T], F32)) for i in range(BANKS)]
        w_ph, w_pl = (sb(n, [P, KD, 4 * D], F32R) for n in ("w_ph", "w_pl"))
        w_mh, w_ml = (sb(n, [P, KD, 2 * MLP], F32R) for n in ("w_mh", "w_ml"))
        w_fh, w_fl = (sb(n, [P, KD, HID], F32R) for n in ("w_fh", "w_fl"))
        w_o = sb("w_o", [P, KM, D])
        w_j = sb("w_j", [P, KH, D])
        vec = sb("vec", [P, NV0])
        brow = sb("brow", [P, D])
        gb = sb("gb", [P, 8])
        gw = sb("gw", [P, KD, 8])
        low_v = sb("low_v", [RANK, D])
        low_b = sb("low_b", [RANK, RANK])
        mg = sb("mg", [P, 2, T])
        low_u = mg[0:RANK].rearrange("p a t -> p (a t)")
        low_g = sb("low_g", [RANK, 1])
        low_z = sb("low_z", [RANK, D])
        ident = sb("ident", [P, P])
        inv_d = sb("inv_d", [P, P])
        inv_h = sb("inv_h", [P, P])
        neghalf = sb("neghalf", [P, SUB])
        eps_ln, eps_rms0, eps_rms1 = (sb(f"eps_{n}", [P, SUB]) for n in ("ln", "rms0", "rms1"))
        sp = sb("sp", [P, 3, KD])
        eps0 = sb("eps0", [P, 1])
        ca = sb("ca", [P, KD])
        xt = sb("xt", [P, SUB, D])
        xres = sb("xres", [P, SUB, D])
        xn = sb("xn", [P, SUB, D])
        hn = sb("hn", [P, SUB, D])
        x1 = sb("x1", [P, SUB, D])
        xn1 = sb("xn1", [P, SUB, D])
        xr1 = sb("xr1", [P, SUB, D])
        x1p = sb("x1p", [P, SUB, D])
        stats = sb("stats", [P, SUB, 6])
        mv = sb("mv", [P, SUB, 2])
        stats1 = sb("stats1", [P, SUB, 6])
        seen = sb("seen", [P, SUB])
        mv1 = sb("mv1", [P, SUB, 2])
        small = sb("small", [P, 6, SUB])
        small1 = sb("small1", [P, 6, SUB])
        lg = sb("lg", [P, NCH * SUB, 8])
        xnTh, xnTl, hTh, hTl, h2h, h2l = (sb(n, [P, KD, T], F32R) for n in ("xnTh", "xnTl", "hTh", "hTl", "h2h", "h2l"))
        rT = sb("rT", [P, KD, T])
        iT = sb("iT", [P, KD, T])
        gT = sb("gT", [P, KD, T])
        tT = sb("tT", [P, KD, T])
        aT = sb("aT", [P, KD, T])
        qT = sb("qT", [P, KD, T])
        oT = qT
        quad = sb("quad", [P, 4 * KD, T])
        hs2, xn1T, xr1T = (quad[:, j * KD:(j + 1) * KD] for j in (0, 2, 3))
        sq = quad[:, KD:2 * KD]
        rms = sq[:, KD - 1]
        rinv = sb("rinv", [P, T])
        fm = sb("fm", [P, (KH + KM) * T])
        fT = fm[:, 0:KH * T].rearrange("p (k t) -> p k t", t=T)
        mT = fm[:, KH * T:(KH + KM) * T].rearrange("p (k t) -> p k t", t=T)
        ends = [0, 4 * D * KD, (4 * D + 2 * MLP) * KD, (4 * D + 2 * MLP + HID) * KD]
        assert ends[3] <= (KH + KM) * T
        w_p, w_m, w_f = (fm[:, a:b].rearrange("p (k n) -> p k n", k=KD) for a, b in zip(ends, ends[1:]))
        abs_f, abs_j = quad[:, 0:2 * KD], quad[:, 2 * KD:4 * KD]
        zero = x1p
        carry = sb("carry", [P, KD])
        keep = sb("keep", [P, 1])

        filled = [sem(f"filled{i}") for i in range(BANKS)]
        drained = [sem(f"drained{i}") for i in range(BANKS)]
        weights_in = sem("weights_in")
        x_in = sem("x_in")
        xres_in = sem("xres_in")
        x1p_out, xn1_out, xrT_out, lg_out = sem("x1p_out"), sem("xn1_out"), sem("xrT_out"), sem("lg_out")
        s_id = sem("s_id")
        s_const = sem("s_const")
        s_zero, zero_out = sem("s_zero"), sem("zero_out")
        s_prep = sem("s_prep")
        s_prepa = sem("s_prepa")
        s_split = sem("s_split")
        s_hTh, s_xsum, s_h2h, s_h2l = sem("s_hTh"), sem("s_xsum"), sem("s_h2h"), sem("s_h2l")
        s_xTh, s_xb = sem("s_xTh"), sem("s_xb")
        p_prep = sem("p_prep")
        s_st = sem("s_st")
        s_pw = sem("s_pw")
        s_ln = sem("s_ln")
        s_a = sem("s_a")
        s_a2 = sem("s_a2")
        s_q = sem("s_q")
        s_s = sem("s_s")
        s_scan = sem("s_scan")
        s_carry = sem("s_carry")
        s_og = sem("s_og")
        s_hs2 = sem("s_hs2")
        s_sq = sem("s_sq")
        s_rinv = sem("s_rinv")
        s_h2 = sem("s_h2")
        s_fsq = sem("s_fsq")
        s_st1 = sem("s_st1")
        s_pw1 = sem("s_pw1")
        s_l1 = sem("s_l1")
        block = ctx.enter_context(nc.Block())

        def wait_filled(eng, g, c):
            b, i = place[g]
            eng.wait_ge(filled[b], c * uses + (uses + i + 1))

        def wait_drained(eng, g, c):
            b, i = place[g]
            eng.wait_ge(drained[b], c * uses + (uses + i + 1))

        def wait_bank(pe, g, c):
            b, i = place[g]
            pe.wait_ge(drained[b], c * uses + (uses + i))

        def inc_filled(ins, g):
            ins.then_inc(filled[place[g][0]], 1)

        def inc_drained(ins, g):
            ins.then_inc(drained[place[g][0]], 1)

        def ps(g):
            return bank[place[g][0]]

        def rows(ap, c):
            return ap[bass.ds(c * T, T), :].rearrange("(s p) d -> p s d", p=P)

        w_loads = [(w_p, dram["w_p"]), (w_m, dram["w_m"]), (w_o[:], dram["w_o"]), (w_f, dram["w_f"]),
                   (w_j[:], dram["w_j"]), (vec[:], dram["vec0"]), (brow[:], dram["out_b"].to_broadcast([P, D])),
                   (gb[:], dram["gate_b"].to_broadcast([P, 8])), (gw[:], dram["gate_w"]),
                   (low_v[:], dram["low_v"]), (low_b[:], dram["low_b"]), (low_u, dram["low_u"]),
                   (low_g[:], dram["low_g"].to_broadcast([RANK, 1]))]
        weights_all = 16 * len(w_loads)

        def f32(ap):
            return ap.bitcast(F32)

        @block.sync
        def _(sp_):
            sp_.dma_start(xt[:], rows(dram["x"], 0)).then_inc(x_in, 16)
            for dst, src in w_loads:
                sp_.dma_start(dst, src).then_inc(weights_in, 16)
            sp_.wait_ge(s_zero, 1)
            for at in range(0, NSLOT, T):
                part = dram["xg"][at:min(at + T, NSLOT), :].rearrange("(s p) d -> p s d", p=P)
                sp_.dma_start(part, zero[:, 0:part.shape[1]]).then_inc(zero_out, 16)
            with sp_.Fori(0, NCH) as c:
                wait_drained(sp_, "O1", c - 1)
                sp_.dma_start(xres[:], rows(dram["x"], c)).then_inc(xres_in, 16)
                sp_.wait_ge(s_ln, c * 8 + 8)
                sp_.dma_start(xt[:], rows(dram["x"], c + 1)).then_inc(x_in, 16)
                sp_.wait_ge(s_l1, c * 12 + 12)
                sp_.dma_start(rows(dram["x1p"], c), x1p[:]).then_inc(x1p_out, 16)
                sp_.dma_start(rows(dram["xn1"], c), xn1[:]).then_inc(xn1_out, 16)
                wait_drained(sp_, "Q1", c)
                wait_drained(sp_, "Q0", c)
                sp_.dma_start(dram["xrT"][bass.ds(c * P, P), :, :], xr1T).then_inc(xrT_out, 16)
            wait_drained(sp_, "L", NCH - 1)
            sp_.dma_start(dram["logits"], lg[:]).then_inc(lg_out, 16)
            sp_.wait_ge(lg_out, 16)
            sp_.wait_ge(zero_out, 16 * -(-NSLOT // T))
            for s in (x1p_out, xn1_out, xrT_out):
                sp_.wait_ge(s, 16 * NCH + 16)

        @block.gpsimd
        def _(pool):
            identity(pool, ident, s_id)
            for tile, value in ((inv_d, 1.0 / D), (inv_h, 1.0 / HID), (neghalf, -0.5),
                                (carry, 0.0), (keep, 1.0), (eps_ln, EPS_LN), (eps_rms0, EPS_RMS0),
                                (eps_rms1, EPS_RMS1)):
                pool.memset(tile[:], value).then_inc(s_const, 1)
            pool.memset(zero[:], 0.0).then_inc(s_zero, 1)
            pool.wait_ge(s_const, 8)

            def row_scales(sm, mvt, done, base, eps_rms):
                var = mvt[:, :, 1]
                pool.tensor_tensor(sm[:, 0], var, eps_ln[:], ALU.add).then_inc(done, 1)
                pool.wait_ge(done, base + 1)
                pool.tensor_tensor(sm[:, 1], sm[:, 0], neghalf[:], ALU.pow).then_inc(done, 1)
                pool.wait_ge(done, base + 2)
                pool.tensor_tensor(sm[:, 2], sm[:, 1], sm[:, 1], ALU.mult).then_inc(done, 1)
                pool.wait_ge(done, base + 3)
                pool.tensor_tensor(sm[:, 3], sm[:, 2], var, ALU.mult).then_inc(done, 1)
                pool.wait_ge(done, base + 4)
                pool.tensor_tensor(sm[:, 2], sm[:, 3], eps_rms[:], ALU.add).then_inc(done, 1)
                pool.wait_ge(done, base + 5)
                pool.tensor_tensor(sm[:, 4], sm[:, 2], neghalf[:], ALU.pow).then_inc(done, 1)
                pool.wait_ge(done, base + 6)
                pool.tensor_tensor(sm[:, 5], sm[:, 4], sm[:, 1], ALU.mult).then_inc(done, 1)

            pool.wait_ge(s_st, 9)
            row_scales(small, mv, s_pw, 0, eps_rms0)
            pool.wait_ge(s_prepa, 7)
            pool.tensor_tensor(w_ml[:], w_m, f32(w_mh[:]), ALU.subtract).then_inc(s_split, 1)
            with pool.Fori(0, NCH) as c:
                pool.wait_ge(s_st, c * 9 + 18)
                row_scales(small, mv, s_pw, c * 7 + 7, eps_rms0)
                for m in range(KH):
                    wait_drained(pool, f"F{m}", c)
                    pool.tensor_tensor(fT[:, m], fT[:, m], fT[:, m], ALU.mult).then_inc(s_fsq, 1)
                pool.wait_ge(xres_in, c * 16 + 16)
                pool.tensor_tensor(xres[:], xres[:], brow[:].rearrange("p (o d) -> p o d", o=1).to_broadcast([P, SUB, D]),
                                   ALU.add).then_inc(s_xb, 1)
                pool.wait_ge(s_st1, c * 9 + 9)
                row_scales(small1, mv1, s_pw1, c * 7, eps_rms1)

        @block.scalar
        def _(act):
            act.wait_ge(weights_in, weights_all)
            al = vec[:, V0["alpha"]:V0["alpha"] + KD]
            act.activation(sp[:, 0], al, ACT.Abs).then_inc(s_prepa, 1)
            act.wait_ge(s_prepa, 1)
            act.activation(sp[:, 1], sp[:, 0], ACT.Exp, scale=-1.0).then_inc(s_prepa, 1)
            act.wait_ge(s_prepa, 2)
            act.activation(sp[:, 2], sp[:, 1], ACT.Ln, bias=1.0).then_inc(s_prepa, 1)
            act.activation(abs_f, w_f.rearrange("p k (a n) -> p (k a) n", n=T), ACT.Abs).then_inc(s_prepa, 1)
            act.activation(abs_j, w_j[:].rearrange("p (k a) n -> p k (a n)", a=2), ACT.Abs).then_inc(s_prepa, 1)

            def project(c):
                for k in range(KD):
                    wait_filled(act, f"XT{k}", c)
                    act.activation(xnTh[:, k], ps(f"XT{k}")[:], ACT.Copy).then_inc(s_xTh, 1)
                for name, dst, b, f in (("R", rT, "r_b", ACT.Sigmoid), ("I", iT, "i_b", ACT.Sigmoid),
                                        ("GA", gT, "gate_b", ACT.Gelu)):
                    for k in range(KD):
                        wait_filled(act, f"{name}{k}", c)
                        inc_drained(act.activation(dst[:, k], ps(f"{name}{k}")[:], f,
                                                   bias=vec[:, V0[b] + k:V0[b] + k + 1]), f"{name}{k}")

            act.wait_ge(s_prep, 1)
            act.wait_ge(s_prep, 1 + 2 * KD)
            act.activation(w_ph[:], w_p, ACT.Copy).then_inc(s_prepa, 1)
            act.activation(w_mh[:], w_m, ACT.Copy).then_inc(s_prepa, 1)
            act.wait_ge(s_prep, PREP_STEPS)
            act.activation(w_fh[:], w_f, ACT.Copy).then_inc(s_prepa, 1)

            def relu(ms, c):
                for m in ms:
                    wait_filled(act, f"F{m}", c)
                    inc_drained(act.activation(fT[:, m], ps(f"F{m}")[:], ACT.Relu), f"F{m}")

            def decay(c):
                for k in range(KD):
                    wait_drained(act, f"R{k}", c)
                    if k == 0:
                        act.wait_ge(s_scan, (c + 1) * KD + KD)
                    act.activation(aT[:, k], rT[:, k], ACT.Exp, scale=ca[:, k:k + 1]).then_inc(s_a, 1)

            project(-1)
            decay(-1)
            with act.Fori(0, NCH) as c:
                for k in range(KD):
                    act.wait_ge(s_a2, c * KD + (k + 1))
                    act.activation(qT[:, k], qT[:, k], ACT.Sqrt, bias=1.0, scale=-1.0).then_inc(s_q, 1)
                relu(range(FMS), c)
                wait_filled(act, "MS", c)
                act.wait_ge(s_rinv, c + 1)
                inc_drained(act.activation(rms, ps("MS")[:], ACT.Sqrt, bias=eps0[:, 0:1]), "MS")
                relu(range(FMS, KH), c)
                for m in range(KM):
                    g = f"MG{m}"
                    wait_filled(act, g, c)
                    if m >= 2:
                        wait_drained(act, f"MF{m - 2}", c)
                    inc_drained(act.activation(mg[:, m % 2], ps(g)[:], ACT.Gelu,
                                               bias=vec[:, V0["mg_b"] + m:V0["mg_b"] + m + 1]), g)
                project(c)
                decay(c)
                act.wait_ge(xrT_out, c * 16 + 16)
                for k in range(KD):
                    wait_filled(act, f"Q{k}", c)
                    inc_drained(act.activation(xr1T[:, k], ps(f"Q{k}")[:], ACT.Copy), f"Q{k}")

        @block.vector
        def _(dve):
            dve.memset(eps0[:], EPS_RMS0).then_inc(s_prep, 1)

            def statistics(src, st, mvt, done, base):
                for s in range(SUB):
                    dve.bn_stats(st[:, s], src[:, s]).then_inc(done, 1)
                dve.wait_ge(done, base + SUB)
                dve.tensor_copy(seen[:], st[:, :, 0]).then_inc(done, 1)
                for s in range(SUB):
                    dve.bn_aggr(mvt[:, s], st[:, s]).then_inc(done, 1)

            def centre(src, mvt, sm, done, normed, rms_normed):
                for s in range(SUB):
                    dve.tensor_scalar(normed[:, s], src[:, s], mvt[:, s, 0:1], sm[:, 1, s:s + 1],
                                      ALU.subtract, ALU.mult).then_inc(done, 1)
                    dve.tensor_scalar(rms_normed[:, s], src[:, s], mvt[:, s, 0:1], sm[:, 5, s:s + 1],
                                      ALU.subtract, ALU.mult).then_inc(done, 1)

            def next_rows(c):
                dve.wait_ge(x_in, c * 16 + 32)
                statistics(xt, stats, mv, s_st, c * 9 + 9)
                dve.wait_ge(s_st, c * 9 + 18)
                dve.wait_ge(s_pw, c * 7 + 14)
                centre(xt, mv, small, s_ln, xn, hn)

            next_rows(-1)
            dve.wait_ge(weights_in, weights_all)
            n = [1]

            def step(ins, then_wait=True):
                ins.then_inc(s_prep, 1)
                n[0] += 1
                if then_wait:
                    dve.wait_ge(s_prep, n[0])

            for k in range(KD):
                step(dve.tensor_scalar(w_p[:, k], w_p[:, k], vec[:, V0["norm_w"] + k:V0["norm_w"] + k + 1], None, ALU.mult))
                step(dve.tensor_scalar(w_m[:, k], w_m[:, k], vec[:, V0["norm2_w"] + k:V0["norm2_w"] + k + 1], None, ALU.mult))
            dve.wait_ge(s_prepa, 3)
            al = vec[:, V0["alpha"]:V0["alpha"] + KD]
            step(dve.tensor_scalar(sp[:, 0], al, 0.0, None, ALU.max))
            step(dve.tensor_tensor(sp[:, 1], sp[:, 0], sp[:, 2], ALU.add))
            step(dve.tensor_scalar(ca[:], sp[:, 1], -8.0, None, ALU.mult))
            dve.wait_ge(p_prep, 1)
            step(dve.tensor_scalar(low_z[:], bank[0][0:RANK, 0:D], low_g[:, 0:1], None, ALU.mult))

            def ternary(parts, mean, scale, half_scale, ready):
                dve.wait_ge(p_prep, ready)
                step(dve.tensor_scalar(scale, mean, 1e-5, None, ALU.max))
                step(dve.tensor_scalar(half_scale, scale, 0.5, None, ALU.mult))
                for w, over, under in parts:
                    step(dve.tensor_tensor(over, w, half_scale, ALU.is_gt))
                    step(dve.scalar_tensor_tensor(out=under, in0=w, scalar=-1.0, in1=half_scale, op0=ALU.mult,
                                                  op1=ALU.is_gt))
                    step(dve.tensor_tensor(over, over, under, ALU.subtract))
                    step(dve.tensor_tensor(w, over, scale, ALU.mult))

            for a in range(2):
                half = slice(a * T, (a + 1) * T)
                ternary([(w_f[:, k, half], qT[:, k], tT[:, k]) for k in range(KD)], bank[1 + a][:], rms, rinv[:], 2)
            ternary([(w_j[:, k], x1[:, 0], x1[:, 1]) for k in range(KH)], bank[3][:, 0:D], rms[:, 0:D],
                    rinv[:, 0:D], 3)
            dve.wait_ge(p_prep, 4)
            for k in range(KD):
                for a in range(2):
                    half = slice(a * T, (a + 1) * T)
                    step(dve.tensor_tensor(w_f[:, k, half], w_f[:, k, half], bank[4 + 2 * k + a][:], ALU.add))
            assert n[0] == PREP_STEPS, n[0]
            dve.wait_ge(s_prepa, 7)
            dve.tensor_tensor(w_pl[:], w_p, f32(w_ph[:]), ALU.subtract).then_inc(s_split, 1)
            dve.wait_ge(s_prepa, 8)
            dve.tensor_tensor(w_fl[:], w_f, f32(w_fh[:]), ALU.subtract).then_inc(s_split, 1)

            def turned_h(c):
                for k in range(KD):
                    wait_filled(dve, f"HT{k}", c)
                    dve.tensor_copy(hTh[:, k], ps(f"HT{k}")[:]).then_inc(s_hTh, 1)
                for k in range(KD):
                    dve.wait_ge(s_hTh, c * KD + (KD + k + 1))
                    inc_drained(dve.tensor_tensor(hTl[:, k], ps(f"HT{k}")[:], f32(hTh[:, k]), ALU.subtract), f"HT{k}")

            def project(c):
                for k in range(KD):
                    dve.wait_ge(s_xTh, c * KD + (KD + k + 1))
                    inc_drained(dve.tensor_tensor(xnTl[:, k], ps(f"XT{k}")[:], f32(xnTh[:, k]), ALU.subtract), f"XT{k}")
                for k in range(KD):
                    wait_filled(dve, f"H{k}", c)
                    wait_drained(dve, f"I{k}", c)
                    inc_drained(dve.scalar_tensor_tensor(
                        out=tT[:, k], in0=ps(f"H{k}")[:], scalar=vec[:, V0["hs_b"] + k:V0["hs_b"] + k + 1],
                        in1=iT[:, k], op0=ALU.add, op1=ALU.mult), f"H{k}")

            def squares(c):
                for k in range(KD):
                    dve.wait_ge(s_a, c * KD + (KD + k + 1))
                    dve.tensor_tensor(qT[:, k], aT[:, k], aT[:, k], ALU.mult).then_inc(s_a2, 1)
                for k in range(KD):
                    wait_drained(dve, f"XT{k}", c)
                    dve.tensor_tensor(hs2[:, k], f32(xnTh[:, k]), f32(xnTl[:, k]), ALU.add).then_inc(s_xsum, 1)

            dve.sem_inc(s_scan, KD)
            dve.sem_inc(s_rinv, 1)
            dve.sem_inc(s_carry, 3)
            dve.sem_inc(xrT_out, 16)
            dve.sem_inc(x1p_out, 16)
            dve.sem_inc(xn1_out, 16)
            turned_h(-1)
            project(-1)
            squares(-1)
            dve.wait_ge(s_const, 8)
            with dve.Fori(0, NCH) as c:
                for k in range(KD):
                    dve.wait_ge(s_q, c * KD + (k + 1))
                    wait_drained(dve, f"H{k}", c - 1)
                    dve.tensor_tensor(tT[:, k], tT[:, k], qT[:, k], ALU.mult).then_inc(s_s, 1)
                for k in range(KD):
                    dve.wait_ge(s_s, c * KD + (k + 1))
                    dve.wait_ge(s_carry, c * 3 + 3)
                    dve.tensor_tensor_scan(oT[:, k], aT[:, k], tT[:, k], carry[:, k:k + 1],
                                           ALU.mult, ALU.add).then_inc(s_scan, 1)
                for k in range(KD):
                    dve.wait_ge(s_scan, c * KD + (KD + k + 1))
                    dve.tensor_scalar(carry[:, k:k + 1], oT[:, k, T - 1:T], keep[:, 0:1], None, ALU.mult).then_inc(s_carry, 1)
                dve.wait_ge(s_carry, c * 3 + 5)
                dve.tensor_scalar(keep[:], keep[:], -1.0, 1.0, ALU.mult, ALU.add).then_inc(s_carry, 1)
                for k in range(KD):
                    wait_drained(dve, f"GA{k}", c - 1)
                    dve.tensor_tensor(oT[:, k], oT[:, k], gT[:, k], ALU.mult).then_inc(s_og, 1)
                for k in range(KD):
                    dve.wait_ge(s_og, c * KD + (k + 1))
                    dve.wait_ge(s_xsum, c * KD + (k + 1))
                    dve.tensor_tensor(hs2[:, k], oT[:, k], hs2[:, k], ALU.add).then_inc(s_hs2, 1)
                for k in range(KD):
                    dve.wait_ge(s_hs2, c * KD + (k + 1))
                    dve.tensor_tensor(sq[:, k], hs2[:, k], hs2[:, k], ALU.mult).then_inc(s_sq, 1)
                wait_drained(dve, "MS", c)
                dve.reciprocal(rinv[:], rms).then_inc(s_rinv, 1)
                dve.wait_ge(s_rinv, c + 2)
                for k in range(KD):
                    dve.tensor_tensor(h2h[:, k], hs2[:, k], rinv[:], ALU.mult).then_inc(s_h2h, 1)
                for k in range(KD):
                    dve.tensor_tensor(sq[:, k], hs2[:, k], rinv[:], ALU.mult).then_inc(s_h2, 1)
                    dve.wait_ge(s_h2, c * KD + (k + 1))
                    dve.tensor_tensor(h2l[:, k], sq[:, k], f32(h2h[:, k]), ALU.subtract).then_inc(s_h2l, 1)
                dve.wait_ge(x_in, c * 16 + 32)
                statistics(xt, stats, mv, s_st, c * 9 + 9)
                dve.wait_ge(s_st, c * 9 + 18)
                dve.wait_ge(s_pw, c * 7 + 14)
                centre(xt, mv, small, s_ln, xn, hn)
                for m in range(KM):
                    wait_filled(dve, f"MF{m}", c)
                    wait_drained(dve, f"MG{m}", c)
                    inc_drained(dve.scalar_tensor_tensor(
                        out=mT[:, m], in0=ps(f"MF{m}")[:], scalar=vec[:, V0["mf_b"] + m:V0["mf_b"] + m + 1],
                        in1=mg[:, m % 2], op0=ALU.add, op1=ALU.mult), f"MF{m}")
                dve.wait_ge(s_xb, c + 1)
                for j in range(2):
                    wait_filled(dve, f"O{j}", c)
                    inc_drained(dve.tensor_tensor(x1[:, 2 * j:2 * j + 2], ps(f"O{j}")[:].rearrange("p (s d) -> p s d", s=2),
                                                  xres[:, 2 * j:2 * j + 2], ALU.add), f"O{j}")
                turned_h(c)
                wait_drained(dve, "O0", c)
                wait_drained(dve, "O1", c)
                statistics(x1, stats1, mv1, s_st1, c * 9)
                project(c)
                dve.wait_ge(s_st1, c * 9 + 9)
                dve.wait_ge(s_pw1, c * 7 + 7)
                dve.wait_ge(xn1_out, c * 16 + 16)
                dve.wait_ge(x1p_out, c * 16 + 16)
                centre(x1, mv1, small1, s_l1, xn1, xr1)
                dve.wait_ge(zero_out, 16 * -(-NSLOT // T))
                dve.wait_ge(s_l1, c * 12 + 8)
                for s in range(SUB):
                    dve.tensor_tensor(x1p[:, s], x1[:, s], xn1[:, s], ALU.add).then_inc(s_l1, 1)
                for k in range(KD):
                    wait_filled(dve, f"N{k}", c)
                    inc_drained(dve.tensor_copy(xn1T[:, k], ps(f"N{k}")[:]), f"N{k}")
                squares(c)
                wait_filled(dve, "L", c)
                inc_drained(dve.tensor_tensor(lg[:, bass.ds(c * SUB, SUB), :], ps("L")[:, 0:SUB * 8].rearrange("p (s e) -> p s e", e=8),
                                              gb[:].rearrange("p (o e) -> p o e", o=1).to_broadcast([P, SUB, 8]),
                                              ALU.add), "L")

        @block.tensor
        def _(pe):
            mm = pe.matmul
            pe.wait_ge(weights_in, weights_all)
            pe.wait_ge(s_const, 8)
            pe.wait_ge(s_id, 2)
            mm(bank[0][0:RANK, 0:D], low_b[:], low_v[:], start=True, stop=True).then_inc(p_prep, 1)
            pe.wait_ge(s_prepa, 5)
            wabs = abs_f.rearrange("p (k a) n -> p k a n", a=2)
            for a in range(2):
                for k in range(KD):
                    last = mm(bank[1 + a][:], inv_d[:], wabs[:, k, a], start=(k == 0), stop=(k == KD - 1))
            last.then_inc(p_prep, 1)
            wabs = abs_j.rearrange("p k (a n) -> p (k a) n", a=2)
            for k in range(KH):
                last = mm(bank[3][:, 0:D], inv_h[:], wabs[:, k], start=(k == 0), stop=(k == KH - 1))
            last.then_inc(p_prep, 1)
            pe.wait_ge(s_prep, LOWZ_STEP)
            for k in range(KD):
                for a in range(2):
                    last = mm(bank[4 + 2 * k + a][:], low_z[:, k * P:(k + 1) * P], low_u[:, a * T:(a + 1) * T],
                              start=True, stop=True)
            last.then_inc(p_prep, 1)
            pe.wait_ge(s_prep, PREP_STEPS)
            pe.wait_ge(s_split, 3)
            first = order.index("XT0")
            after = order.index("N0")
            for b in range(BANKS):
                skipped = sum(1 for p in range(first) if p % BANKS == b)
                pe.sem_inc(drained[b], skipped)
                pe.sem_inc(filled[b], skipped)

            def product(g, w, cols, rhs, nk, c, ready=None):
                wait_bank(pe, g, c)
                for k in range(nk):
                    if ready is not None:
                        ready(0, k)
                    mm(ps(g)[:], w[0][:, k, cols], rhs[0][:, k], start=(k == 0), stop=False)
                    mm(ps(g)[:], w[1][:, k, cols], rhs[0][:, k], start=False, stop=False)
                for k in range(nk):
                    if ready is not None:
                        ready(1, k)
                    last = mm(ps(g)[:], w[0][:, k, cols], rhs[1][:, k], start=False, stop=(k == nk - 1))
                inc_filled(last, g)

            def turn(g, src, k, c):
                wait_bank(pe, g, c)
                for s in range(SUB):
                    last = pe.transpose(ps(g)[:, s * P:(s + 1) * P], src[:, s, k * P:(k + 1) * P], ident[:])
                inc_filled(last, g)

            def project(c):
                def h_ready(part, k):
                    if part == 0:
                        pe.wait_ge(s_hTh, c * KD + (KD + k + 1))
                    else:
                        wait_drained(pe, f"HT{k}", c)

                pe.wait_ge(s_ln, c * 8 + 16)
                for k in range(KD):
                    turn(f"XT{k}", xn, k, c)
                for k in range(KD):
                    turn(f"HT{k}", hn, k, c)
                for j, name in enumerate(("R", "I", "H", "GA")):
                    for m in range(KD):
                        product(f"{name}{m}", (w_ph, w_pl), slice(j * D + m * P, j * D + (m + 1) * P), (hTh, hTl), KD, c,
                                ready=h_ready if j + m == 0 else None)

            project(-1)
            for p in range(after, len(order)):
                b = p % BANKS
                pe.wait_ge(drained[b], p // BANKS)
                pe.sem_inc(filled[b], 1)
                pe.sem_inc(drained[b], 1)
            with pe.Fori(0, NCH) as c:
                def x_ready(part, k):
                    if part == 0:
                        pe.wait_ge(s_xTh, c * KD + (k + 1))
                    else:
                        wait_drained(pe, f"XT{k}", c - 1)

                def h2_ready(part, k):
                    pe.wait_ge((s_h2h, s_h2l)[part], c * KD + (k + 1))

                for m in range(KH):
                    if m == FMS:
                        wait_bank(pe, "MS", c)
                        for k in range(KD):
                            pe.wait_ge(s_sq, c * KD + (k + 1))
                            last = mm(ps("MS")[:], inv_d[:], sq[:, k], start=(k == 0), stop=(k == KD - 1))
                        inc_filled(last, "MS")
                    product(f"F{m}", (w_fh, w_fl), slice(m * P, (m + 1) * P), (xnTh, xnTl), KD, c,
                            ready=x_ready if m == 0 else None)
                for m in range(KM):
                    for j, name in enumerate(("MG", "MF")):
                        product(f"{name}{m}", (w_mh, w_ml), slice(j * MLP + m * P, j * MLP + (m + 1) * P), (h2h, h2l), KD, c,
                                ready=h2_ready if m + j == 0 else None)
                pe.wait_ge(s_hs2, c * KD + KD)
                for j in range(2):
                    wait_bank(pe, f"O{j}", c)
                    for s in (2 * j, 2 * j + 1):
                        cols = slice(s * P, (s + 1) * P)
                        out = ps(f"O{j}")[:, (s % 2) * D:(s % 2 + 1) * D]
                        for k in range(KD):
                            mm(out[:, k * P:(k + 1) * P], hs2[:, k, cols], ident[:], start=(s % 2 + k == 0), stop=False,
                               skip_group_check=True)
                        for m in range(KH):
                            if s == 0:
                                pe.wait_ge(s_fsq, c * KH + (m + 1))
                            mm(out, fT[:, m, cols], w_j[:, m], start=False, stop=False, skip_group_check=True)
                        for m in range(KM):
                            if s == 0:
                                wait_drained(pe, f"MF{m}", c)
                            last = mm(out, mT[:, m, cols], w_o[:, m], start=False, stop=(s % 2 == 1 and m == KM - 1),
                                      skip_group_check=True)
                    inc_filled(last, f"O{j}")
                project(c)
                pe.wait_ge(s_l1, c * 12 + 8)
                for k in range(KD):
                    turn(f"N{k}", xn1, k, c)
                for k in range(KD):
                    turn(f"Q{k}", xr1, k, c)
                wait_bank(pe, "L", c)
                for s in range(SUB):
                    for k in range(KD):
                        if s == 0:
                            wait_drained(pe, f"N{k}", c)
                        last = mm(ps("L")[:, s * 8:(s + 1) * 8], xn1T[:, k, s * P:(s + 1) * P], gw[:, k],
                                  start=(k == 0), stop=(k == KD - 1))
                inc_filled(last, "L")


LOWZ_STEP = 1 + 2 * KD + 3 + 1
PREP_STEPS = LOWZ_STEP + 2 * (2 + 4 * KD) + 2 + 4 * KH + 2 * KD


E_IN = 512
KE = E_IN // P
NST = 16
DR = 64
TAPS = 4
PAD = TAPS - 1
NSEQ = NTOK // SEQ
V1 = {}
_at = 0
for _name, _n in (("norm_w", KD), ("conv_w", KE * TAPS), ("conv_b", KE), ("dt_b", KE), ("A_log", KE * NST),
                  ("W_D", KE)):
    V1[_name] = _at
    _at += _n
NV1 = _at


def mamba(nc, dram):
    RING = 4
    NA = 4
    SCAN0 = NA * KE
    OUT = {0: "O0", 1: "O1"}
    ahead = {n: [] for n in range(NST)}
    for e in range(KE):
        ahead[2 + e].append(f"IN{e}")
        ahead[3 + e].append(f"SK{e}")
        ahead[10 + e // 2].append(f"DT{e}")
    ahead[8] = ["BC"]
    ahead[9] = ["DR"]

    def spread_at(n):
        return [(f"B{(n + 2) % NST}", n + 2 >= NST), (f"C{(n + 1) % NST}", n + 1 >= NST)]

    def listing(last):
        order = []
        for n in range(NST):
            order += [g for g, of_next in spread_at(n) if not (last and of_next)]
            if n in OUT:
                order += [OUT[n]]
            if not last:
                order += ahead[n]
        return order + (["Z0", "Z1"] if last else [])

    first = [g for n in range(NST) for g in ahead[n]] + ["B0", "C15", "B1", "C0"]
    place = {"first": {g: p for p, g in enumerate(first)}, "body": {g: p for p, g in enumerate(listing(False))},
             "last": {g: p for p, g in enumerate(listing(True))}}
    lead, per = len(first), len(listing(False))
    assert per % RING == 0 and all(lead + place["body"][g] - per == place["first"][g] for g in ("B0", "C15", "B1", "C0"))

    with ExitStack() as ctx:
        def sb(name, shape, dt=F32):
            return ctx.enter_context(nc.sbuf_tensor("m_" + name, shape, dt))

        def sem(name):
            return ctx.enter_context(nc.semaphore("m_" + name))

        ybank = [ctx.enter_context(nc.psum_tensor(f"m_y{e}", [P, T], F32)) for e in range(KE)]
        ring = [ctx.enter_context(nc.psum_tensor(f"m_ring{i}", [P, T], F32)) for i in range(RING)]
        w_si = sb("w_si", [P, KD, 2 * E_IN])
        w_x = sb("w_x", [P, KE, DR + 2 * NST])
        w_dt = sb("w_dt", [DR, E_IN])
        w_out = sb("w_out", [P, KE, D])
        vec = sb("vec", [P, NV1])
        A = sb("A", [P, KE * NST])
        ident = sb("ident", [P, P])
        sel = sb("sel", [3 * 2 * NST, 2 * NST], BF16)
        xr = sb("xr", [P, KD, T])
        xpad = [sb(f"xpad{h}", [P, KE, PAD + T]) for h in range(2)]
        cv = sb("cv", [P, KE, T])
        xs = [sb(f"xs{h}", [P, KE, T]) for h in range(2)]
        sk = [sb(f"sk{h}", [P, KE, T]) for h in range(2)]
        dl = [sb(f"dl{h}", [P, KE, T]) for h in range(2)]
        ux = [sb(f"ux{h}", [P, KE, T]) for h in range(2)]
        bc3 = [sb(f"bc3{h}", [3 * 2 * NST, T], BF16) for h in range(2)]
        bc2 = sb("bc2", [2 * NST, T], BF16)
        dr = sb("dr", [DR, T])
        z = sb("z", [P, KE, T])
        ez = sb("ez", [P, KE, T])
        bcr = ez[0:2 * NST, 0]
        dA = sb("dA", [P, NA, KE, T])
        bb = sb("bb", [P, 2, T])
        bx_hc = sb("bx_hc", [P, 4, KE, T])
        bx, hc = bx_hc[:, 0:2], bx_hc[:, 2:4]
        hh = sb("hh", [P, 1, KE, T])
        rows = bx_hc[:].rearrange("p a e t -> p (a e t)").rearrange("p (j d) -> p j d", d=D)
        dst = sb("dst", [P, NPICK], I32)
        carry = sb("carry", [P, NST, KE])
        y1 = ez
        mo = z[:, 0:SUB * D // T].rearrange("p e t -> p (e t)").rearrange("p (s d) -> p s d", d=D)

        filled = [sem(f"filled{i}") for i in range(RING)]
        drained = [sem(f"drained{i}") for i in range(RING)]
        w_in, xr_in, mo_out = sem("w_in"), sem("xr_in"), sem("mo_out")
        rows_in, picks_out = [sem(f"rows_in{c}") for c in range(NCH)], sem("picks_out")
        s_id, s_sel, s_pad, s_prep, s_A = sem("s_id"), sem("s_sel"), sem("s_pad"), sem("s_prep"), sem("s_A")
        s_xp, s_conv, s_xs, s_sk, s_bca, s_bcd = sem("s_xp"), sem("s_conv"), sem("s_xs"), sem("s_sk"), sem("s_bca"), sem("s_bcd")
        s_abs, s_ez, s_w, s_ln, s_dl, s_ux = (sem("s_abs"), sem("s_ez"), sem("s_w"), sem("s_ln"), sem("s_dl"),
                                              sem("s_ux"))
        s_exp, s_bx, s_scan, s_carry, s_y = sem("s_exp"), sem("s_bx"), sem("s_scan"), sem("s_carry"), sem("s_y")
        s_yf, s_y2, s_zero = sem("s_yf"), sem("s_y2"), sem("s_zero")
        block = ctx.enter_context(nc.Block())

        def spot(g, at):
            kind, i, h = at
            p = place[kind][g]
            if kind == "first":
                return p % RING, p // RING
            return (lead + p) % RING, i * (per // RING) + (lead + p) // RING

        def bank_of(g, at):
            return (place[at[0]][g] + (0 if at[0] == "first" else lead)) % RING

        def wait_filled(eng, g, at):
            b, k = spot(g, at)
            eng.wait_ge(filled[b], k + 1)

        def wait_drained(eng, g, at):
            b, k = spot(g, at)
            eng.wait_ge(drained[b], k + 1)

        def wait_bank(pe, g, at):
            b, k = spot(g, at)
            if not (isinstance(k, int) and k == 0):
                pe.wait_ge(drained[b], k)

        def inc(ins, sems, g, at):
            ins.then_inc(sems[bank_of(g, at)], 1)

        def tile_of(g, at):
            return ring[bank_of(g, at)]

        START = ("first", -1, 1)

        def before(at):
            return ("body", at[1] - 1, 1 - at[2])

        def at_of(at, g):
            return before(at) if g in ("B0", "B1", "C0") else at

        def program(eng, ahead_of, step, end):
            ahead_of(START, 0, 0, range(NST))

            def chunk(i, h, last):
                at = ("last" if last else "body", i, h)
                for n in range(NST):
                    step(at, i, h, n, last)
                    if n in OUT:
                        end(at, i, 1 - h, OUT[n])
                    if not last:
                        ahead_of(at, i + 1, 1 - h, [n])

            with eng.Fori(0, NSEQ - 1) as b:
                chunk(b * 2, 0, False)
                chunk(b * 2 + 1, 1, False)
            chunk(2 * NSEQ - 2, 0, False)
            chunk(2 * NSEQ - 1, 1, True)
            for g in ("Z0", "Z1"):
                end(("last", 2 * NSEQ - 1, 1), 2 * NSEQ, 1, g)

        w_loads = [(w_si, dram["w_si"]), (w_x, dram["w_x"]), (w_dt, dram["w_dt"]), (w_out, dram["w_out"]),
                   (vec, dram["vec1"])]

        @block.sync
        def _(sp):
            sp.dma_start(xr[:], dram["xrT"][0:P]).then_inc(xr_in, 16)
            sp.dma_start(dst[:], dram["dst"]).then_inc(rows_in[0], 16)

            def load_rows(c):
                sp.dma_start(rows[:, c * SUB:(c + 1) * SUB],
                             dram["xn1"][c * T:(c + 1) * T, :].rearrange("(s p) d -> p s d", p=P)).then_inc(rows_in[c], 16)

            load_rows(0)
            for tile, src in w_loads:
                sp.dma_start(tile[:], src).then_inc(w_in, 16)
            for c in range(1, NCH):
                load_rows(c)

            def ahead_of(at, q, h, slots):
                if 6 in slots:
                    if not (isinstance(q, int) and q == 2 * NSEQ - 1):
                        wait_filled(sp, "SK3", at)
                        sp.dma_start(xr[:], dram["xrT"][bass.ds((q + 1) * P, P), :, :]).then_inc(xr_in, 16)

            def end(at, i, h, g):
                if g[1] == "0":
                    return
                wait_drained(sp, g[0] + "0", at)
                wait_drained(sp, g, at)
                sp.dma_start(dram["mo"][bass.ds(i * T, T), :].rearrange("(s p) d -> p s d", p=P), mo).then_inc(mo_out, 16)

            program(sp, ahead_of, lambda *_: None, end)
            sp.wait_ge(mo_out, 16 * (NCH + 1) + 16)

        @block.gpsimd
        def _(pool):
            identity(pool, ident, s_id)
            pool.memset(sel[:], 0.0).then_inc(s_sel, 1)
            pool.memset(xpad[0][:, :, 0:PAD], 0.0).then_inc(s_pad, 1)
            for j in range(3):
                pool.wait_ge(s_sel, j + 1)
                pool.affine_select(out=sel[:], in_=sel[:], compare_op=ALU.not_equal, fill=1.0, base=-2 * NST * j,
                                   pattern=[[-1, 2 * NST]], channel_multiplier=1).then_inc(s_sel, 1)
            pool.sem_inc(s_bx, 2)
            pool.memset(xs[1][:], 0.0).then_inc(s_zero, 1)
            pool.memset(sk[1][:], 0.0).then_inc(s_zero, 1)

            for c in range(NCH):
                pool.wait_ge(rows_in[c], 32 if c == 0 else 16)
                for j in range(c * SUB, (c + 1) * SUB):
                    for k in range(TOPK):
                        a = k * NJ + j
                        pool.indirect_dma_start(dram["xg"][:, :], bass.IndirectOffsetOnAxis(ap=dst[:, a:a + 1], axis=0),
                                                rows[:, j, :], None).then_inc(picks_out, 16)
            pool.wait_ge(picks_out, 16 * NPICK)

            def step(at, i, h, n, last):
                wait_drained(pool, f"B{n}", at_of(at, f"B{n}"))
                if n == 0:
                    pool.wait_ge(s_ux, i + 1)
                pool.wait_ge(s_scan, i * (NST * KE) + (SCAN0 + KE * (n - 1)))
                pool.tensor_tensor(bx[:, n % 2], ux[h][:], bb[:, n % 2:n % 2 + 1, :].to_broadcast([P, KE, T]),
                                   ALU.mult).then_inc(s_bx, 1)

            program(pool, lambda *_: None, step, lambda *_: None)

        @block.scalar
        def _(act):
            act.wait_ge(w_in, 16 * len(w_loads))
            act.activation(A[:], vec[:, V1["A_log"]:V1["A_log"] + KE * NST], ACT.Exp).then_inc(s_prep, 1)
            act.sem_inc(mo_out, 16)
            act.sem_inc(s_sk, 1)

            def b_row(i, n, at):
                wait_filled(act, f"B{n}", at)
                act.wait_ge(s_bx, i * NST + (n + 1))
                inc(act.activation(bb[:, n % 2], tile_of(f"B{n}", at)[:], ACT.Copy), drained, f"B{n}", at)

            def decays(i, h, n):
                if n == 0:
                    act.wait_ge(s_dl, i * 3 + 3)
                    act.wait_ge(s_A, 1)
                act.wait_ge(s_scan, i * (NST * KE) + (SCAN0 + KE * (n + 1 - NA)))
                for e in range(KE):
                    act.activation(dA[:, n % NA, e], dl[h][:, e], ACT.Exp,
                                   scale=A[:, e * NST + n:e * NST + n + 1]).then_inc(s_exp, 1)

            def ahead_of(at, q, h, slots):
                for n in slots:
                    for g in ahead[n]:
                        if g in ("BC", "DR"):
                            continue
                        e = int(g[2:])
                        wait_filled(act, g, at)
                        if g[:2] == "IN":
                            act.activation(xpad[h][:, e, PAD:PAD + T], tile_of(g, at)[:], ACT.Copy).then_inc(s_xp, 1)
                            if e == 0 and at[0] != "first":
                                act.wait_ge(s_dl, q * 3)
                            tap = V1["conv_w"] + e * TAPS + PAD
                            ins = act.activation(cv[:, e], tile_of(g, at)[:], ACT.Identity, scale=vec[:, tap:tap + 1],
                                                 bias=vec[:, V1["conv_b"] + e:V1["conv_b"] + e + 1])
                        elif g[:2] == "SK":
                            if e == 0 and at[0] != "first":
                                act.wait_ge(s_y2, q)
                            ins = act.activation(sk[h][:, e], tile_of(g, at)[:], ACT.Copy)
                        else:
                            if e == 0:
                                act.wait_ge(mo_out, q * 16 + 16)
                            ins = act.activation(z[:, e], tile_of(g, at)[:], ACT.Identity,
                                                 bias=vec[:, V1["dt_b"] + e:V1["dt_b"] + e + 1])
                        inc(ins, drained, g, at)
                    if n == 7:
                        wait_drained(act, "SK3", at)
                        act.wait_ge(s_conv, q * (KE * PAD) + (KE * PAD))
                        act.activation(xs[h][:], cv[:], ACT.Silu).then_inc(s_xs, 1)
                        act.activation(sk[h][:], sk[h][:], ACT.Silu).then_inc(s_sk, 1)
                    if n == 8:
                        wait_filled(act, "BC", at)
                        act.activation(bc3[h][0:2 * NST, :], tile_of("BC", at)[0:2 * NST, :], ACT.Copy).then_inc(s_bca, 1)
                    if n == 9:
                        wait_filled(act, "DR", at)
                        inc(act.activation(dr[:], tile_of("DR", at)[0:DR, :], ACT.Copy), drained, "DR", at)
                    if n == 10:
                        act.wait_ge(s_bcd, q * 3 + 3)
                        act.activation(bc3[h][2 * NST:4 * NST, :], bc2[:], ACT.Copy).then_inc(s_bca, 1)
                    if n == 11:
                        wait_drained(act, f"DT{KE - 1}", at)
                        act.activation(ez[:], z[:], ACT.Abs).then_inc(s_abs, 1)
                        act.wait_ge(s_abs, q + 1)
                        act.activation(ez[:], ez[:], ACT.Exp, scale=-1.0).then_inc(s_ez, 1)
                    if n == 12:
                        act.wait_ge(s_dl, q * 3 + 1)
                        act.activation(cv[:], cv[:], ACT.Ln).then_inc(s_ln, 1)
                if at[0] == "first":
                    for n in range(2):
                        b_row(0, n, START)
                    for n in range(2):
                        decays(0, 0, n)

            def step(at, i, h, n, last):
                if n < NST - 2:
                    decays(i, h, n + 2)
                elif not last:
                    decays(i + 1, 1 - h, n + 2 - NST)
                for g, of_next in spread_at(n):
                    if g[0] == "B" and not (last and of_next):
                        b_row(i + 1 if of_next else i, int(g[1:]), at)

            def end(at, i, h, g):
                j = int(g[1])
                if j == 0:
                    act.wait_ge(mo_out, i * 16 + 16)
                    act.wait_ge(s_dl, i * 3 + (0 if g == "Z0" else 3))
                wait_filled(act, g, at)
                inc(act.activation(mo[:, 2 * j:2 * j + 2], tile_of(g, at)[:].rearrange("p (s d) -> p s d", s=2),
                                   ACT.Copy), drained, g, at)

            program(act, ahead_of, step, end)

        @block.vector
        def _(dve):
            dve.wait_ge(s_prep, 1)
            dve.tensor_scalar(A[:], A[:], -1.0, None, ALU.mult).then_inc(s_A, 1)
            for k in range(KD):
                dve.tensor_scalar(w_si[:, k], w_si[:, k], vec[:, V1["norm_w"] + k:V1["norm_w"] + k + 1], None,
                                  ALU.mult).then_inc(s_prep, 1)
            dve.sem_inc(s_scan, SCAN0)
            for e in range(KE):
                dve.memset(ybank[e][:], 0.0).then_inc(s_zero, 1)
            dve.wait_ge(s_zero, 2 + KE)
            dve.wait_ge(s_pad, 1)

            def ahead_of(at, q, h, slots):
                for n in slots:
                    if 3 <= n < KE + 3:
                        e = n - 3
                        w = [vec[:, V1["conv_w"] + e * TAPS + k:V1["conv_w"] + e * TAPS + k + 1] for k in range(TAPS)]
                        base = q * (KE * PAD) + e * PAD
                        if h == 1:
                            dve.tensor_copy(xpad[1][:, e, 0:PAD], xpad[0][:, e, T:T + PAD]).then_inc(s_pad, 1)
                            dve.wait_ge(s_pad, (q - 1) * 2 + (e + 2))
                        wait_drained(dve, f"IN{e}", at)
                        for k in range(PAD):
                            if k > 0:
                                dve.wait_ge(s_conv, base + k)
                            dve.scalar_tensor_tensor(out=cv[:, e], in0=xpad[h][:, e, k:k + T], scalar=w[k], in1=cv[:, e],
                                                     op0=ALU.mult, op1=ALU.add).then_inc(s_conv, 1)
                    if n == 9:
                        dve.wait_ge(s_bca, q * 2 + 1)
                        inc(dve.tensor_tensor(bcr, tile_of("BC", at)[0:2 * NST, :], bc3[h][0:2 * NST, :], ALU.subtract),
                            drained, "BC", at)
                        dve.sem_inc(s_bcd, 1)
                        wait_drained(dve, "BC", at)
                        dve.tensor_copy(bc2[:], bcr).then_inc(s_bcd, 1)
                        dve.wait_ge(s_bcd, q * 3 + 2)
                        dve.tensor_tensor(bc3[h][4 * NST:6 * NST, :], bcr, bc2[:], ALU.subtract).then_inc(s_bcd, 1)
                    if n == 12:
                        dve.wait_ge(s_ez, q + 1)
                        dve.tensor_scalar(cv[:], ez[:], 1.0, None, ALU.add).then_inc(s_w, 1)
                        dve.wait_ge(s_w, q + 1)
                        dve.scalar_tensor_tensor(out=ez[:], in0=cv[:], scalar=-1.0, in1=ez[:], op0=ALU.add,
                                                 op1=ALU.subtract).then_inc(s_dl, 1)
                    if n == 13:
                        dve.wait_ge(s_ln, q + 1)
                        dve.tensor_tensor(ez[:], cv[:], ez[:], ALU.subtract).then_inc(s_dl, 1)
                        dve.wait_ge(s_dl, q * 3 + 2)
                        dve.scalar_tensor_tensor(out=dl[h][:], in0=z[:], scalar=0.0, in1=ez[:], op0=ALU.max,
                                                 op1=ALU.add).then_inc(s_dl, 1)
                    if n == 14:
                        dve.wait_ge(s_dl, q * 3 + 3)
                        dve.wait_ge(s_xs, q + 1)
                        dve.tensor_tensor(ux[h][:], dl[h][:], xs[h][:], ALU.mult).then_inc(s_ux, 1)

            def finish(i, h):
                dve.wait_ge(s_y, i * NST + 2)
                for e in range(KE):
                    dve.scalar_tensor_tensor(out=y1[:, e], in0=xs[h][:, e], scalar=vec[:, V1["W_D"] + e:V1["W_D"] + e + 1],
                                             in1=ybank[e][:], op0=ALU.mult, op1=ALU.add).then_inc(s_yf, 1)
                dve.wait_ge(s_yf, i * KE + KE)
                dve.wait_ge(s_sk, i + 1)
                dve.tensor_tensor(y1[:], y1[:], sk[h][:], ALU.mult).then_inc(s_y2, 1)

            def step(at, i, h, n, last):
                here = at_of(at, f"C{n}")
                if n == 0:
                    wait_drained(dve, f"C{NST - 1}", before(at))
                else:
                    wait_drained(dve, f"C{n - 1}", at_of(at, f"C{n - 1}"))
                if h == 0 and n > 0:
                    dve.wait_ge(s_carry, i * (NST // 2) + n)
                dve.wait_ge(s_bx, i * NST + (2 + n + 1))
                for e in range(KE):
                    dve.wait_ge(s_exp, i * (NST * KE) + (KE * n + e + 1))
                    if h == 1 and n == 0 and e == 0:
                        dve.wait_ge(s_carry, (i - 1) * (NST // 2) + NST)
                    dve.tensor_tensor_scan(hh[:, 0, e], dA[:, n % NA, e], bx[:, n % 2, e],
                                           0.0 if h == 0 else carry[:, n, e:e + 1], ALU.mult, ALU.add).then_inc(s_scan, 1)
                if n == 0:
                    finish(i, 1 - h)
                wait_filled(dve, f"C{n}", here)
                dve.wait_ge(s_scan, i * (NST * KE) + (SCAN0 + KE * (n + 1)))
                dve.wait_ge(s_y, i * NST + (n + 1))
                inc(dve.tensor_tensor(hc[:, n % 2], hh[:, 0],
                                      tile_of(f"C{n}", here)[:].rearrange("p (o t) -> p o t", o=1).to_broadcast([P, KE, T]),
                                      ALU.mult), drained, f"C{n}", here)
                if h == 0:
                    dve.tensor_copy(carry[:, n, :], hh[:, 0, :, T - 1]).then_inc(s_carry, 1)

            def end(at, i, h, g):
                if g == "Z0":
                    finish(i, h)

            program(dve, ahead_of, step, end)

        @block.tensor
        def _(pe):
            mm = pe.matmul
            pe.wait_ge(w_in, 16 * len(w_loads))
            pe.wait_ge(s_prep, 1 + KD)
            pe.wait_ge(s_id, 2)
            pe.wait_ge(s_sel, 4)
            pe.sem_inc(s_y, 2)

            def spread(g, q, h, at):
                n = int(g[1:]) + (NST if g[0] == "C" else 0)
                wait_bank(pe, g, at)
                if g == "B0":
                    pe.wait_ge(s_bca, q * 2 + 2)
                    pe.wait_ge(s_bcd, q * 3 + 3)
                inc(mm(tile_of(g, at)[:], sel[:, n:n + 1].to_broadcast([3 * 2 * NST, P]), bc3[h][:], start=True, stop=True), filled, g, at)

            def pieces(at, q, h, slots):
                for n in slots:
                    for g in ahead[n]:
                        wait_bank(pe, g, at)
                        out = tile_of(g, at)
                        if g[:2] in ("IN", "SK"):
                            e = int(g[2:])
                            if g == "IN0":
                                pe.wait_ge(xr_in, q * 16 + 16)
                            col = (E_IN if g[:2] == "IN" else 0) + e * P
                            for k in range(KD):
                                last = mm(out[:], w_si[:, k, col:col + P], xr[:, k], start=(k == 0), stop=(k == KD - 1))
                        elif g in ("BC", "DR"):
                            pe.wait_ge(s_xs, q + 1)
                            cols = slice(0, 2 * NST) if g == "BC" else slice(2 * NST, 2 * NST + DR)
                            for e in range(KE):
                                last = mm(out[0:cols.stop - cols.start, :], w_x[:, e, cols], xs[h][:, e],
                                          start=(e == 0), stop=(e == KE - 1))
                        else:
                            e = int(g[2:])
                            wait_drained(pe, "DR", at)
                            last = mm(out[:], w_dt[:, e * P:(e + 1) * P], dr[:], start=True, stop=True)
                        inc(last, filled, g, at)
            def ahead_of(at, q, h, slots):
                if at[0] == "first":
                    pieces(at, q, h, slots)
                    for g in first[-4:]:
                        if g in ("B0", "B1", "C0"):
                            spread(g, q, h, at)
                            continue
                        wait_bank(pe, g, at)
                        pe.sem_inc(filled[bank_of(g, at)], 1)
                        pe.sem_inc(drained[bank_of(g, at)], 1)

            def step(at, i, h, n, last):
                for g, of_next in spread_at(n):
                    if not of_next:
                        spread(g, i, h, at)
                    elif not last:
                        spread(g, i + 1, 1 - h, at)
                if n in OUT:
                    out_rows(at, i, OUT[n])
                if not last:
                    pieces(at, i + 1, 1 - h, [n])
                here = at_of(at, f"C{n}")
                wait_drained(pe, f"C{n}", here)
                if n == 0:
                    pe.wait_ge(s_yf, i * KE + KE)
                for e in range(KE):
                    last_mm = mm(ybank[e][:], ident[:], hc[:, n % 2, e], start=(n == 0), stop=(n == NST - 1))
                last_mm.then_inc(s_y, 1)

            def out_rows(at, i, g):
                j = int(g[1])
                if j == 0:
                    pe.wait_ge(s_y2, i + 1)
                wait_bank(pe, g, at)
                for s in (2 * j, 2 * j + 1):
                    for e in range(KE):
                        last = mm(tile_of(g, at)[:, (s % 2) * D:(s % 2 + 1) * D], y1[:, e, s * P:(s + 1) * P],
                                  w_out[:, e], start=(e == 0 and s % 2 == 0), stop=(e == KE - 1 and s % 2 == 1),
                                  skip_group_check=True)
                inc(last, filled, g, at)

            def end(at, i, h, g):
                if g[0] == "Z":
                    out_rows(at, i, g)

            program(pe, ahead_of, step, end)



def routing(nc, dram):
    with ExitStack() as ctx:
        def sb(name, shape, dt=F32):
            return ctx.enter_context(nc.sbuf_tensor("r_" + name, shape, dt))

        def sem(name):
            return ctx.enter_context(nc.semaphore("r_" + name))

        ps_before = ctx.enter_context(nc.psum_tensor("r_ps_before", [P, NPICK * NE], F32))
        ps_total = ctx.enter_context(nc.psum_tensor("r_ps_total", [P, NPICK * NE], F32))
        lg = sb("lg", [P, NJ, NE])
        m8 = sb("m8", [P, NJ, 8])
        i8 = sb("i8", [P, NJ, 8], U32)
        pick = sb("pick", [P, TOPK, NJ])
        oh = sb("oh", [P, NPICK, NE])
        wts = sb("wts", [P, TOPK, NJ])
        ex = sb("ex", [P, 3, NJ])
        upper = sb("upper", [P, P])
        ones = sb("ones", [P, P])
        io_e = sb("io_e", [P, NE])
        io_m = sb("io_m", [P, TMAX])
        io_t = sb("io_t", [1, NT])
        tot = sb("tot", [P, NE, NPICK])
        incl = sb("incl", [P, NE, NPICK])
        cmp = sb("cmp", [P, NE, TMAX])
        nt = sb("nt", [P, NE])
        tend = sb("tend", [P, NE])
        base = sb("base", [P, NE])
        onesrow = ones[:, 0:NPICK]
        before = sb("before", [P, NPICK, NE])
        dstf = sb("dstf", [P, NPICK])
        dst = sb("dst", [P, NPICK], I32)
        cmpt = sb("cmpt", [1, NT, NE])
        texf = sb("texf", [1, NT])
        tex = sb("tex", [1, NT], I32)
        lg_in, s_c, s_d, s_ex, s_mm, s_out = sem("lg_in"), sem("c"), sem("d"), sem("ex"), sem("mm"), sem("out")
        block = ctx.enter_context(nc.Block())

        @block.gpsimd
        def _(pool):
            pool.memset(ones[:], 1.0).then_inc(s_c, 1)
            pool.wait_ge(s_c, 1)
            pool.affine_select(out=upper[:], in_=ones[:], compare_op=ALU.is_gt, fill=0.0, base=0, pattern=[[1, P]],
                               channel_multiplier=-1).then_inc(s_c, 1)
            pool.iota(io_e[:], pattern=[[1, NE]], base=0, channel_multiplier=0,
                      allow_small_or_imprecise_dtypes=True).then_inc(s_c, 1)
            pool.iota(io_m[:], pattern=[[S, TMAX]], base=0, channel_multiplier=0,
                      allow_small_or_imprecise_dtypes=True).then_inc(s_c, 1)
            pool.iota(io_t[:], pattern=[[1, NT]], base=0, channel_multiplier=0,
                      allow_small_or_imprecise_dtypes=True).then_inc(s_c, 1)

        @block.sync
        def _(sp):
            sp.dma_start(lg[:], dram["logits"]).then_inc(lg_in, 16)
            sp.wait_ge(s_d, D_STEPS)
            sp.dma_start(dram["dst"], dst[:]).then_inc(s_out, 16)
            sp.dma_start(dram["tex"], tex[:]).then_inc(s_out, 16)
            sp.dma_start(dram["wts"], wts[:].rearrange("p k j -> p (k j)")).then_inc(s_out, 16)
            sp.wait_ge(s_out, 48)

        @block.scalar
        def _(act):
            act.wait_ge(s_d, 2 * NJ + 1)
            act.activation(ex[:, 1], ex[:, 0], ACT.Exp).then_inc(s_ex, 1)

        @block.tensor
        def _(pe):
            pe.wait_ge(s_c, 5)
            pe.wait_ge(s_d, 2 * NJ + 1 + 1 + 1)
            r = oh[:].rearrange("p a e -> p (a e)")
            pe.matmul(ps_before[:], upper[:], r, start=True, stop=True).then_inc(s_mm, 1)
            pe.matmul(ps_total[:], ones[:], r, start=True, stop=True).then_inc(s_mm, 1)

        @block.vector
        def _(dve):
            n = [0]

            def step(ins, wait=True):
                ins.then_inc(s_d, 1)
                n[0] += 1
                if wait:
                    dve.wait_ge(s_d, n[0])

            def over(row, k):
                return row.rearrange("p (o n) -> p o n", o=1).to_broadcast([row.shape[0], k, row.shape[1]])

            dve.wait_ge(lg_in, 16)
            for j in range(NJ):
                step(dve.max(m8[:, j], lg[:, j]), False)
            dve.wait_ge(s_d, NJ)
            for j in range(NJ):
                step(dve.max_index(i8[:, j], m8[:, j], lg[:, j]), False)
            step(dve.tensor_tensor(ex[:, 0], m8[:, :, 1], m8[:, :, 0], ALU.subtract))
            step(dve.tensor_copy(pick[:], i8[:, :, 0:TOPK].rearrange("p j k -> p k j")))
            dve.wait_ge(s_c, 5)
            picks = pick[:].rearrange("p k (j o) -> p (k j) o", o=1).to_broadcast([P, NPICK, NE])
            step(dve.tensor_tensor(oh[:], picks, over(io_e[:], NPICK), ALU.is_equal))
            dve.wait_ge(s_ex, 1)
            step(dve.tensor_scalar(ex[:, 2], ex[:, 1], 1.0, None, ALU.add))
            step(dve.reciprocal(wts[:, 0], ex[:, 2]))
            step(dve.tensor_tensor(wts[:, 1], ex[:, 1], wts[:, 0], ALU.mult))
            dve.wait_ge(s_mm, 2)
            step(dve.tensor_copy(tot[:], ps_total[:].rearrange("p (a e) -> p e a", e=NE)))
            for e in range(NE):
                step(dve.tensor_tensor_scan(incl[:, e], onesrow, tot[:, e], 0.0, ALU.mult, ALU.add), False)
            dve.wait_ge(s_d, n[0])
            step(dve.tensor_tensor(cmp[:], over(io_m[:], NE), incl[:, :, NPICK - 1:NPICK].to_broadcast([P, NE, TMAX]), ALU.is_lt))
            step(dve.tensor_reduce(nt[:], cmp[:], AX_X, ALU.add))
            step(dve.tensor_tensor_scan(tend[:], ones[:, 0:NE], nt[:], 0.0, ALU.mult, ALU.add))
            step(dve.tensor_tensor(base[:], tend[:], nt[:], ALU.subtract))
            step(dve.tensor_scalar(base[:], base[:], float(S), None, ALU.mult))
            step(dve.tensor_tensor(incl[:], incl[:], tot[:], ALU.subtract))
            step(dve.tensor_tensor(before[:], ps_before[:].rearrange("p (a e) -> p a e", e=NE),
                                   incl[:].rearrange("p e a -> p a e"), ALU.add))
            step(dve.tensor_tensor(before[:], before[:], over(base[:], NPICK), ALU.add))
            step(dve.tensor_tensor(before[:], before[:], oh[:], ALU.mult))
            step(dve.tensor_reduce(dstf[:], before[:], AX_X, ALU.add))
            step(dve.tensor_copy(dst[:], dstf[:]))
            step(dve.tensor_tensor(cmpt[:], io_t[:].rearrange("p (t o) -> p t o", o=1).to_broadcast([1, NT, NE]),
                                   over(tend[0:1, :], NT), ALU.is_ge))
            step(dve.tensor_reduce(texf[:], cmpt[:], AX_X, ALU.add))
            step(dve.tensor_scalar(texf[:], texf[:], float(NE - 1), None, ALU.min))
            step(dve.tensor_copy(tex[:], texf[:]))
            assert n[0] == D_STEPS, n[0]


SPLITS = 2 * KF
D_STEPS = 2 * NJ + 3 + 3 + 1 + NE + 15


def experts(nc, dram):
    with ExitStack() as ctx:
        def sb(name, shape, dt=F32):
            return ctx.enter_context(nc.sbuf_tensor("e_" + name, shape, dt))

        def sem(name):
            return ctx.enter_context(nc.semaphore("e_" + name))

        NS = S // P
        HR = 4
        turned = [ctx.enter_context(nc.psum_tensor(f"e_turned{i}", [P, KD, S], F32)) for i in range(2)]
        hbank = [ctx.enter_context(nc.psum_tensor(f"e_h{i}", [P, 2, S], F32)) for i in range(HR)]
        obank = [ctx.enter_context(nc.psum_tensor(f"e_o{i}", [P, NS, D], F32)) for i in range(2)]
        ident = sb("ident", [P, P])
        tex = sb("tex", [1, NT], I32)
        w1 = [sb(f"w1{i}", [P, KD, 2 * FF]) for i in range(2)]
        w2 = [sb(f"w2{i}", [P, KF, D]) for i in range(2)]
        w1h, w1l, w2h, w2l = ([sb(f"{n}{i}", shape, F32R) for i in range(2)] for n, shape in
                              (("w1h", [P, KD, 2 * FF]), ("w1l", [P, KD, 2 * FF]), ("w2h", [P, KF, D]), ("w2l", [P, KF, D])))
        b1 = [sb(f"b1{i}", [P, 2 * KF]) for i in range(2)]
        b2 = [sb(f"b2{i}", [P, D]) for i in range(2)]
        xg = [sb(f"xg{i}", [P, NS, D]) for i in range(2)]
        xTh, xTl = ([sb(f"{n}{i}", [P, KD, S], F32R) for i in range(2)] for n in ("xTh", "xTl"))
        sg = sb("sg", [P, 2, S])
        ac = sb("ac", [P, 2, S])
        ach, acl = ([sb(f"{n}{i}", [P, KF, S], F32R) for i in range(2)] for n in ("ach", "acl"))
        yo = [sb(f"yo{i}", [P, NS, D]) for i in range(2)]
        tex_in, s_id = sem("tex_in"), sem("id")
        w_in = [sem(f"w_in{i}") for i in range(2)]
        x_in = [sem(f"x_in{i}") for i in range(2)]
        y_out = [sem(f"y_out{i}") for i in range(2)]
        small_in = [sem(f"small_in{i}") for i in range(2)]
        s_wh, s_wl, s_xTl, s_ah, s_al = sem("wh"), sem("wl"), sem("xTl"), sem("ah"), sem("al")
        s_turn, s_xT, s_h, s_sg, s_ac, s_o, s_y = (sem("turn"), sem("xT"), sem("h"), sem("sg"), sem("ac"), sem("o"),
                                                   sem("y"))
        block = ctx.enter_context(nc.Block())

        def f32(ap):
            return ap.bitcast(F32)

        def pairs(eng, tile):
            with eng.Fori(0, NT // 2) as g:
                tile(g * 2, g, 0, True)
                tile(g * 2 + 1, g, 1, True)
            tile(NT - 1, NT // 2, 0, False)

        def after(t, g, i):
            return t + 1, g + i, 1 - i

        def piece(w, m):
            return w[:].rearrange("p k (j n) -> p k j n", j=2)[:, :, :, m * P:(m + 1) * P]

        @block.gpsimd
        def _(pool):
            identity(pool, ident, s_id)
            pool.sem_inc(s_al, 2)

            def tile(t, g, i, follows):
                for m in range(KF):
                    pool.wait_ge(s_ah, t * KF + (m + 1))
                    pool.tensor_tensor(acl[i][:, m], ac[:, m % 2], f32(ach[i][:, m]), ALU.subtract).then_inc(s_al, 1)

            pairs(pool, tile)

        @block.sync
        def _(sp):
            sp.dma_start(tex[:], dram["tex"]).then_inc(tex_in, 16)
            sp.wait_ge(tex_in, 16)

            def load_weights(t, i):
                e = sp.value_load(tex[0:1, bass.ds(t, 1)], min_val=0, max_val=NE - 1)
                sp.wait_ge(s_wl, t * SPLITS + SPLITS)
                sp.wait_ge(tex_in, 16)
                sp.dma_start(w1[i][:], dram["w1"][bass.ds(e * P, P), :, :]).then_inc(w_in[i], 16)
                sp.dma_start(w2[i][:], dram["w2"][bass.ds(e * P, P), :, :]).then_inc(w_in[i], 16)

            def load_rows(t, i):
                e = sp.value_load(tex[0:1, bass.ds(t, 1)], min_val=0, max_val=NE - 1)
                sp.wait_ge(s_y, t + 1)
                sp.wait_ge(tex_in, 16)
                sp.dma_start(xg[i][:], dram["xg"][bass.ds(t * S, S), :].rearrange("(s p) d -> p s d", p=P)).then_inc(x_in[i], 16)
                sp.dma_start(b1[i][:], dram["b1"][bass.ds(e * P, P), :]).then_inc(small_in[i], 16)
                sp.dma_start(b2[i][:], dram["b2"][bass.ds(e, 1), :].to_broadcast([P, D])).then_inc(small_in[i], 16)

            def store(t, i):
                sp.wait_ge(s_y, t + 3)
                sp.dma_start(dram["yg"][bass.ds(t * S, S), :].rearrange("(s p) d -> p s d", p=P), yo[i][:]).then_inc(y_out[i], 16)

            for t in range(2):
                load_rows(t, t)
                load_weights(t, t)
            with sp.Fori(0, NT // 2 - 1) as g:
                for i in range(2):
                    load_weights(g * 2 + (2 + i), i)
                    load_rows(g * 2 + (2 + i), i)
                    store(g * 2 + i, i)
            load_weights(NT - 1, 0)
            load_rows(NT - 1, 0)
            for t in range(NT - 3, NT):
                store(t, t % 2)
            sp.wait_ge(y_out[0], 16 * ((NT + 1) // 2 + 1))
            sp.wait_ge(y_out[1], 16 * (NT // 2 + 1))

        @block.scalar
        def _(act):
            def high(t, g, i, m):
                if m == 0:
                    act.wait_ge(w_in[i], g * 32 + 32)
                    act.wait_ge(s_o, t + 1)
                act.activation(piece(w1h[i], m), piece(w1[i], m), ACT.Copy).then_inc(s_wh, 1)
                act.activation(w2h[i][:, m], w2[i][:, m], ACT.Copy).then_inc(s_wh, 1)

            def high_rows(t, i):
                act.wait_ge(s_turn, t + 1)
                act.activation(xTh[i][:], turned[i][:], ACT.Copy).then_inc(s_xT, 1)

            def tile(t, g, i, follows):
                for m in range(KF):
                    act.wait_ge(s_h, t * KF + (m + 1))
                    if m == 0:
                        act.wait_ge(small_in[i], g * 32 + 32)
                    act.wait_ge(s_ac, t * KF + (m + 1))
                    act.activation(sg[:, m % 2], hbank[m % HR][:, 1], ACT.Silu,
                                   bias=b1[i][:, KF + m:KF + m + 1]).then_inc(s_sg, 1)
                    if follows:
                        high(*after(t, g, i), m)
                if follows:
                    high_rows(t + 1, 1 - i)

            for m in range(KF):
                high(0, 0, 0, m)
            high_rows(0, 0)
            pairs(act, tile)

        @block.vector
        def _(dve):
            dve.sem_inc(s_ac, 2)
            dve.sem_inc(s_o, 2)
            dve.sem_inc(s_y, 2)
            dve.sem_inc(s_wl, 2 * SPLITS)
            for i in range(2):
                dve.sem_inc(y_out[i], 16)

            def low(t, i, m):
                dve.wait_ge(s_wh, t * SPLITS + 2 * (m + 1))
                dve.tensor_tensor(piece(w1l[i], m), piece(w1[i], m), f32(piece(w1h[i], m)), ALU.subtract).then_inc(s_wl, 1)
                dve.tensor_tensor(w2l[i][:, m], w2[i][:, m], f32(w2h[i][:, m]), ALU.subtract).then_inc(s_wl, 1)

            def low_rows(t, i):
                dve.wait_ge(s_xT, t + 1)
                dve.tensor_tensor(xTl[i][:], turned[i][:], f32(xTh[i][:]), ALU.subtract).then_inc(s_xTl, 1)

            def tile(t, g, i, follows):
                for m in range(KF):
                    dve.wait_ge(s_sg, t * KF + (m + 1))
                    dve.wait_ge(s_al, t * KF + (m + 1))
                    dve.scalar_tensor_tensor(out=ac[:, m % 2], in0=hbank[m % HR][:, 0], scalar=b1[i][:, m:m + 1],
                                             in1=sg[:, m % 2], op0=ALU.add, op1=ALU.mult).then_inc(s_ac, 1)
                    dve.wait_ge(s_ac, t * KF + (2 + m + 1))
                    if m == 0:
                        dve.wait_ge(s_o, t + 1)
                    dve.tensor_copy(ach[i][:, m], ac[:, m % 2]).then_inc(s_ah, 1)
                    if follows:
                        low(t + 1, 1 - i, m)
                if follows:
                    low_rows(t + 1, 1 - i)
                dve.wait_ge(s_o, t + 3)
                dve.wait_ge(y_out[i], g * 16 + 16)
                dve.tensor_tensor(yo[i][:], obank[i][:],
                                  b2[i][:].rearrange("p (o d) -> p o d", o=1).to_broadcast([P, NS, D]), ALU.add).then_inc(s_y, 1)

            for m in range(KF):
                low(0, 0, m)
            low_rows(0, 0)
            pairs(dve, tile)

        @block.tensor
        def _(pe):
            mm = pe.matmul
            pe.wait_ge(s_id, 2)

            def turn(t, g, i):
                pe.wait_ge(x_in[i], g * 16 + 16)
                if not (isinstance(t, int) and t < 2):
                    pe.wait_ge(s_xTl, t - 1)
                for k in range(KD):
                    for s in range(NS):
                        last = pe.transpose(turned[i][:, k, s * P:(s + 1) * P], xg[i][:, s, k * P:(k + 1) * P], ident[:])
                last.then_inc(s_turn, 1)

            def tile(t, g, i, nxt):
                pe.wait_ge(s_xTl, t + 1)
                for m in range(KF):
                    pe.wait_ge(s_wl, t * SPLITS + (2 * SPLITS + 2 * (m + 1)))
                    if m >= HR or not isinstance(t, int) or t > 0:
                        pe.wait_ge(s_ac, t * KF + (2 + m + 1 - HR))
                    for j in range(2):
                        cols = slice(j * FF + m * P, j * FF + (m + 1) * P)
                        for k in range(KD):
                            for p, (w, x) in enumerate(((w1h, xTh), (w1h, xTl), (w1l, xTh))):
                                last = mm(hbank[m % HR][:, j], w[i][:, k, cols], x[i][:, k],
                                          start=(p == 0 and k == 0 and j == 0), stop=(p == 2 and k == KD - 1 and j == 1),
                                          skip_group_check=True)
                    last.then_inc(s_h, 1)
                if nxt is not None:
                    turn(*nxt)
                pe.wait_ge(s_y, t + 1)
                for m in range(KF):
                    pe.wait_ge(s_al, t * KF + (2 + m + 1))
                    for s in range(NS):
                        for p, (a, w) in enumerate(((ach, w2h), (ach, w2l), (acl, w2h))):
                            last = mm(obank[i][:, s], a[i][:, m, s * P:(s + 1) * P], w[i][:, m], start=(m + s + p == 0),
                                      stop=(p == 2 and m == KF - 1 and s == NS - 1), skip_group_check=True)
                last.then_inc(s_o, 1)

            turn(0, 0, 0)
            tile(0, 0, 0, (1, 0, 1))
            with pe.Fori(0, NT // 2 - 1) as g:
                tile(g * 2 + 1, g, 1, (g * 2 + 2, g + 1, 0))
                tile(g * 2 + 2, g + 1, 0, (g * 2 + 3, g + 1, 1))
            tile(NT - 2, NT // 2 - 1, 1, (NT - 1, NT // 2, 0))
            tile(NT - 1, NT // 2, 0, None)


def combine(nc, dram, out):
    with ExitStack() as ctx:
        def sb(name, shape, dt=F32):
            return ctx.enter_context(nc.sbuf_tensor("c_" + name, shape, dt))

        def sem(name):
            return ctx.enter_context(nc.semaphore("c_" + name))

        dst = sb("dst", [P, NPICK], I32)
        wts = sb("wts", [P, NPICK])
        ya = sb("ya", [P, NPICK, D])
        xa = sb("xa", [P, NJ, D])
        mo = sb("mo", [P, NJ, D])
        small_in, y_in, out_done = sem("small_in"), sem("y_in"), sem("out_done")
        x_in = [sem(f"x_in{i}") for i in range(NCH)]
        s_add, s_y1, s_y2 = sem("add"), sem("y1"), sem("y2")
        yj = [sem(f"yj{i}") for i in range(NCH)]
        block = ctx.enter_context(nc.Block())

        @block.sync
        def _(sp):
            sp.dma_start(dst[:], dram["dst"]).then_inc(small_in, 16)
            sp.dma_start(wts[:], dram["wts"]).then_inc(small_in, 16)
            for c in range(NCH):
                for tile, src in ((xa, dram["x1p"]), (mo, dram["mo"][T:, :])):
                    sp.dma_start(tile[:, c * SUB:(c + 1) * SUB], src[c * T:(c + 1) * T, :].rearrange("(s p) d -> p s d", p=P)).then_inc(x_in[c], 16)
            for c in range(NCH):
                sp.wait_ge(s_y2, (c + 1) * SUB)
                sp.dma_start(out[c * T:(c + 1) * T, :].rearrange("(s p) d -> p s d", p=P), xa[:, c * SUB:(c + 1) * SUB]).then_inc(out_done, 16)
            sp.wait_ge(out_done, 16 * NCH)

        @block.gpsimd
        def _(pool):
            pool.wait_ge(small_in, 32)
            for c in range(NCH):
                for j in range(c * SUB, (c + 1) * SUB):
                    for k in range(TOPK):
                        a = k * NJ + j
                        pool.indirect_dma_start(ya[:, a, :], None, dram["yg"][:, :],
                                                bass.IndirectOffsetOnAxis(ap=dst[:, a:a + 1], axis=0)).then_inc(yj[c], 16)

        @block.vector
        def _(dve):
            dve.wait_ge(small_in, 32)
            for c in range(NCH):
                cs = slice(c * SUB, (c + 1) * SUB)
                dve.wait_ge(x_in[c], 32)
                dve.tensor_tensor(xa[:, cs], xa[:, cs], mo[:, cs], ALU.add).then_inc(s_add, 1)
                dve.wait_ge(s_add, c + 1)
                dve.wait_ge(yj[c], 16 * SUB * TOPK)
                for k, done in ((0, s_y1), (1, s_y2)):
                    for j in range(c * SUB, (c + 1) * SUB):
                        a = k * NJ + j
                        if k == 1:
                            dve.wait_ge(s_y1, j + 1)
                        dve.scalar_tensor_tensor(out=xa[:, j], in0=ya[:, a], scalar=wts[:, a:a + 1], in1=xa[:, j],
                                                 op0=ALU.mult, op1=ALU.add).then_inc(done, 1)


def kernel(**inputs):
    import numpy as np
    import concourse.bacc as bacc
    from concourse.bass_utils import run_bass_kernel_spmd

    a = {k: np.ascontiguousarray(v) for k, v in inputs.items()}
    g = lambda n: a["L0_attn_" + n]
    f = lambda n: a["L0_ffn_" + n]
    m = lambda n: a["L1_attn_" + n]
    x = lambda n: a["L1_ffn_" + n]

    def blocks(w):
        return np.ascontiguousarray(w.reshape(-1, P, w.shape[1]).transpose(1, 0, 2))

    def cols(v):
        return np.ascontiguousarray(v.reshape(-1, P, v[0].size).transpose(1, 0, 2).reshape(P, -1))

    arrays = {
        "x": np.concatenate([g("hidden_states").reshape(NTOK, D), np.zeros((T, D), np.float32)]),
        "w_p": blocks(np.concatenate([g("fc_r_w"), g("fc_i_w"), g("fc_w"), g("fc_gate_w")]).T),
        "w_m": blocks(np.concatenate([g("mlp_gate_w"), g("mlp_fc_w")]).T),
        "w_o": blocks(g("out_w").T),
        "w_f": blocks(f("w_fc").T),
        "w_j": blocks(f("w_proj").T),
        "vec0": np.concatenate([cols(v) for v in (g("fc_r_b"), g("fc_i_b"), g("fc_b"), g("fc_gate_b"), g("mlp_gate_b"),
                                                  g("mlp_fc_b"), g("norm_w"), g("norm2_w"), g("alpha").reshape(-1))], axis=1),
        "out_b": g("out_b").reshape(1, D),
        "gate_b": x("gate_b").reshape(1, NE),
        "gate_w": blocks(x("gate_w")),
        "low_v": f("v"),
        "low_b": np.ascontiguousarray(f("fast_b").T),
        "low_u": np.ascontiguousarray(f("u").T),
        "low_g": f("gate").reshape(1, 1),
        "w_si": blocks(np.concatenate([m("skip_w"), m("in_w")]).T),
        "w_x": blocks(np.concatenate([m("wB"), m("wC"), m("wd1")]).T),
        "w_dt": np.ascontiguousarray(m("wd2").T),
        "w_out": blocks(m("out_w").T),
        "vec1": np.concatenate([cols(v) for v in (m("norm_w"), m("conv_w"), m("conv_b"), m("wd2_b"), m("A_log"), m("W_D"))], axis=1),
        "w1": np.ascontiguousarray(x("w1").reshape(NE, KD, P, 2 * FF).transpose(0, 2, 1, 3).reshape(NE * P, KD, 2 * FF)),
        "w2": np.ascontiguousarray(x("w2").reshape(NE, KF, P, D).transpose(0, 2, 1, 3).reshape(NE * P, KF, D)),
        "b1": np.ascontiguousarray(x("b1").reshape(NE, 2 * KF, P).transpose(0, 2, 1).reshape(NE * P, 2 * KF)),
        "b2": x("b2"),
    }
    nc = bacc.Bacc("TRN2", target_bir_lowering=False, num_devices=1)
    dram = {n: nc.dram_tensor("in_" + n, v.shape, F32, kind="ExternalInput").ap() for n, v in arrays.items()}
    out = nc.dram_tensor("out", (NTOK, D), F32, kind="ExternalOutput").ap()
    program(nc, dram, out)
    r = run_bass_kernel_spmd(nc, [{"in_" + n: v for n, v in arrays.items()}], core_ids=[0])
    return r.results[0]["out"].reshape(NTOK // SEQ, SEQ, D)


def program(nc, dram, out):
    dram = dict(dram)
    for name, shape, dt in (("x1p", (NTOK, D), F32), ("xn1", (NTOK, D), F32), ("xrT", (NCH * P, KD, T), F32),
                            ("logits", (P, NJ, NE), F32), ("mo", (T + NTOK, D), F32), ("xg", (NSLOT, D), F32),
                            ("yg", (NSLOT, D), F32), ("dst", (P, NPICK), I32), ("tex", (1, NT), I32),
                            ("wts", (P, NPICK), F32)):
        dram[name] = nc.dram_tensor("scratch_" + name, shape, dt, kind="Internal").ap()
    layer0(nc, dram)
    routing(nc, dram)
    mamba(nc, dram)
    experts(nc, dram)
    combine(nc, dram, out)
```
